# Optimizing a Trainium2 kernel written in Bass

```python
import numpy as np
import jax
import jax.numpy as jnp

def _softmax(x, axis=-1):
    return jax.nn.softmax(x, axis=axis)

def _gelu(x):
    return jax.nn.gelu(x, approximate=True)

def _silu(x):
    return jax.nn.silu(x)

def _sigmoid(x):
    return jax.nn.sigmoid(x)

def _layernorm(x, axis=-1, eps=1e-05):
    m = jnp.mean(x, axis=axis, keepdims=True)
    v = jnp.var(x, axis=axis, keepdims=True)
    return (x - m) / jnp.sqrt(v + eps)

def _scatter_add(tgt, idx, src, axis=0):
    return tgt.at[idx].add(src)

def _segment_sum(src, seg, n):
    return jax.ops.segment_sum(src, seg, n)
kernel_name = 'mk_audio_tower_d2_tok_audfeat512_r4_9ebbff'

def setup_inputs(seed: int=0):
    np.random.seed(seed)
    _w = jnp.asarray

    def _rec_inputs():
        import jax
        import jax.numpy as jnp
        _rk = jax.random.key(seed)
        x = 7.22013e-05 + 1.00017 * jax.random.normal(jax.random.fold_in(_rk, 1), (64, 64, 125), jnp.float32)
        return x
    x = _rec_inputs()

    def _L0_tok_setup():
        import jax, jax.numpy as jnp
        import numpy as np
        B, C_IN, DIM, L = (8, 64, 128, 1024)

        def _layer_norm(y, gamma, beta, eps=1e-05):
            mu = jnp.mean(y, axis=-1, keepdims=True)
            var = jnp.mean(jnp.square(y - mu), axis=-1, keepdims=True)
            return (y - mu) * jax.lax.rsqrt(var + eps) * gamma + beta
        key = jax.random.key(seed)
        ks = jax.random.split(key, 4)
        x = jax.random.normal(ks[0], (B, C_IN, L), dtype=jnp.float32)
        W_proj = jax.random.normal(ks[1], (DIM, C_IN), dtype=jnp.float32) * (1.0 / np.sqrt(C_IN))
        b_proj = jnp.zeros((DIM,), dtype=jnp.float32)
        W_dw = jax.random.normal(ks[2], (DIM, 3), dtype=jnp.float32) * (1.0 / np.sqrt(3.0))
        b_dw = jnp.zeros((DIM,), dtype=jnp.float32)
        W_pw = jax.random.normal(ks[3], (DIM, DIM), dtype=jnp.float32) * (1.0 / np.sqrt(DIM))
        b_pw = jnp.zeros((DIM,), dtype=jnp.float32)
        gamma = jnp.ones((DIM,), dtype=jnp.float32)
        beta = jnp.zeros((DIM,), dtype=jnp.float32)
        return {'x': x, 'W_proj': W_proj, 'b_proj': b_proj, 'W_dw': W_dw, 'b_dw': b_dw, 'W_pw': W_pw, 'b_pw': b_pw, 'gamma': gamma, 'beta': beta}
    _L0_tok_all = _L0_tok_setup()
    _L0_tok_in = {k: v for k, v in _L0_tok_all.items() if k in ('W_proj', 'b_proj', 'W_dw', 'b_dw', 'W_pw', 'b_pw', 'gamma', 'beta')}
    del _L0_tok_all

    def _L0_attn_setup():
        import jax, jax.numpy as jnp
        import numpy as np
        from math import sqrt
        key = jax.random.key(seed)
        k1, k2, k3, k4 = jax.random.split(key, 4)
        bs, N, D, H = (2, 1024, 128, 8)
        z = jax.random.normal(k1, (bs, N, D), dtype=jnp.float32)
        w_qkv = jax.random.normal(k2, (3 * D, D), dtype=jnp.float32) * (1.0 / sqrt(D))
        w_agg = jax.random.normal(k3, (D, D), dtype=jnp.float32) * (1.0 / sqrt(D))
        b_agg = jax.random.normal(k4, (D,), dtype=jnp.float32) * 0.01
        return {'z': z, 'w_qkv': w_qkv, 'w_agg': w_agg, 'b_agg': b_agg}
    _L0_attn_all = _L0_attn_setup()
    _L0_attn_in = {k: v for k, v in _L0_attn_all.items() if k in ('w_qkv', 'w_agg', 'b_agg')}
    del _L0_attn_all

    def _L0_ffn_setup():
        import jax, jax.numpy as jnp
        import numpy as np
        B, T, D = (4, 2048, 128)
        E, F, CAP = (8, 512, 1024)
        key = jax.random.key(seed)
        ks = jax.random.split(key, 6)
        s = 0.02
        return {'x': jax.random.normal(ks[0], (B, T, D), dtype=jnp.float32), 'Wr': jax.random.normal(ks[1], (D, E), dtype=jnp.float32) * s, 'W1': jax.random.normal(ks[2], (E, D, F), dtype=jnp.float32) * s, 'b1': jax.random.normal(ks[3], (E, F), dtype=jnp.float32) * s, 'W2': jax.random.normal(ks[4], (E, F, D), dtype=jnp.float32) * s, 'b2': jax.random.normal(ks[5], (E, D), dtype=jnp.float32) * s}
    _L0_ffn_all = _L0_ffn_setup()
    _L0_ffn_in = {k: v for k, v in _L0_ffn_all.items() if k in ('Wr', 'W1', 'b1', 'W2', 'b2')}
    del _L0_ffn_all

    def _L1_attn_setup():
        import jax, jax.numpy as jnp
        import numpy as np
        import math
        _DENSE_LOCAL_W = 32
        _DYADIC = [48, 64, 96, 128, 192, 64, 96, 128, 192, 256, 384, 512, 768, 1024]
        OFFSETS = np.array(sorted(set(range(0, _DENSE_LOCAL_W + 1)) | set(_DYADIC)), dtype=np.int32)
        NUM_OFFSETS = len(OFFSETS)
        H = 8
        _LOG_MAX = math.log(1.0 + 4096.0)
        _HEAD_OMEGAS = [0.0, 0.0, 1 * math.pi / _LOG_MAX, 1 * math.pi / _LOG_MAX, 4 * math.pi / _LOG_MAX, 4 * math.pi / _LOG_MAX, 6 * math.pi / _LOG_MAX, 6 * math.pi / _LOG_MAX]
        _log_d = np.log(1.0 + OFFSETS.astype(np.float64))
        _CK = np.zeros((NUM_OFFSETS, H), dtype=np.float32)
        for _h, _om in enumerate(_HEAD_OMEGAS):
            if _om > 0.0:
                _CK[:, _h] = np.cos(_om * _log_d)
        DISP_COS_KERNEL = jnp.asarray(_CK)
        B, N, D = (1, 512, 128)
        HD = D // H
        key = jax.random.key(seed)
        ks = jax.random.split(key, 8)
        s = 0.02
        return {'x': jax.random.normal(ks[0], (B, N, D), jnp.float32), 'W_qkv': jax.random.normal(ks[1], (D, 3 * D), jnp.float32) * s, 'b_qkv': jax.random.normal(ks[2], (3 * D,), jnp.float32) * s, 'W_out': jax.random.normal(ks[3], (D, D), jnp.float32) * s, 'b_out': jax.random.normal(ks[4], (D,), jnp.float32) * s, 'W_gate': jax.random.normal(ks[5], (D, D), jnp.float32) * s, 'b_gate': jnp.zeros((D,), jnp.float32), 'pos_bias': jnp.zeros((NUM_OFFSETS, H), jnp.float32) + 0.001, 'scale_embed': jnp.zeros((NUM_OFFSETS, HD), jnp.float32), 'if_gain': jnp.ones((H,), jnp.float32), 'disp_amp': jnp.full((H,), 0.1, jnp.float32)}
    _L1_attn_all = _L1_attn_setup()
    _L1_attn_in = {k: v for k, v in _L1_attn_all.items() if k in ('W_qkv', 'b_qkv', 'W_out', 'b_out', 'W_gate', 'b_gate', 'pos_bias', 'scale_embed', 'if_gain', 'disp_amp')}
    del _L1_attn_all

    def _L1_ffn_setup():
        import jax, jax.numpy as jnp
        import numpy as np
        B, S, D, H, E = (4, 256, 128, 512, 8)
        key = jax.random.key(seed)
        ks = jax.random.split(key, 7)
        scale = 1.0 / np.sqrt(D)
        return {'x': jax.random.normal(ks[0], (B, S, D), dtype=jnp.float32), 'Wg': jax.random.normal(ks[1], (D, E), dtype=jnp.float32) * scale, 'bg': jnp.zeros((E,), dtype=jnp.float32), 'W1': jax.random.normal(ks[2], (E, D, H), dtype=jnp.float32) * scale, 'b1': jnp.zeros((E, H), dtype=jnp.float32), 'W2': jax.random.normal(ks[3], (E, H, D), dtype=jnp.float32) * (1.0 / np.sqrt(H)), 'b2': jnp.zeros((E, D), dtype=jnp.float32)}
    _L1_ffn_all = _L1_ffn_setup()
    _L1_ffn_in = {k: v for k, v in _L1_ffn_all.items() if k in ('Wg', 'bg', 'W1', 'b1', 'W2', 'b2')}
    del _L1_ffn_all
    return {'x': x, 'L0_tok_W_proj': _L0_tok_in['W_proj'], 'L0_tok_b_proj': _L0_tok_in['b_proj'], 'L0_tok_W_dw': _L0_tok_in['W_dw'], 'L0_tok_b_dw': _L0_tok_in['b_dw'], 'L0_tok_W_pw': _L0_tok_in['W_pw'], 'L0_tok_b_pw': _L0_tok_in['b_pw'], 'L0_tok_gamma': _L0_tok_in['gamma'], 'L0_tok_beta': _L0_tok_in['beta'], 'L0_attn_w_qkv': _L0_attn_in['w_qkv'], 'L0_attn_w_agg': _L0_attn_in['w_agg'], 'L0_attn_b_agg': _L0_attn_in['b_agg'], 'L0_ffn_Wr': _L0_ffn_in['Wr'], 'L0_ffn_W1': _L0_ffn_in['W1'], 'L0_ffn_b1': _L0_ffn_in['b1'], 'L0_ffn_W2': _L0_ffn_in['W2'], 'L0_ffn_b2': _L0_ffn_in['b2'], 'L1_attn_W_qkv': _L1_attn_in['W_qkv'], 'L1_attn_b_qkv': _L1_attn_in['b_qkv'], 'L1_attn_W_out': _L1_attn_in['W_out'], 'L1_attn_b_out': _L1_attn_in['b_out'], 'L1_attn_W_gate': _L1_attn_in['W_gate'], 'L1_attn_b_gate': _L1_attn_in['b_gate'], 'L1_attn_pos_bias': _L1_attn_in['pos_bias'], 'L1_attn_scale_embed': _L1_attn_in['scale_embed'], 'L1_attn_if_gain': _L1_attn_in['if_gain'], 'L1_attn_disp_amp': _L1_attn_in['disp_amp'], 'L1_ffn_Wg': _L1_ffn_in['Wg'], 'L1_ffn_bg': _L1_ffn_in['bg'], 'L1_ffn_W1': _L1_ffn_in['W1'], 'L1_ffn_b1': _L1_ffn_in['b1'], 'L1_ffn_W2': _L1_ffn_in['W2'], 'L1_ffn_b2': _L1_ffn_in['b2']}

def reference(x, L0_tok_W_proj, L0_tok_b_proj, L0_tok_W_dw, L0_tok_b_dw, L0_tok_W_pw, L0_tok_b_pw, L0_tok_gamma, L0_tok_beta, L0_attn_w_qkv, L0_attn_w_agg, L0_attn_b_agg, L0_ffn_Wr, L0_ffn_W1, L0_ffn_b1, L0_ffn_W2, L0_ffn_b2, L1_attn_W_qkv, L1_attn_b_qkv, L1_attn_W_out, L1_attn_b_out, L1_attn_W_gate, L1_attn_b_gate, L1_attn_pos_bias, L1_attn_scale_embed, L1_attn_if_gain, L1_attn_disp_amp, L1_ffn_Wg, L1_ffn_bg, L1_ffn_W1, L1_ffn_b1, L1_ffn_W2, L1_ffn_b2):
    import jax
    import jax.numpy as jnp

    def _L0_tok_ref(x, W_proj, b_proj, W_dw, b_dw, W_pw, b_pw, gamma, beta):
        import jax, jax.numpy as jnp
        import numpy as np
        B, C_IN, DIM, L = (8, 64, 128, 1024)

        def _layer_norm(y, gamma, beta, eps=1e-05):
            mu = jnp.mean(y, axis=-1, keepdims=True)
            var = jnp.mean(jnp.square(y - mu), axis=-1, keepdims=True)
            return (y - mu) * jax.lax.rsqrt(var + eps) * gamma + beta
        y = jnp.einsum('bcl,dc->bdl', x, W_proj) + b_proj[None, :, None]
        yp = jnp.pad(y, ((0, 0), (0, 0), (1, 1)))
        n = y.shape[-1]
        y = W_dw[None, :, 0:1] * yp[:, :, 0:n] + W_dw[None, :, 1:2] * yp[:, :, 1:n + 1] + W_dw[None, :, 2:3] * yp[:, :, 2:n + 2] + b_dw[None, :, None]
        y = jnp.einsum('bdl,ed->bel', y, W_pw) + b_pw[None, :, None]
        y = jax.nn.silu(y)
        y = jnp.transpose(y, (0, 2, 1))
        return _layer_norm(y, gamma, beta)

    def _L0_attn_ref(z, w_qkv, w_agg, b_agg):
        import jax, jax.numpy as jnp
        import numpy as np
        from math import sqrt
        bs, N, D = z.shape
        H = 8
        Dh = D // H
        qkv = jnp.einsum('bnd,ed->bne', z, w_qkv).reshape(bs, N, 3, H, Dh)
        q, k, v = jnp.moveaxis(qkv, 2, 0)
        q = q.transpose(0, 2, 1, 3)
        k = k.transpose(0, 2, 1, 3)
        v = v.transpose(0, 2, 1, 3)
        scores = jnp.einsum('bhnd,bhmd->bhnm', q, k) / sqrt(Dh)
        attn = jax.nn.softmax(scores, axis=-1)
        sa = jnp.einsum('bhnm,bhmd->bhnd', attn, v)
        sa = sa.transpose(0, 2, 1, 3).reshape(bs, N, H * Dh)
        out = jnp.einsum('bnd,ed->bne', sa, w_agg) + b_agg
        return out

    def _L0_ffn_ref(x, Wr, W1, b1, W2, b2):
        import jax, jax.numpy as jnp
        import numpy as np
        B, T, D = (4, 2048, 128)
        E, F, CAP = (8, 512, 1024)
        Bb, Tt, Dd = x.shape
        N = Bb * Tt
        C = min(CAP, N)
        x_flat = x.reshape(N, Dd)
        logits = x_flat @ Wr
        probs = jax.nn.softmax(logits, axis=0)
        vals, idx = jax.lax.top_k(probs.T, C)
        selected = x_flat[idx]
        h = jax.nn.gelu(jnp.einsum('ecd,edf->ecf', selected, W1) + b1[:, None, :], approximate=False)
        out_e = jnp.einsum('ecf,efd->ecd', h, W2) + b2[:, None, :]
        weighted = vals[..., None] * out_e
        output = jnp.zeros_like(x_flat).at[idx.reshape(-1)].add(weighted.reshape(-1, Dd))
        return output.reshape(Bb, Tt, Dd)

    def _L1_attn_ref(x, W_qkv, b_qkv, W_out, b_out, W_gate, b_gate, pos_bias, scale_embed, if_gain, disp_amp):
        import jax, jax.numpy as jnp
        import numpy as np
        import math
        _DENSE_LOCAL_W = 32
        _DYADIC = [48, 64, 96, 128, 192, 64, 96, 128, 192, 256, 384, 512, 768, 1024]
        OFFSETS = np.array(sorted(set(range(0, _DENSE_LOCAL_W + 1)) | set(_DYADIC)), dtype=np.int32)
        NUM_OFFSETS = len(OFFSETS)
        H = 8
        _LOG_MAX = math.log(1.0 + 4096.0)
        _HEAD_OMEGAS = [0.0, 0.0, 1 * math.pi / _LOG_MAX, 1 * math.pi / _LOG_MAX, 4 * math.pi / _LOG_MAX, 4 * math.pi / _LOG_MAX, 6 * math.pi / _LOG_MAX, 6 * math.pi / _LOG_MAX]
        _log_d = np.log(1.0 + OFFSETS.astype(np.float64))
        _CK = np.zeros((NUM_OFFSETS, H), dtype=np.float32)
        for _h, _om in enumerate(_HEAD_OMEGAS):
            if _om > 0.0:
                _CK[:, _h] = np.cos(_om * _log_d)
        DISP_COS_KERNEL = jnp.asarray(_CK)
        B, N, D = (1, 512, 128)
        HD = D // H
        Bx, Nx, Dx = x.shape
        qkv = x @ W_qkv + b_qkv
        q, k, v = jnp.split(qkv, 3, axis=-1)
        q = q.reshape(Bx, Nx, H, HD).transpose(0, 2, 1, 3)
        k = k.reshape(Bx, Nx, H, HD).transpose(0, 2, 1, 3)
        v = v.reshape(Bx, Nx, H, HD).transpose(0, 2, 1, 3)
        deltas = jnp.asarray(OFFSETS)
        pos = jnp.arange(Nx)
        j = pos[None, :] - deltas[:, None]
        valid = j >= 0
        jc = jnp.maximum(j, 0)
        kg = k[:, :, jc]
        vg = v[:, :, jc]
        km = kg * (1.0 + scale_embed)[None, None, :, None, :]
        eff_pb = pos_bias + DISP_COS_KERNEL * disp_amp[None, :]
        scores = jnp.einsum('bhnd,bhond->bhon', q, km) / math.sqrt(HD)
        scores = scores + eff_pb.T[None, :, :, None]
        scores = jnp.where(valid[None, None], scores, -jnp.inf)
        attn = jax.nn.softmax(scores, axis=2)
        out = jnp.einsum('bhon,bhond->bhnd', attn, vg)
        out = out * if_gain[None, :, None, None]
        out_flat = out.transpose(0, 2, 1, 3).reshape(Bx, Nx, Dx)
        gate = jax.nn.sigmoid(x @ W_gate + b_gate)
        return out_flat * gate @ W_out + b_out

    def _L1_ffn_ref(x, Wg, bg, W1, b1, W2, b2):
        import jax, jax.numpy as jnp
        import numpy as np
        B, S, D, H, E = (4, 256, 128, 512, 8)
        b, s, d = x.shape
        xf = x.reshape(-1, d)
        logits = xf @ Wg + bg
        scores = jax.nn.softmax(logits, axis=-1)
        top_s, top_i = jax.lax.top_k(scores, 1)
        idx = top_i[:, 0]
        sc = top_s[:, 0]
        n_experts = Wg.shape[1]
        out = jnp.zeros_like(xf)
        for e in range(n_experts):
            h = jax.nn.relu(xf @ W1[e] + b1[e]) @ W2[e] + b2[e]
            out = jnp.where((idx == e)[:, None], h, out)
        out = out * sc[:, None]
        return out.reshape(b, s, d)
    h = _L0_tok_ref(x, L0_tok_W_proj, L0_tok_b_proj, L0_tok_W_dw, L0_tok_b_dw, L0_tok_W_pw, L0_tok_b_pw, L0_tok_gamma, L0_tok_beta)
    h = h + _L0_attn_ref(_layernorm(h, axis=-1), L0_attn_w_qkv, L0_attn_w_agg, L0_attn_b_agg)
    h = h + _L0_ffn_ref(_layernorm(h, axis=-1), L0_ffn_Wr, L0_ffn_W1, L0_ffn_b1, L0_ffn_W2, L0_ffn_b2)
    h = h + _L1_attn_ref(_layernorm(h, axis=-1), L1_attn_W_qkv, L1_attn_b_qkv, L1_attn_W_out, L1_attn_b_out, L1_attn_W_gate, L1_attn_b_gate, L1_attn_pos_bias, L1_attn_scale_embed, L1_attn_if_gain, L1_attn_disp_amp)
    h = h + _L1_ffn_ref(_layernorm(h, axis=-1), L1_ffn_Wg, L1_ffn_bg, L1_ffn_W1, L1_ffn_b1, L1_ffn_W2, L1_ffn_b2)
    return h

_drawn_inputs = setup_inputs


def setup_inputs(seed=0):
    import zlib

    import numpy as np

    out = dict(_drawn_inputs(seed))
    spreads = {'L0_tok_b_proj': (0.0, 0.1),
     'L0_tok_b_dw': (0.0, 0.1),
     'L0_tok_b_pw': (0.0, 0.1),
     'L0_tok_gamma': (1.0, 0.2),
     'L0_tok_beta': (0.0, 0.1),
     'L1_attn_b_gate': (0.0, 2.0),
     'L1_attn_pos_bias': (0.0010000000474974513, 0.6),
     'L1_attn_scale_embed': (0.0, 2.0),
     'L1_attn_if_gain': (1.0, 0.6),
     'L1_attn_disp_amp': (0.10000000149011612, 0.6),
     'L1_ffn_bg': (0.0, 0.401),
     'L1_ffn_b1': (0.0, 1.246),
     'L1_ffn_b2': (0.0, 0.8)}
    factors = {'L0_ffn_Wr': 40.328,
     'L0_ffn_W1': 56.158,
     'L0_ffn_b1': 64.0,
     'L0_ffn_W2': 44.21,
     'L0_ffn_b2': 200.0,
     'L1_attn_W_qkv': 2.989,
     'L1_attn_b_qkv': 7.551,
     'L1_attn_W_out': 3.303,
     'L1_attn_W_gate': 8.0,
     'L0_attn_b_agg': 4.058,
     'L1_attn_b_out': 6.854}
    for name, (base, spread) in spreads.items():
        noise = np.random.default_rng([zlib.crc32(name.encode()), seed]).standard_normal(out[name].shape)
        drawn = base * np.exp(spread * noise) if base else spread * noise
        out[name] = jnp.asarray(drawn.astype(out[name].dtype))
    for name, factor in factors.items():
        out[name] = (out[name] * factor).astype(out[name].dtype)
    return out
```

```python
from contextlib import ExitStack

import concourse.bass as bass
from concourse import mybir

F32 = mybir.dt.float32
BF16 = mybir.dt.bfloat16
I32 = mybir.dt.int32
U32 = mybir.dt.uint32
ALU = mybir.AluOpType
ACT = mybir.ActivationFunctionType
AX_X = mybir.AxisListType.X

B, CIN, L, D = 64, 64, 125, 128
GB = 4
NG = B // GB
GT = GB * L
N = B * L
NH, DH = 8, 16
EPS = 1e-5
E, F, CAP = 8, 512, 1024
OFF_LOCAL = 32
OFFS = list(range(OFF_LOCAL, -1, -1)) + [o for o in (48, 64, 96, 128, 192, 256, 384, 512, 768, 1024) if o < L]
OFF_SPLIT = 19
TILE = 256
NTILES = (N + E * (TILE - 1)) // TILE
NTILES += NTILES % 2
ROW = 2 * D + 2


class Tower:

    def __init__(self, nc, ctx, t, out):
        self.nc, self.ctx, self.t, self.out = nc, ctx, t, out
        self.H = self.sb("H", [L, B, D])
        self.ident = self.sb("ident", [128, 128])
        self.ident_bf = self.sb("ident_bf", [128, 128], BF16)
        self.chosen = self.sb("chosen", [128, E * CAP // 128], I32)
        self.head_mask = self.sb("head_mask", [D, NH])
        self.h_rows = self.dram("h_rows", [N, D])
        self.z_rows = self.dram("z_rows", [N, D + E])
        self.logits = self.dram("logits", [E, N])
        self.diagonals = [self.dram(f"diagonals{p}", [OFFS[-1] + L, L, GB * NH]) for p in range(2)]
        self.slot_rows = self.dram("slot_rows", [NTILES * TILE, ROW])
        self.tile_expert = self.sb("tile_expert", [1, NTILES], I32)
        self.out_rows = out.rearrange("b l d -> (b l) d")
        self.chosen_rows = self.dram("chosen_rows", [E * CAP])
        self.neg_half = self.sb("neg_half", [L, GB])
        self.consts_done = ctx.enter_context(nc.semaphore("consts_done"))
        self.waited = ctx.enter_context(nc.semaphore("waited"))
        self.old_ctx, self.stage_ctx, self.stage_sems = ExitStack(), ExitStack(), []
        self.eps = self.sb("eps", [L, GB])

    def dram(self, name, shape, dt=F32):
        return self.nc.dram_tensor(name, shape, dt, kind="Internal").ap()

    def sb(self, name, shape, dt=F32):
        return self.ctx.enter_context(self.nc.sbuf_tensor(name, shape, dt))

    def wait_alone(self, eng, sem, value):
        eng.wait_ge(sem, value)
        if not isinstance(value, int):
            eng.sem_inc(self.waited, 1)

    def sem(self, name):
        s = self.stage_ctx.enter_context(self.nc.semaphore(name))
        self.stage_sems.append(s)
        return s

    def next_stage(self):
        self.old_ctx.close()
        self.old_ctx, self.old_sems = self.stage_ctx, self.stage_sems
        self.stage_ctx, self.stage_sems = self.ctx.enter_context(ExitStack()), []

    def clear_old(self, sp):
        for s in self.old_sems:
            sp.sem_clear(s)


def at_least(g, n):
    return not isinstance(g, int) or g >= n


def below(g, n):
    return not isinstance(g, int) or g < n


def over(ap, n, axis=1):
    shape = list(ap.shape)
    return ap.unsqueeze(axis).broadcast_to(shape[:axis] + [n] + shape[axis:])


def stage_tokenizer(T):
    nc, t, sem = T.nc, T.t, T.sem
    with ExitStack() as ctx:
        def sb(name, shape, dt=F32):
            return ctx.enter_context(nc.sbuf_tensor(name, shape, dt))

        def ps(name, shape, dt=F32):
            return ctx.enter_context(nc.psum_tensor(name, shape, dt))

        w_proj = sb("tk_w_proj", [D, CIN])
        w_pwT = sb("tk_w_pwT", [D, D])
        w_pw_taps = sb("tk_w_pw_taps", [D, 3, D])
        w_dw = sb("tk_w_dw", [D, 3])
        b_proj = sb("tk_b_proj", [D, 1])
        b_dw = sb("tk_b_dw", [D, 1])
        b_pw = sb("tk_b_pw", [L, D])
        gamma = sb("tk_gamma", [L, D])
        beta = sb("tk_beta", [L, D])
        taps02 = sb("tk_taps02", [2 * CIN, D])
        tap1 = sb("tk_tap1", [CIN, D])
        edge = sb("tk_edge", [D, 3])
        conv_bias = sb("tk_conv_bias", [D, L])
        bias_tok = sb("tk_bias_tok", [L, D])
        x_in = [sb(f"tk_x{p}", [2 * CIN, GB, L + 2]) for p in range(2)]
        pre = [sb(f"tk_pre{p}", [L, GB, D]) for p in range(2)]
        y = [sb(f"tk_y{p}", [L, GB, D]) for p in range(2)]
        z = [sb(f"tk_z{p}", [L, GB, D]) for p in range(2)]
        stats = [sb(f"tk_stats{p}", [L, GB, 6]) for p in range(2)]
        mv = [sb(f"tk_mv{p}", [L, GB, 2]) for p in range(2)]
        var_eps = [sb(f"tk_var_eps{p}", [L, GB]) for p in range(2)]
        rstd = [sb(f"tk_rstd{p}", [L, GB]) for p in range(2)]
        p_w = ps("tk_p_w", [128, 2, D])
        p_bias = ps("tk_p_bias", [L, D])
        p_y = [ps(f"tk_p_y{p}", [L, GB, D]) for p in range(2)]

        weights_in = sem("tk_weights_in")
        ident_zero = sem("tk_ident_zero")
        padded = sem("tk_padded")
        taps_scaled = sem("tk_taps_scaled")
        bias_col = sem("tk_bias_col")
        joined = sem("tk_joined")
        joined_sb = sem("tk_joined_sb")
        x_ready = [sem(f"tk_x_ready{p}") for p in range(2)]
        mm_done = sem("tk_mm_done")
        pre_ready = sem("tk_pre_ready")
        silu_done = sem("tk_silu_done")
        stats_done = sem("tk_stats_done")
        mv_done = sem("tk_mv_done")
        eps_added = sem("tk_eps_added")
        rstd_done = sem("tk_rstd_done")
        z_done = sem("tk_z_done")
        scaled = sem("tk_scaled")
        h_done = sem("tk_h_done")

        block = ctx.enter_context(nc.Block())

        @block.sync
        def _(sp):
            T.clear_old(sp)
            for dst, src in ((w_proj[:], t["w_proj"]), (w_pwT[:], t["w_pwT"]), (w_dw[:], t["w_dw"]),
                             (b_proj[:], t["b_proj"].unsqueeze(1)), (b_dw[:], t["b_dw"].unsqueeze(1)),
                             (b_pw[:], t["b_pw"].partition_broadcast(L)),
                             (gamma[:], t["gamma"].partition_broadcast(L)),
                             (beta[:], t["beta"].partition_broadcast(L))):
                sp.dma_start(dst, src).then_inc(weights_in, 16)

            def load(k, p):
                src = t["x"][bass.ds((2 * k + p) * GB, GB), :, :].rearrange("b c l -> c b l")
                sp.dma_start(x_in[p][0:CIN, :, 1:L + 1], src).then_inc(x_ready[p], 16)
                sp.dma_start(x_in[p][CIN:2 * CIN, :, 0:L - 1], src[:, :, 1:L]).then_inc(x_ready[p], 16)

            sp.wait_ge(padded, 4)
            load(0, 0)
            load(0, 1)
            with sp.Fori(1, NG // 2) as k:
                for p in range(2):
                    sp.wait_ge(mm_done, 2 * k + p - 1)
                    load(k, p)

        @block.gpsimd
        def _(pool):
            pool.memset(T.neg_half[:], -0.5)
            pool.memset(T.eps[:], EPS).then_inc(T.consts_done, 1)
            pool.memset(T.ident[:], 0.0).then_inc(ident_zero, 1)
            pool.wait_ge(ident_zero, 1)
            pool.affine_select(out=T.ident[:], in_=T.ident[:], compare_op=ALU.not_equal, fill=1.0,
                               base=0, pattern=[[-1, 128]], channel_multiplier=1).then_inc(T.consts_done, 1)
            pool.wait_ge(T.consts_done, 2)
            pool.tensor_copy(T.ident_bf[:], T.ident[:]).then_inc(T.consts_done, 1)
            pool.wait_ge(weights_in, 128)

            def finish(k, p):
                g = 2 * k + p
                pool.wait_ge(mv_done, GB * (g + 1))
                pool.tensor_tensor(var_eps[p][:], mv[p][:, :, 1], T.eps[:], ALU.add).then_inc(eps_added, 1)
                pool.wait_ge(eps_added, g + 1)
                pool.tensor_tensor(rstd[p][:], var_eps[p][:], T.neg_half[:], ALU.pow).then_inc(rstd_done, 1)
                pool.wait_ge(z_done, g + 3)
                pool.tensor_tensor(z[p][:], z[p][:], over(gamma[:], GB), ALU.mult).then_inc(scaled, 1)
                pool.wait_ge(scaled, g + 1)
                pool.tensor_tensor(T.H[:, bass.ds(g * GB, GB), :], z[p][:], over(beta[:], GB),
                                   ALU.add).then_inc(h_done, 1)

            with pool.Fori(0, NG // 2) as k:
                for p in range(2):
                    finish(k, p)

        @block.tensor
        def _(pe):
            pe.wait_ge(weights_in, 128)
            pe.wait_ge(taps_scaled, 3)
            pe.matmul(p_w[0:CIN, 0, :], w_proj[:], w_pw_taps[:, 0, :], start=True, stop=True)
            pe.matmul(p_w[CIN:2 * CIN, 0, :], w_proj[:], w_pw_taps[:, 2, :], start=True, stop=True)
            pe.matmul(p_w[0:CIN, 1, :], w_proj[:], w_pw_taps[:, 1, :], start=True, stop=True)
            pe.wait_ge(bias_col, 4)
            pe.matmul(p_bias[:], conv_bias[:], w_pwT[:], start=True, stop=True).then_inc(joined, 1)
            pe.wait_ge(joined_sb, 3)
            with pe.Fori(0, NG // 2) as k:
                for p in range(2):
                    pe.wait_ge(x_ready[p], 32 * k + 32)
                    pe.wait_ge(pre_ready, 2 * k + p + 1)
                    for b in range(GB):
                        pe.matmul(p_y[p][:, b, :], x_in[p][:, b, 0:L], taps02[:], start=True, stop=False)
                        last = pe.matmul(p_y[p][:, b, :], x_in[p][0:CIN, b, 1:L + 1], tap1[:],
                                         start=False, stop=True)
                    last.then_inc(mm_done, 1)

        @block.scalar
        def _(act):
            with act.Fori(0, NG // 2) as k:
                for p in range(2):
                    act.wait_ge(pre_ready, 2 * k + p + 3)
                    act.wait_ge(z_done, 2 * k + p + 1)
                    act.activation(y[p][:], pre[p][:], ACT.Silu).then_inc(silu_done, 1)

        @block.vector
        def _(dve):
            for p in range(2):
                dve.memset(x_in[p][0:CIN, :, 0:1], 0.0)
                dve.memset(x_in[p][0:CIN, :, L + 1:L + 2], 0.0).then_inc(padded, 1)
                dve.memset(x_in[p][CIN:2 * CIN, :, L - 1:L + 2], 0.0).then_inc(padded, 1)
            dve.sem_inc(pre_ready, 2)
            dve.sem_inc(z_done, 2)
            dve.sem_inc(h_done, 2)
            dve.wait_ge(weights_in, 128)
            for j in range(3):
                dve.tensor_scalar(w_pw_taps[:, j, :], w_pwT[:], w_dw[:, j:j + 1], None,
                                  ALU.mult).then_inc(taps_scaled, 1)
            dve.tensor_scalar(edge[:, 0:3], w_dw[:], b_proj[:, 0:1], None, ALU.mult).then_inc(bias_col, 1)
            dve.wait_ge(bias_col, 1)
            dve.tensor_scalar(conv_bias[:], edge[:, 1:2].broadcast_to([D, L]), b_dw[:, 0:1], edge[:, 0:1],
                              ALU.add, ALU.add).then_inc(bias_col, 1)
            dve.wait_ge(bias_col, 2)
            dve.tensor_scalar(conv_bias[:, 0:1], conv_bias[:, 1:2], edge[:, 0:1], None,
                              ALU.subtract).then_inc(bias_col, 1)
            dve.wait_ge(bias_col, 3)
            dve.tensor_scalar(conv_bias[:, 0:L - 1], conv_bias[:, 0:L - 1], edge[:, 2:3], None,
                              ALU.add).then_inc(bias_col, 1)
            dve.wait_ge(joined, 1)
            dve.tensor_copy(taps02[:], p_w[:, 0, :]).then_inc(joined_sb, 1)
            dve.tensor_copy(tap1[:], p_w[0:CIN, 1, :]).then_inc(joined_sb, 1)
            dve.tensor_tensor(bias_tok[:], p_bias[:], b_pw[:], ALU.add).then_inc(joined_sb, 1)
            dve.wait_ge(joined_sb, 3)

            def add_bias(k, p):
                dve.wait_ge(mm_done, 2 * k + p + 1)
                dve.tensor_tensor(pre[p][:], p_y[p][:], over(bias_tok[:], GB), ALU.add).then_inc(pre_ready, 1)

            def moments(k, p):
                g = 2 * k + p
                dve.wait_ge(silu_done, g + 1)
                for b in range(GB):
                    dve.bn_stats(stats[p][:, b, :], y[p][:, b, :]).then_inc(stats_done, 1)
                T.wait_alone(dve, stats_done, GB * (g + 1))
                for b in range(GB):
                    dve.bn_aggr(mv[p][:, b, :], stats[p][:, b, :]).then_inc(mv_done, 1)

            def normalize(k, p):
                g = 2 * k + p
                dve.wait_ge(rstd_done, g + 1)
                dve.wait_ge(h_done, g + 1)
                for b in range(GB):
                    last = dve.tensor_scalar(z[p][:, b, :], y[p][:, b, :], mv[p][:, b, 0:1],
                                             rstd[p][:, b:b + 1], ALU.subtract, ALU.mult)
                last.then_inc(z_done, 1)

            add_bias(0, 0)
            with dve.Fori(0, NG // 2 - 1) as k:
                for p in range(2):
                    moments(k, p)
                    add_bias(k + p, 1 - p)
                    normalize(k, p)
            moments(NG // 2 - 1, 0)
            add_bias(NG // 2 - 1, 1)
            normalize(NG // 2 - 1, 0)
            moments(NG // 2 - 1, 1)
            normalize(NG // 2 - 1, 1)


def stage_attention(T):
    nc, t, sem = T.nc, T.t, T.sem
    HALF = NH // 2
    NHF = 2 * GB
    with ExitStack() as ctx:
        def sb(name, shape, dt=F32):
            return ctx.enter_context(nc.sbuf_tensor(name, shape, dt))

        def ps(name, shape, dt=F32):
            return ctx.enter_context(nc.psum_tensor(name, shape, dt))

        w_qkvT = sb("at_w_qkvT", [D, 3, D])
        w_aggT = sb("at_w_aggT", [D, D])
        b_agg = sb("at_b_agg", [L, D])
        head_mask = T.head_mask
        pick = sb("at_pick", [GB * 2 * NH, GB, NH, L], BF16)
        stats = sb("at_stats", [L, GB, 6])
        mv = sb("at_mv", [L, GB, 2])
        var_eps = sb("at_var_eps", [L, GB])
        rstd = sb("at_rstd", [L, GB])
        z = [sb(f"at_z{p}", [L, GB, D]) for p in range(2)]
        zT = [sb(f"at_zT{p}", [D, GB, L]) for p in range(2)]
        q_sb = [sb(f"at_q{p}", [D, GB, L]) for p in range(2)]
        k_sb = sb("at_k", [D, GB, L])
        k_heads = [sb(f"at_k_heads{p}", [D, NH, GB, L]) for p in range(2)]
        v_ones = [sb(f"at_v_ones{p}", [L, GB, NH, DH + 1]) for p in range(2)]
        top = sb("at_top", [L, GB, NH])
        neg_top = sb("at_neg_top", [L, GB, 2, NH], BF16)
        neg_topT = sb("at_neg_topT", [GB * 2 * NH, L], BF16)
        probsT = [sb(f"at_probsT{i}", [L, HALF, L]) for i in range(2)]
        inv_sum = sb("at_inv_sum", [L, GB, NH])
        heads_out = sb("at_heads_out", [L, GB, D])
        heads_outT = sb("at_heads_outT", [D, GB, L])
        p_s = [ps(f"at_p_s{i}", [128, 512]) for i in range(2)]
        p_st = [ps(f"at_p_st{i}", [L, HALF, L]) for i in range(2)]
        p_o = [ps(f"at_p_o{i}", [L, 2, NH, DH + 1]) for i in range(2)]
        p_agg = ps("at_p_agg", [128, 512])
        p_q = ps("at_p_q", [128, 512])

        def tokens(bank, rows=L):
            return bank[0:rows, :].rearrange("p (b d) -> p b d", b=GB)

        def features(bank):
            return bank[:, 0:GT].rearrange("p (b l) -> p b l", b=GB)

        neg_topT_ps = p_s[0][:, :].bitcast(BF16)[0:GB * 2 * NH, 0:L]

        weights_in = sem("at_weights_in")
        pool_consts = sem("at_pool_consts")
        stats_done = sem("at_stats_done")
        mv_done = sem("at_mv_done")
        eps_added = sem("at_eps_added")
        rstd_done = sem("at_rstd_done")
        z_done = sem("at_z_done")
        zT_made = sem("at_zT_made")
        zT_kept = sem("at_zT_kept")
        q_made = sem("at_q_made")
        k_made = sem("at_k_made")
        v_made = sem("at_v_made")
        q_kept = sem("at_q_kept")
        k_kept = sem("at_k_kept")
        v_kept = sem("at_v_kept")
        k_masked = sem("at_k_masked")
        bias_added = sem("at_bias_added")
        s_made = sem("at_s_made")
        top_done = sem("at_top_done")
        neg_hi = sem("at_neg_hi")
        neg_lo = sem("at_neg_lo")
        negT_made = sem("at_negT_made")
        negT_kept = sem("at_negT_kept")
        st_made = sem("at_st_made")
        exp_done = sem("at_exp_done")
        pv_done = sem("at_pv_done")
        inv_done = sem("at_inv_done")
        out_done = sem("at_out_done")
        outT_made = sem("at_outT_made")
        outT_kept = sem("at_outT_kept")
        agg_made = sem("at_agg_made")
        h_done = sem("at_h_done")

        block = ctx.enter_context(nc.Block())

        @block.sync
        def _(sp):
            T.clear_old(sp)
            sp.dma_start(w_qkvT[:], t["w_qkvT"].rearrange("d (j e) -> d j e", j=3)).then_inc(weights_in, 16)
            sp.dma_start(w_aggT[:], t["w_aggT"]).then_inc(weights_in, 16)
            sp.dma_start(b_agg[:], t["b_agg"].partition_broadcast(L)).then_inc(weights_in, 16)

        @block.gpsimd
        def _(pool):
            pool.memset(head_mask[:], 1.0).then_inc(pool_consts, 1)
            pool.memset(pick[:], 0.0).then_inc(pool_consts, 1)
            pool.wait_ge(pool_consts, 2)
            pool.affine_select(out=head_mask[:], in_=head_mask[:], compare_op=ALU.is_ge, fill=0.0,
                               base=0, pattern=[[-DH, NH]], channel_multiplier=1).then_inc(pool_consts, 1)
            pool.wait_ge(pool_consts, 3)
            pool.affine_select(out=head_mask[:], in_=head_mask[:], compare_op=ALU.is_ge, fill=0.0,
                               base=DH - 1, pattern=[[DH, NH]], channel_multiplier=-1).then_inc(pool_consts, 1)
            for part in range(2):
                pool.wait_ge(pool_consts, 4 + part)
                pool.affine_select(out=pick[:], in_=pick[:], compare_op=ALU.not_equal, fill=1.0,
                                   base=-NH * part, pattern=[[-2 * NH, GB], [-1, NH], [0, L]],
                                   channel_multiplier=1).then_inc(pool_consts, 1)
            pool.wait_ge(pool_consts, 6)

            def rstd_of(g):
                pool.wait_ge(mv_done, GB * (g + 1))
                pool.tensor_tensor(var_eps[:], mv[:, :, 1], T.eps[:], ALU.add).then_inc(eps_added, 1)
                pool.wait_ge(eps_added, g + 1)
                pool.tensor_tensor(rstd[:], var_eps[:], T.neg_half[:], ALU.pow).then_inc(rstd_done, 1)

            def mask_k(g, p):
                T.wait_alone(pool, k_kept, g + 1)
                if at_least(g, 2):
                    T.wait_alone(pool, st_made, NHF * (g - 1))
                for h in range(NH):
                    last = pool.tensor_scalar(k_heads[p][:, h], k_sb[:], head_mask[:, h:h + 1], 1.0, ALU.mult,
                                              ALU.mult)
                last.then_inc(k_masked, 1)

            def add_b_agg(g):
                rows = T.H[:, bass.ds(g * GB, GB), :]
                pool.wait_ge(z_done, g + 1)
                pool.tensor_tensor(rows, rows, over(b_agg[:], GB), ALU.add).then_inc(bias_added, 1)

            pool.wait_ge(weights_in, 48)
            rstd_of(0)
            rstd_of(1)
            mask_k(0, 0)
            add_b_agg(0)

            def turn(g, p):
                if below(g, NG - 2):
                    rstd_of(g + 2)
                if below(g, NG - 1):
                    mask_k(g + 1, 1 - p)
                    add_b_agg(g + 1)

            turn(0, 0)
            with pool.Fori(0, NG // 2 - 2) as k:
                turn(2 * k + 1, 1)
                turn(2 * k + 2, 0)
            turn(NG - 3, 1)
            turn(NG - 2, 0)
            turn(NG - 1, 1)

        @block.tensor
        def _(pe):
            pe.wait_ge(weights_in, 48)
            pe.wait_ge(pool_consts, 6)

            def z_transposes(g, p):
                T.wait_alone(pe, z_done, g + 1)
                if at_least(g, 1):
                    T.wait_alone(pe, q_kept, g)
                for b in range(GB):
                    last = pe.transpose(features(p_q)[:, b, :], z[p][:, b, :], T.ident[0:L, 0:L])
                last.then_inc(zT_made, 1)

            def qkv(g, p):
                pe.wait_ge(zT_kept, g + 1)
                pe.matmul(features(p_q), w_qkvT[:, 0, :], zT[p][:], start=True, stop=True).then_inc(q_made, 1)
                pe.matmul(features(p_s[1]), w_qkvT[:, 1, :], zT[p][:], start=True, stop=True).then_inc(k_made, 1)
                if at_least(g, 1):
                    pe.wait_ge(negT_kept, g)
                for b in range(GB):
                    last = pe.matmul(tokens(p_s[0])[:, b, :], zT[p][:, b, :], w_qkvT[:, 2, :],
                                     start=True, stop=True)
                last.then_inc(v_made, 1)

            def scores(g, p):
                pe.wait_ge(k_masked, g + 1)
                pe.wait_ge(q_kept, g + 1)
                pe.wait_ge(v_kept, g + 1)
                for f in range(NHF):
                    b, half = f // 2, f % 2
                    if f >= 2:
                        pe.wait_ge(top_done, NHF * g + f - 1)
                    pe.matmul(p_s[half][0:L, 0:HALF * L].rearrange("n (h m) -> n h m", h=HALF),
                              q_sb[p][:, b, :], k_heads[p][:, half * HALF:(half + 1) * HALF, b, :],
                              start=True, stop=True).then_inc(s_made, 1)

            def maxima_transpose(g):
                T.wait_alone(pe, neg_lo, g + 1)
                pe.transpose(neg_topT_ps, neg_top[:].rearrange("n b s h -> n (b s h)"),
                             T.ident_bf[0:L, 0:L]).then_inc(negT_made, 1)

            def scoresT_and_values(g, p):
                pe.wait_ge(negT_kept, g + 1)
                if at_least(g, 1):
                    pe.wait_ge(out_done, 2 * g)
                for f in range(NHF + 1):
                    if f < NHF:
                        b, half = f // 2, f % 2
                        if at_least(g, 1) or f >= 2:
                            pe.wait_ge(exp_done, NHF * g + f - 1)
                        for j in range(HALF):
                            h = half * HALF + j
                            pe.matmul(p_st[half][:, j, :], k_heads[p][:, h, b, :], q_sb[p][:, b, :],
                                      start=True, stop=False)
                            last = pe.matmul(p_st[half][:, j, :], pick[:, b, h, :], neg_topT[:],
                                             start=False, stop=True)
                        last.then_inc(st_made, 1)
                    if f >= 1:
                        b, half = (f - 1) // 2, (f - 1) % 2
                        pe.wait_ge(exp_done, NHF * g + f)
                        for j in range(HALF):
                            h = half * HALF + j
                            last = pe.matmul(p_o[b // 2][:, b % 2, h, :], probsT[half][:, j, :],
                                             v_ones[p][:, b, h, :], start=True, stop=True)
                        last.then_inc(pv_done, 1)

            def out_transposes(g):
                T.wait_alone(pe, out_done, 2 * (g + 1))
                if at_least(g, 1):
                    T.wait_alone(pe, h_done, g)
                for b in range(GB):
                    last = pe.transpose(features(p_agg)[:, b, :], heads_out[:, b, :], T.ident[0:L, 0:L])
                last.then_inc(outT_made, 1)

            def aggregate(g):
                pe.wait_ge(outT_kept, g + 1)
                for b in range(GB):
                    last = pe.matmul(tokens(p_agg)[:, b, :], heads_outT[:, b, :], w_aggT[:],
                                     start=True, stop=True)
                last.then_inc(agg_made, 1)

            def turn(g, p):
                first, final = not at_least(g, 1), not below(g, NG - 1)
                scores(g, p)
                if not first:
                    out_transposes(g - 1)
                if not final:
                    z_transposes(g + 1, 1 - p)
                maxima_transpose(g)
                if not first:
                    aggregate(g - 1)
                if not final:
                    qkv(g + 1, 1 - p)
                scoresT_and_values(g, p)

            z_transposes(0, 0)
            qkv(0, 0)
            turn(0, 0)
            with pe.Fori(0, NG // 2 - 1) as k:
                turn(2 * k + 1, 1)
                turn(2 * k + 2, 0)
            turn(NG - 1, 1)
            out_transposes(NG - 1)
            aggregate(NG - 1)

        @block.scalar
        def _(act):
            def keep_qk(g, p):
                act.wait_ge(zT_made, g + 1)
                if at_least(g, 2):
                    act.wait_ge(v_made, g - 1)
                act.copy(zT[p][:], features(p_q)).then_inc(zT_kept, 1)
                act.wait_ge(q_made, g + 1)
                if at_least(g, 2):
                    act.wait_ge(st_made, NHF * (g - 1))
                act.mul(q_sb[p][:], features(p_q), DH ** -0.5).then_inc(q_kept, 1)
                act.wait_ge(k_made, g + 1)
                if at_least(g, 1):
                    act.wait_ge(k_masked, g)
                act.copy(k_sb[:], features(p_s[1])).then_inc(k_kept, 1)

            def keep_outT(g):
                act.wait_ge(outT_made, g + 1)
                if at_least(g, 1):
                    act.wait_ge(agg_made, g)
                act.copy(heads_outT[:], features(p_agg)).then_inc(outT_kept, 1)

            def exponentials(g):
                for f in range(NHF):
                    act.wait_ge(st_made, NHF * g + f + 1)
                    if at_least(g, 1) or f >= 2:
                        act.wait_ge(pv_done, NHF * g + f - 1)
                    act.activation(probsT[f % 2][:], p_st[f % 2][:], ACT.Exp).then_inc(exp_done, 1)

            def turn(g, p):
                if at_least(g, 1):
                    keep_outT(g - 1)
                if below(g, NG - 1):
                    keep_qk(g + 1, 1 - p)
                exponentials(g)

            keep_qk(0, 0)
            turn(0, 0)
            with act.Fori(0, NG // 2 - 1) as k:
                turn(2 * k + 1, 1)
                turn(2 * k + 2, 0)
            turn(NG - 1, 1)
            keep_outT(NG - 1)

        @block.vector
        def _(dve):
            for p in range(2):
                dve.memset(v_ones[p][:], 1.0)

            def norm_in(g, p):
                for b in range(GB):
                    dve.bn_stats(stats[:, b, :], T.H[:, g * GB + b, :]).then_inc(stats_done, 1)
                T.wait_alone(dve, stats_done, GB * (g + 1))
                for b in range(GB):
                    dve.bn_aggr(mv[:, b, :], stats[:, b, :]).then_inc(mv_done, 1)
                T.wait_alone(dve, rstd_done, g + 1)
                if at_least(g, 2):
                    T.wait_alone(dve, zT_made, g - 1)
                for b in range(GB):
                    last = dve.tensor_scalar(z[p][:, b, :], T.H[:, g * GB + b, :], mv[:, b, 0:1],
                                             rstd[:, b:b + 1], ALU.subtract, ALU.mult)
                last.then_inc(z_done, 1)

            def keep_v(g, p):
                dve.wait_ge(v_made, g + 1)
                if at_least(g, 2):
                    dve.wait_ge(pv_done, NHF * (g - 1))
                dve.tensor_copy(v_ones[p][:, :, :, 0:DH],
                                p_s[0][0:L, :].rearrange("p (b h d) -> p b h d", b=GB, h=NH)).then_inc(v_kept, 1)

            def maxima(g):
                for f in range(NHF):
                    b, half = f // 2, f % 2
                    dve.wait_ge(s_made, NHF * g + f + 1)
                    dve.tensor_reduce(top[:, b, half * HALF:(half + 1) * HALF],
                                      p_s[half][0:L, 0:HALF * L].rearrange("n (h m) -> n h m", h=HALF),
                                      AX_X, ALU.max).then_inc(top_done, 1)
                dve.wait_ge(top_done, NHF * (g + 1))
                dve.tensor_scalar(neg_top[:, :, 0, :], top[:], -1.0, None, ALU.mult).then_inc(neg_hi, 1)
                dve.wait_ge(neg_hi, g + 1)
                dve.scalar_tensor_tensor(out=neg_top[:, :, 1, :], in0=top[:], scalar=-1.0,
                                         in1=neg_top[:, :, 0, :], op0=ALU.mult,
                                         op1=ALU.subtract).then_inc(neg_lo, 1)

            def keep_maxima(g):
                dve.wait_ge(negT_made, g + 1)
                dve.tensor_copy(neg_topT[:], neg_topT_ps).then_inc(negT_kept, 1)

            def divide(g):
                for i in range(2):
                    dve.wait_ge(pv_done, NHF * g + 4 * (i + 1))
                    dve.reciprocal(inv_sum[:, 2 * i:2 * i + 2, :], p_o[i][:, :, :, DH]).then_inc(inv_done, 1)
                    dve.wait_ge(inv_done, 2 * g + i + 1)
                    if at_least(g, 1):
                        dve.wait_ge(outT_made, g)
                    dve.tensor_tensor(heads_out[:, 2 * i:2 * i + 2, :].rearrange("n b (h d) -> n b h d", h=NH),
                                      p_o[i][:, :, :, 0:DH], over(inv_sum[:, 2 * i:2 * i + 2, :], DH, 3),
                                      ALU.mult).then_inc(out_done, 1)

            def add_to_h(g):
                dve.wait_ge(agg_made, g + 1)
                dve.wait_ge(bias_added, g + 1)
                rows = T.H[:, bass.ds(g * GB, GB), :]
                dve.tensor_tensor(rows, rows, tokens(p_agg), ALU.add).then_inc(h_done, 1)

            def turn(g, p):
                first, final = not at_least(g, 1), not below(g, NG - 1)
                if not first:
                    divide(g - 1)
                maxima(g)
                keep_maxima(g)
                if not first:
                    add_to_h(g - 1)
                if not final:
                    keep_v(g + 1, 1 - p)
                if below(g, NG - 2):
                    norm_in(g + 2, p)

            norm_in(0, 0)
            norm_in(1, 1)
            keep_v(0, 0)
            turn(0, 0)
            with dve.Fori(0, NG // 2 - 2) as k:
                turn(2 * k + 1, 1)
                turn(2 * k + 2, 0)
            turn(NG - 3, 1)
            turn(NG - 2, 0)
            turn(NG - 1, 1)
            divide(NG - 1)
            add_to_h(NG - 1)


def stage_router_logits(T):
    nc, t, sem = T.nc, T.t, T.sem
    with ExitStack() as ctx:
        def sb(name, shape, dt=F32):
            return ctx.enter_context(nc.sbuf_tensor(name, shape, dt))

        def ps(name, shape, dt=F32):
            return ctx.enter_context(nc.psum_tensor(name, shape, dt))

        w_router = sb("rl_w_router", [D, E])
        stats = sb("rl_stats", [L, GB, 6])
        mv = sb("rl_mv", [L, GB, 2])
        var_eps = sb("rl_var_eps", [L, GB])
        rstd = sb("rl_rstd", [L, GB])
        z = [sb(f"rl_z{p}", [L, GB, D]) for p in range(2)]
        zT = [sb(f"rl_zT{p}", [D, GB, L]) for p in range(2)]
        logits = [sb(f"rl_logits{p}", [E, GT]) for p in range(2)]
        p_zT = [ps(f"rl_p_zT{p}", [D, GB, L]) for p in range(2)]
        p_logits = [ps(f"rl_p_logits{p}", [E, GT]) for p in range(2)]

        weights_in = sem("rl_weights_in")
        stats_done = sem("rl_stats_done")
        mv_done = sem("rl_mv_done")
        eps_added = sem("rl_eps_added")
        rstd_done = sem("rl_rstd_done")
        z_done = sem("rl_z_done")
        z_stored = [sem(f"rl_z_stored{p}") for p in range(2)]
        zT_made = sem("rl_zT_made")
        zT_kept = sem("rl_zT_kept")
        logits_made = sem("rl_logits_made")
        logits_kept = sem("rl_logits_kept")
        logits_stored = [sem(f"rl_logits_stored{p}") for p in range(2)]
        h_stored = sem("rl_h_stored")

        block = ctx.enter_context(nc.Block())

        @block.sync
        def _(sp):
            T.clear_old(sp)
            sp.dma_start(w_router[:], t["w_router"]).then_inc(weights_in, 16)
            sp.dma_start(T.h_rows.rearrange("(b l) d -> l b d", l=L), T.H[:]).then_inc(h_stored, 16)
            z_rows = T.z_rows.rearrange("(b l) c -> l b c", l=L)
            with sp.Fori(0, NG // 2) as k:
                for p in range(2):
                    g = 2 * k + p
                    sp.wait_ge(z_done, g + 1)
                    sp.dma_start(z_rows[:, bass.ds(g * GB, GB), 0:D], z[p][:]).then_inc(z_stored[p], 16)
                    sp.wait_ge(logits_kept, g + 1)
                    sp.dma_start(T.logits[:, bass.ds(g * GT, GT)], logits[p][:]).then_inc(logits_stored[p], 16)
            sp.wait_ge(h_stored, 16)
            for p in range(2):
                sp.wait_ge(z_stored[p], 16 * (NG // 2))
                sp.wait_ge(logits_stored[p], 16 * (NG // 2))

        @block.gpsimd
        def _(pool):
            with pool.Fori(0, NG) as g:
                pool.wait_ge(mv_done, GB * (g + 1))
                pool.tensor_tensor(var_eps[:], mv[:, :, 1], T.eps[:], ALU.add).then_inc(eps_added, 1)
                pool.wait_ge(eps_added, g + 1)
                pool.tensor_tensor(rstd[:], var_eps[:], T.neg_half[:], ALU.pow).then_inc(rstd_done, 1)

        @block.tensor
        def _(pe):
            pe.wait_ge(weights_in, 16)

            def transposes(g, p):
                T.wait_alone(pe, z_done, g + 1)
                if at_least(g, 2):
                    T.wait_alone(pe, zT_kept, g - 1)
                for b in range(GB):
                    last = pe.transpose(p_zT[p][:, b, :], z[p][:, b, :], T.ident[0:L, 0:L])
                last.then_inc(zT_made, 1)

            def route(g, p):
                T.wait_alone(pe, zT_kept, g + 1)
                if at_least(g, 2):
                    T.wait_alone(pe, logits_kept, g - 1)
                pe.matmul(p_logits[p][:], w_router[:], zT[p][:], start=True, stop=True).then_inc(logits_made, 1)

            transposes(0, 0)
            transposes(1, 1)
            route(0, 0)
            with pe.Fori(1, NG // 2) as k:
                transposes(2 * k, 0)
                route(2 * k - 1, 1)
                transposes(2 * k + 1, 1)
                route(2 * k, 0)
            route(NG - 1, 1)

        @block.scalar
        def _(act):
            with act.Fori(0, NG // 2) as k:
                for p in range(2):
                    act.wait_ge(zT_made, 2 * k + p + 1)
                    act.wait_ge(logits_made, 2 * k + p + 1)
                    act.copy(zT[p][:], p_zT[p][:]).then_inc(zT_kept, 1)

        @block.vector
        def _(dve):
            dve.sem_inc(logits_made, 2)

            def norm(g, p, w):
                for b in range(GB):
                    dve.bn_stats(stats[:, b, :], T.H[:, g * GB + b, :]).then_inc(stats_done, 1)
                T.wait_alone(dve, stats_done, GB * (g + 1))
                for b in range(GB):
                    dve.bn_aggr(mv[:, b, :], stats[:, b, :]).then_inc(mv_done, 1)
                T.wait_alone(dve, rstd_done, g + 1)
                if at_least(g, 2):
                    T.wait_alone(dve, zT_made, g - 1)
                    T.wait_alone(dve, z_stored[p], 16 * w)
                for b in range(GB):
                    last = dve.tensor_scalar(z[p][:, b, :], T.H[:, g * GB + b, :], mv[:, b, 0:1],
                                             rstd[:, b:b + 1], ALU.subtract, ALU.mult)
                last.then_inc(z_done, 1)

            def keep_logits(g, p, w):
                dve.wait_ge(logits_made, g + 3)
                if at_least(g, 2):
                    dve.wait_ge(logits_stored[p], 16 * w)
                dve.tensor_copy(logits[p][:], p_logits[p][:]).then_inc(logits_kept, 1)

            norm(0, 0, 0)
            norm(1, 1, 0)
            keep_logits(0, 0, 0)
            norm(2, 0, 1)
            keep_logits(1, 1, 0)
            norm(3, 1, 1)
            with dve.Fori(2, NG // 2) as k:
                keep_logits(2 * k - 2, 0, k - 1)
                norm(2 * k, 0, k)
                keep_logits(2 * k - 1, 1, k - 1)
                norm(2 * k + 1, 1, k)
            keep_logits(NG - 2, 0, NG // 2 - 1)
            keep_logits(NG - 1, 1, NG // 2 - 1)


def stage_choose(T):
    nc, t, sem = T.nc, T.t, T.sem
    R = 128 // E
    C = N // R
    assert C == GT
    LO = 32
    HI = CAP // LO
    tiles = E * CAP // 128
    PB = 8
    NCH = B // PB
    with ExitStack() as ctx:
        def sb(name, shape, dt=F32):
            return ctx.enter_context(nc.sbuf_tensor(name, shape, dt))

        def ps(name, shape, dt=F32):
            return ctx.enter_context(nc.psum_tensor(name, shape, dt))

        logit = sb("ch_logit", [128, C])
        u = sb("ch_u", [128, C])
        weight = sb("ch_weight", [128, C])
        same = sb("ch_same", [128, 128])
        before = sb("ch_before", [128, 128])
        ones = sb("ch_ones", [128, C])
        scratch = sb("ch_scratch", [128, C])
        lower = sb("ch_lower", [128, C])
        equal = sb("ch_equal", [128, C])
        tied = sb("ch_tied", [128, C])
        taken = sb("ch_taken", [128, C])
        count = sb("ch_count", [128, C])
        slot = sb("ch_slot", [128, C])
        row_max = sb("ch_row_max", [128, 1])
        max_e = sb("ch_max_e", [1, E])
        max_row = sb("ch_max_row", [1, E, R])
        top = sb("ch_top", [128, 1])
        row_sum = sb("ch_row_sum", [128, 1])
        inv_sum = sb("ch_inv_sum", [128, 1])
        kth = sb("ch_kth", [128, 1], I32)
        bit = sb("ch_bit", [128, 1])
        bit_int = sb("ch_bit_int", [128, 1], I32)
        trial = sb("ch_trial", [128, 1], I32)
        gain = sb("ch_gain", [128, 1], I32)
        row_count = sb("ch_row_count", [128, 1])
        tie_room = sb("ch_tie_room", [128, 1])
        ahead = sb("ch_ahead", [128, 2])
        weightT = sb("ch_weightT", [L, B, E])
        slot_int = sb("ch_slot_int", [L, GB, 128], I32)
        hi_int = sb("ch_hi_int", [L, GB, 128], I32)
        lo_int = sb("ch_lo_int", [L, GB, 128], I32)
        hi = sb("ch_hi", [L, B, E], BF16)
        lo = sb("ch_lo", [L, B, E], BF16)
        iota = sb("ch_iota", [L, LO], BF16)
        iota_int = sb("ch_iota_int", [L, LO], I32)
        seq_no = sb("ch_seq_no", [L, B, E], BF16)
        seq_no_int = sb("ch_seq_no_int", [L, B, E], I32)
        tok_no = sb("ch_tok_no", [L, 1])
        tok_no_int = sb("ch_tok_no_int", [L, 1], I32)
        hot_hi = [sb(f"ch_hot_hi{p}", [L, PB * E, HI], BF16) for p in range(2)]
        hot_lo = [sb(f"ch_hot_lo{p}", [L, PB * E, LO], BF16) for p in range(2)]
        numbers = [sb(f"ch_numbers{p}", [L, PB * E, 2, LO], BF16) for p in range(2)]
        zeros = sb("ch_zeros", [L, 2 * LO], BF16)
        rows_f = sb("ch_rows_f", [128, E // 4, LO])
        rows_t = sb("ch_rows_t", [tiles, 128])
        p_small = ps("ch_p_small", [128, 512])
        p_tot = ps("ch_p_tot", [128, 1])
        p_slot = ps("ch_p_slot", [L, GB, 128])
        p_weight = ps("ch_p_weight", [L, GB, 128])
        p_chosen = ps("ch_p_chosen", [128, tiles])
        p_rows = [ps(f"ch_p_rows{i}", [128, 2, LO]) for i in range(E // 4)]

        loaded = sem("ch_loaded")
        consts = sem("ch_consts")
        small = sem("ch_small")
        max_made = sem("ch_max_made")
        max_spread = sem("ch_max_spread")
        u_done = sem("ch_u_done")
        exp_done = sem("ch_exp_done")
        sum_made = sem("ch_sum_made")
        weight_done = sem("ch_weight_done")
        trial_done = sem("ch_trial_done")
        counted = sem("ch_counted")
        total_made = sem("ch_total_made")
        gain_done = sem("ch_gain_done")
        kth_done = sem("ch_kth_done")
        bit_done = sem("ch_bit_done")
        marked = sem("ch_marked")
        offsets_made = sem("ch_offsets_made")
        slot_done = sem("ch_slot_done")
        turned = sem("ch_turned")
        weightT_kept = sem("ch_weightT_kept")
        parts_done = sem("ch_parts_done")
        hot_done = sem("ch_hot_done")
        lo_hot_done = sem("ch_lo_hot_done")
        tok_numbered = sem("ch_tok_numbered")
        seq_numbered = sem("ch_seq_numbered")
        chunk_used = sem("ch_chunk_used")
        rows_made = sem("ch_rows_made")
        rows_out = sem("ch_rows_out")
        rows_back = sem("ch_rows_back")
        rows_turned = sem("ch_rows_turned")
        chosen_done = sem("ch_chosen_done")
        weights_stored = sem("ch_weights_stored")

        block = ctx.enter_context(nc.Block())

        @block.sync
        def _(sp):
            T.clear_old(sp)
            sp.dma_start(logit[:], T.logits.rearrange("e (r c) -> (e r) c", r=R)).then_inc(loaded, 16)
            sp.wait_ge(weightT_kept, 1)
            sp.dma_start(T.z_rows.rearrange("(b l) c -> l b c", l=L)[:, :, D:D + E],
                         weightT[:]).then_inc(weights_stored, 16)
            sp.wait_ge(slot_done, 1 + E // 4)
            sp.dma_start(T.chosen_rows.rearrange("(g p c) -> p g c", p=128, c=LO), rows_f[:]).then_inc(rows_out, 16)
            sp.wait_ge(rows_out, 16)
            sp.dma_start(rows_t[:], T.chosen_rows.rearrange("(t p) -> t p", p=128)).then_inc(rows_back, 16)
            sp.wait_ge(weights_stored, 16)

        @block.gpsimd
        def _(pool):
            pool.memset(same[:], 1.0).then_inc(consts, 1)
            pool.wait_ge(consts, 1)
            sameb = same[:].rearrange("p (e r) -> p e r", e=E)
            pool.affine_select(out=sameb, in_=sameb, compare_op=ALU.is_ge, fill=0.0, base=0,
                               pattern=[[-R, E], [0, R]], channel_multiplier=1).then_inc(consts, 1)
            pool.wait_ge(consts, 2)
            pool.affine_select(out=sameb, in_=sameb, compare_op=ALU.is_ge, fill=0.0, base=R - 1,
                               pattern=[[R, E], [0, R]], channel_multiplier=-1).then_inc(consts, 1)
            pool.wait_ge(consts, 3)
            pool.affine_select(out=before[:], in_=same[:], compare_op=ALU.is_gt, fill=0.0, base=0,
                               pattern=[[1, 128]], channel_multiplier=-1).then_inc(consts, 1)
            pool.iota(iota_int[:], pattern=[[1, LO]], base=0, channel_multiplier=0).then_inc(consts, 1)
            pool.iota(seq_no_int[:], pattern=[[1, B], [0, E]], base=0, channel_multiplier=0).then_inc(consts, 1)
            pool.iota(tok_no_int[:], pattern=[[0, 1]], base=0, channel_multiplier=1).then_inc(consts, 1)
            pool.memset(zeros[:], 0.0)
            pool.wait_ge(consts, 7)
            pool.tensor_copy(iota[:], iota_int[:]).then_inc(consts, 1)
            pool.tensor_copy(seq_no[:], seq_no_int[:]).then_inc(consts, 1)
            pool.tensor_copy(tok_no[:], tok_no_int[:]).then_inc(consts, 1)
            pool.wait_ge(consts, 10)

            def number_sequences(c, p):
                T.wait_alone(pool, lo_hot_done, c + 1)
                T.wait_alone(pool, chunk_used, c + 1)
                pool.tensor_tensor(numbers[p][:, :, 1, :], hot_lo[p][:],
                                   over(seq_no[:, bass.ds(c * PB, PB), :].rearrange("l b e -> l (b e)"), LO, 2),
                                   ALU.mult).then_inc(seq_numbered, 1)

            with pool.Fori(0, NCH // 2) as k:
                for p in range(2):
                    number_sequences(2 * k + p, p)

        @block.tensor
        def _(pe):
            pe.wait_ge(small, 1)
            pe.matmul(p_small[0:1, 0:128], row_max[:], T.ident[:], start=True, stop=True).then_inc(max_made, 1)
            pe.wait_ge(small, 3)
            pe.matmul(p_small[:, 128:129], max_row[:].rearrange("o e r -> o (e r)"), ones[0:1, 0:1],
                      start=True, stop=True).then_inc(max_spread, 1)
            pe.wait_ge(consts, 10)
            pe.wait_ge(exp_done, 1)
            pe.matmul(p_small[:, 129:130], same[:], row_sum[:], start=True, stop=True).then_inc(sum_made, 1)
            with pe.Fori(0, 31) as i:
                T.wait_alone(pe, counted, i + 1)
                pe.matmul(p_tot[:], same[:], row_count[:], start=True, stop=True).then_inc(total_made, 1)
            pe.wait_ge(marked, 1)
            pe.matmul(p_tot[:], same[:], row_count[:], start=True, stop=True).then_inc(offsets_made, 1)
            pe.wait_ge(marked, 3)
            pe.matmul(p_small[:, 130:131], before[:], count[:, C - 1:C], start=True, stop=True).then_inc(offsets_made, 1)
            pe.wait_ge(weight_done, 1)
            for i in range(GB):
                last = pe.transpose(p_weight[:, i, :], weight[:, i * L:(i + 1) * L], T.ident[:])
            last.then_inc(turned, 1)
            pe.wait_ge(marked, 6)
            pe.matmul(p_small[:, 131:132], before[:], count[:, C - 1:C], start=True, stop=True).then_inc(offsets_made, 1)
            pe.wait_ge(slot_done, 1)
            for i in range(GB):
                last = pe.transpose(p_slot[:, i, :], slot[:, i * L:(i + 1) * L], T.ident[:])
            last.then_inc(turned, 1)

            def sums(lhsT, rhs, e, **flags):
                q = e % 4
                return pe.matmul(p_rows[e // 4][HI * q:HI * (q + 1), :, :].rearrange("h s c -> h (s c)"), lhsT, rhs,
                                 skip_group_check=True, **flags)

            for e in range(E):
                sums(zeros[:, 0:HI], zeros[:], e, start=True, stop=False)
            with pe.Fori(0, NCH // 2) as k:
                for p in range(2):
                    c = 2 * k + p
                    T.wait_alone(pe, hot_done, c + 1)
                    T.wait_alone(pe, tok_numbered, c + 1)
                    T.wait_alone(pe, seq_numbered, c + 1)
                    for b in range(PB):
                        for e in range(E):
                            i = b * E + e
                            last = sums(hot_hi[p][:, i, :], numbers[p][:, i, :, :].rearrange("l s c -> l (s c)"), e,
                                        start=False, stop=False)
                    last.then_inc(chunk_used, 1)
            for e in range(E):
                last = sums(zeros[:, 0:HI], zeros[:], e, start=False, stop=True)
            last.then_inc(rows_made, 1)
            pe.wait_ge(rows_back, 16)
            pe.transpose(p_chosen[:], rows_t[:], T.ident[0:tiles, 0:tiles]).then_inc(rows_turned, 1)

        @block.scalar
        def _(act):
            act.wait_ge(u_done, 1)
            act.activation(weight[:], u[:], ACT.Exp, scale=-1.0, accum_out=row_sum[:]).then_inc(exp_done, 1)
            act.wait_ge(consts, 10)

            def number_tokens(c, p):
                act.wait_ge(lo_hot_done, c + 1)
                act.wait_ge(chunk_used, c + 1)
                act.activation(numbers[p][:, :, 0, :], hot_lo[p][:], ACT.Copy, scale=tok_no[:, 0:1]).then_inc(tok_numbered, 1)

            with act.Fori(0, NCH // 2) as k:
                for p in range(2):
                    number_tokens(2 * k + p, p)

        @block.vector
        def _(dve):
            dve.sem_inc(chunk_used, 2)
            dve.memset(ones[:], 1.0).then_inc(bit_done, 1)
            dve.memset(kth[:], 0).then_inc(kth_done, 1)
            dve.memset(bit[:], float(2 ** 30)).then_inc(bit_done, 1)
            dve.wait_ge(bit_done, 2)
            dve.tensor_copy(bit_int[:], bit[:]).then_inc(bit_done, 1)
            dve.wait_ge(loaded, 16)
            dve.tensor_reduce(row_max[:], logit[:], AX_X, ALU.max).then_inc(small, 1)
            dve.wait_ge(max_made, 1)
            dve.tensor_reduce(max_e[:], p_small[0:1, 0:128].rearrange("o (e r) -> o e r", e=E), AX_X,
                              ALU.max).then_inc(small, 1)
            dve.wait_ge(small, 2)
            dve.tensor_copy(max_row[:], over(max_e[:], R, 2)).then_inc(small, 1)
            dve.wait_ge(max_spread, 1)
            dve.tensor_copy(top[:], p_small[:, 128:129]).then_inc(small, 1)
            dve.wait_ge(small, 4)
            dve.tensor_scalar(u[:], logit[:], -1.0, top[:, 0:1], ALU.mult, ALU.add).then_inc(u_done, 1)
            dve.wait_ge(sum_made, 1)
            dve.reciprocal(inv_sum[:], p_small[:, 129:130]).then_inc(small, 1)
            dve.wait_ge(small, 5)
            dve.tensor_scalar(weight[:], weight[:], inv_sum[:, 0:1], None, ALU.mult).then_inc(weight_done, 1)

            with dve.Fori(0, 31) as i:
                dve.wait_ge(bit_done, 2 * i + 3)
                dve.wait_ge(kth_done, i + 1)
                dve.tensor_tensor(trial[:], kth[:], bit_int[:], ALU.bitwise_or).then_inc(trial_done, 1)
                T.wait_alone(dve, trial_done, i + 1)
                dve.tensor_scalar(scratch[:], u[:], trial[:].bitcast(F32), None, ALU.is_lt, ALU.add,
                                  accum_out=row_count[:]).then_inc(counted, 1)
                dve.wait_ge(total_made, i + 1)
                dve.tensor_scalar(gain[:], p_tot[:], CAP - 0.5, bit[:, 0:1], ALU.is_lt, ALU.mult).then_inc(gain_done, 1)
                dve.wait_ge(gain_done, i + 1)
                dve.tensor_tensor(kth[:], kth[:], gain[:], ALU.bitwise_or).then_inc(kth_done, 1)
                dve.tensor_scalar(bit[:], bit[:], 0.5, None, ALU.mult).then_inc(bit_done, 1)
                dve.wait_ge(bit_done, 2 * i + 4)
                dve.tensor_copy(bit_int[:], bit[:]).then_inc(bit_done, 1)

            dve.wait_ge(kth_done, 32)
            kth_f = kth[:].bitcast(F32)
            dve.tensor_scalar(lower[:], u[:], kth_f, None, ALU.is_lt, ALU.add, accum_out=row_count[:]).then_inc(marked, 1)
            dve.tensor_scalar(equal[:], u[:], kth_f, None, ALU.is_equal).then_inc(marked, 1)
            dve.wait_ge(marked, 2)
            dve.tensor_tensor_scan(count[:], ones[:], equal[:], 0.0, ALU.mult, ALU.add).then_inc(marked, 1)
            dve.wait_ge(offsets_made, 2)
            dve.tensor_copy(ahead[:, 0:1], p_small[:, 130:131]).then_inc(marked, 1)
            dve.wait_ge(marked, 4)
            dve.tensor_tensor(tie_room[:], p_tot[:], ahead[:, 0:1], ALU.add).then_inc(small, 1)
            dve.wait_ge(small, 6)
            dve.tensor_scalar(tie_room[:], tie_room[:], -1.0, float(CAP), ALU.mult, ALU.add).then_inc(small, 1)
            dve.wait_ge(small, 7)
            dve.scalar_tensor_tensor(out=tied[:], in0=count[:], scalar=tie_room[:, 0:1], in1=equal[:],
                                     op0=ALU.is_le, op1=ALU.mult).then_inc(small, 1)
            dve.wait_ge(small, 8)
            dve.tensor_tensor(taken[:], lower[:], tied[:], ALU.add).then_inc(marked, 1)
            dve.wait_ge(marked, 5)
            dve.tensor_tensor_scan(count[:], ones[:], taken[:], 0.0, ALU.mult, ALU.add).then_inc(marked, 1)
            dve.wait_ge(offsets_made, 3)
            dve.tensor_copy(ahead[:, 1:2], p_small[:, 131:132]).then_inc(marked, 1)
            dve.wait_ge(marked, 7)
            dve.scalar_tensor_tensor(out=slot[:], in0=count[:], scalar=ahead[:, 1:2], in1=taken[:],
                                     op0=ALU.add, op1=ALU.mult).then_inc(marked, 1)
            dve.wait_ge(marked, 8)
            dve.tensor_scalar(slot[:], slot[:], -1.0, None, ALU.add).then_inc(slot_done, 1)
            dve.wait_ge(turned, 1)

            def by_sequence(tile):
                return tile[:].rearrange("l (r i) e -> l i e r", i=GB)

            def by_group(tile):
                return tile.rearrange("l i (e r) -> l i e r", e=E)

            dve.tensor_copy(by_sequence(weightT), by_group(p_weight[:])).then_inc(weightT_kept, 1)
            dve.wait_ge(turned, 2)
            dve.tensor_copy(slot_int[:], p_slot[:]).then_inc(parts_done, 1)
            dve.wait_ge(parts_done, 1)
            dve.tensor_scalar(hi_int[:], slot_int[:], 5, None, ALU.arith_shift_right).then_inc(parts_done, 1)
            dve.tensor_scalar(lo_int[:], slot_int[:], LO - 1, None, ALU.bitwise_and).then_inc(parts_done, 1)
            dve.wait_ge(parts_done, 3)
            dve.tensor_copy(by_sequence(hi), by_group(hi_int[:])).then_inc(parts_done, 1)
            dve.tensor_copy(by_sequence(lo), by_group(lo_int[:])).then_inc(parts_done, 1)
            dve.wait_ge(parts_done, 5)
            dve.wait_ge(consts, 10)

            def one_hot(c, p):
                T.wait_alone(dve, chunk_used, c + 1)
                pairs = PB * E

                def of(x):
                    return over(x[:, bass.ds(c * PB, PB), :].rearrange("l b e -> l (b e)"), LO, 2)

                dve.tensor_tensor(hot_lo[p][:], over(iota[:], pairs), of(lo), ALU.is_equal).then_inc(lo_hot_done, 1)
                dve.tensor_tensor(hot_hi[p][:], over(iota[:], pairs), of(hi), ALU.is_equal).then_inc(hot_done, 1)

            with dve.Fori(0, NCH // 2) as k:
                for p in range(2):
                    one_hot(2 * k + p, p)
            dve.wait_ge(rows_made, 1)
            for i in range(E // 4):
                dve.tensor_copy(rows_f[:, i, :], p_rows[i][:, 0, :]).then_inc(marked, 1)
                dve.wait_ge(marked, 9 + i)
                dve.scalar_tensor_tensor(out=rows_f[:, i, :], in0=p_rows[i][:, 1, :], scalar=float(L),
                                         in1=rows_f[:, i, :], op0=ALU.mult, op1=ALU.add).then_inc(slot_done, 1)
            dve.wait_ge(rows_turned, 1)
            dve.tensor_copy(T.chosen[:], p_chosen[:]).then_inc(chosen_done, 1)


def stage_expert_choice(T):
    nc, t, sem = T.nc, T.t, T.sem
    ET = CAP // 128
    HT = ET // 2
    FC = F // 128
    HS = HT * 128
    with ExitStack() as ctx:
        def sb(name, shape, dt=F32):
            return ctx.enter_context(nc.sbuf_tensor(name, shape, dt))

        def ps(name, shape, dt=F32):
            return ctx.enter_context(nc.psum_tensor(name, shape, dt))

        w1 = [sb(f"ec_w1{p}", [D, F]) for p in range(2)]
        w2 = [sb(f"ec_w2{p}", [128, FC, D]) for p in range(2)]
        b1 = sb("ec_b1", [128, E, FC])
        b1_now = [sb(f"ec_b1_now{p}", [128, FC]) for p in range(2)]
        b2 = sb("ec_b2", [128, E, D])
        rows_in = [sb(f"ec_rows_in{p}", [128, ET], I32) for p in range(2)]
        rows_out = sb("ec_rows_out", [128, ET], I32)
        x = [sb(f"ec_x{p}", [128, ET, D + E]) for p in range(2)]
        weight = [sb(f"ec_weight{p}", [128, ET]) for p in range(2)]
        xT = [sb(f"ec_xT{s}", [D, HT, 128]) for s in range(2)]
        hidden = [sb(f"ec_hidden{s}", [128, FC, HS]) for s in range(2)]
        plus_b2 = sb("ec_plus_b2", [128, HT, D])
        y = [sb(f"ec_y{p}", [128, ET, D]) for p in range(2)]
        p_xT = ps("ec_p_xT", [D, HT, 128])
        p_hidden = [ps(f"ec_p_hidden{c}", [128, HS]) for c in range(FC)]
        p_y = [ps(f"ec_p_y{s}", [128, HT, D]) for s in range(2)]

        biases_in = sem("ec_biases_in")
        weights_in = [sem(f"ec_weights_in{p}") for p in range(2)]
        rows_in_set = sem("ec_rows_in_set")
        rows_out_set = sem("ec_rows_out_set")
        gathered = [sem(f"ec_gathered{p}") for p in range(2)]
        weight_set = sem("ec_weight_set")
        xT_made = sem("ec_xT_made")
        xT_kept = sem("ec_xT_kept")
        hidden_made = sem("ec_hidden_made")
        gelu_done = sem("ec_gelu_done")
        y_made = sem("ec_y_made")
        b2_added = sem("ec_b2_added")
        y_done = sem("ec_y_done")
        added = [sem(f"ec_added{p}") for p in range(2)]
        h_back = sem("ec_h_back")

        block = ctx.enter_context(nc.Block())


        @block.sync
        def _(sp):
            T.clear_old(sp)
            sp.dma_start(b1[:], t["e_b1"]).then_inc(biases_in, 16)
            sp.dma_start(b2[:], t["e_b2"].rearrange("e d -> (e d)").partition_broadcast(128)).then_inc(biases_in, 16)

            def load(w, p):
                e = 2 * w + p
                sp.dma_start(w1[p][:], t["e_w1"][bass.ds(e * D, D), :]).then_inc(weights_in[p], 16)
                sp.dma_start(w2[p][:], t["e_w2"][bass.ds(e * F, F), :].rearrange("(c k) d -> k c d", k=128)
                             ).then_inc(weights_in[p], 16)

            load(0, 0)
            load(0, 1)
            with sp.Fori(1, E // 2) as w:
                for p in range(2):
                    sp.wait_ge(y_made, 2 * (2 * w + p - 1))
                    load(w, p)
            for p in range(2):
                sp.wait_ge(added[p], 16 * ET * (E // 2))
            sp.dma_start(T.H[:], T.h_rows.rearrange("(b l) d -> l b d", l=L)).then_inc(h_back, 16)
            sp.wait_ge(h_back, 16)

        @block.gpsimd
        def _(pool):
            def gather(w, p):
                e = 2 * w + p
                if at_least(w, 1):
                    T.wait_alone(pool, xT_made, 2 * (e - 1))
                    T.wait_alone(pool, weight_set, e - 1)
                pool.tensor_copy(rows_in[p][:], T.chosen[:, bass.ds(e * ET, ET)]).then_inc(rows_in_set, 1)
                T.wait_alone(pool, rows_in_set, e + 1)
                for s in range(ET):
                    pool.indirect_dma_start(out=x[p][:, s, :], out_offset=None, in_=T.z_rows,
                                            in_offset=bass.IndirectOffsetOnAxis(ap=rows_in[p][:, s:s + 1], axis=0)
                                            ).then_inc(gathered[p], 16)

            def add(w, p):
                e = 2 * w + p
                T.wait_alone(pool, y_done, 2 * e + 2)
                if at_least(w, 1) or p == 1:
                    T.wait_alone(pool, added[1 - p], 16 * ET * (w + p))
                pool.tensor_copy(rows_out[:], T.chosen[:, bass.ds(e * ET, ET)]).then_inc(rows_out_set, 1)
                T.wait_alone(pool, rows_out_set, e + 1)
                for s in range(ET):
                    pool.indirect_dma_start(out=T.h_rows,
                                            out_offset=bass.IndirectOffsetOnAxis(ap=rows_out[:, s:s + 1], axis=0),
                                            in_=y[p][:, s, :], in_offset=None,
                                            compute_op=ALU.add).then_inc(added[p], 16)

            gather(0, 0)
            gather(0, 1)
            with pool.Fori(0, E // 2 - 1) as w:
                for p in range(2):
                    add(w, p)
                    gather(w + 1, p)
            add(E // 2 - 1, 0)
            add(E // 2 - 1, 1)

        @block.tensor
        def _(pe):
            def transposes(w, p, s):
                u = 4 * w + 2 * p + s
                T.wait_alone(pe, gathered[p], 16 * ET * (w + 1))
                if at_least(w, 1) or p + s > 0:
                    T.wait_alone(pe, xT_kept, u)
                for i in range(HT):
                    last = pe.transpose(p_xT[:, i, :], x[p][:, s * HT + i, 0:D], T.ident[:])
                last.then_inc(xT_made, 1)

            def into_hidden(w, p, s):
                u = 4 * w + 2 * p + s
                T.wait_alone(pe, weights_in[p], 32 * (w + 1))
                T.wait_alone(pe, xT_kept, u + 1)
                for c in range(FC):
                    if at_least(w, 1) or p + s > 0:
                        pe.wait_ge(gelu_done, FC * (u - 1) + c + 1)
                    pe.matmul(p_hidden[c][:], w1[p][:, c * 128:(c + 1) * 128],
                              xT[s][:].rearrange("d i n -> d (i n)"), start=True, stop=True).then_inc(hidden_made, 1)

            def out_of_hidden(w, p, s):
                u = 4 * w + 2 * p + s
                T.wait_alone(pe, gelu_done, FC * (u + 1))
                if at_least(w, 1) or p > 0:
                    T.wait_alone(pe, b2_added, u - 1)
                for i in range(HT):
                    for c in range(FC):
                        last = pe.matmul(p_y[s][:, i, :], hidden[s][:, c, i * 128:(i + 1) * 128], w2[p][:, c, :],
                                         start=(c == 0), stop=(c == FC - 1))
                last.then_inc(y_made, 1)

            transposes(0, 0, 0)
            transposes(0, 0, 1)
            into_hidden(0, 0, 0)

            def steps(w, p):
                transposes(w + p, 1 - p, 0)
                into_hidden(w, p, 1)
                out_of_hidden(w, p, 0)
                transposes(w + p, 1 - p, 1)
                into_hidden(w + p, 1 - p, 0)
                out_of_hidden(w, p, 1)

            steps(0, 0)
            with pe.Fori(0, E // 2 - 1) as w:
                steps(w, 1)
                steps(w + 1, 0)
            into_hidden(E // 2 - 1, 1, 1)
            out_of_hidden(E // 2 - 1, 1, 0)
            out_of_hidden(E // 2 - 1, 1, 1)

        @block.scalar
        def _(act):
            def gelus(w, p, s):
                u = 4 * w + 2 * p + s
                if at_least(w, 1) or p > 0:
                    T.wait_alone(act, y_made, u - 1)
                for c in range(FC):
                    act.wait_ge(hidden_made, FC * u + c + 1)
                    act.activation(hidden[s][:, c, :], p_hidden[c][:], ACT.Gelu,
                                   bias=b1_now[p][:, c:c + 1]).then_inc(gelu_done, 1)

            def expert(w, p):
                T.wait_alone(act, weight_set, 2 * w + p + 1)
                gelus(w, p, 0)
                gelus(w, p, 1)

            expert(0, 0)
            expert(0, 1)
            with act.Fori(1, E // 2) as w:
                expert(w, 0)
                expert(w, 1)

        @block.vector
        def _(dve):
            def take_weights(w, p):
                e = 2 * w + p
                T.wait_alone(dve, gathered[p], 16 * ET * (w + 1))
                if at_least(w, 1):
                    T.wait_alone(dve, gelu_done, 2 * FC * (e - 1))
                    T.wait_alone(dve, y_done, 2 * (e - 1))
                dve.tensor_copy(weight[p][:], x[p][:, :, bass.ds(D + e, 1)].rearrange("n s o -> n (s o)"))
                dve.tensor_copy(b1_now[p][:], b1[:, bass.ds(e, 1), :].rearrange("n o c -> n (o c)")
                                ).then_inc(weight_set, 1)

            def keep_xT(w, p, s):
                u = 4 * w + 2 * p + s
                T.wait_alone(dve, xT_made, u + 1)
                if at_least(w, 1) or p > 0:
                    T.wait_alone(dve, hidden_made, FC * (u - 1))
                dve.tensor_copy(xT[s][:], p_xT[:]).then_inc(xT_kept, 1)

            def weigh(w, p, s):
                e, u = 2 * w + p, 4 * w + 2 * p + s
                T.wait_alone(dve, y_made, u + 1)
                if at_least(w, 1) or p + s > 0:
                    T.wait_alone(dve, y_done, u)
                if at_least(w, 1):
                    T.wait_alone(dve, added[p], 16 * ET * w)
                dve.tensor_tensor(plus_b2[:], p_y[s][:],
                                  over(b2[:, bass.ds(e, 1), :].rearrange("n o d -> n (o d)"), HT),
                                  ALU.add).then_inc(b2_added, 1)
                T.wait_alone(dve, b2_added, u + 1)
                dve.tensor_tensor(y[p][:, s * HT:(s + 1) * HT, :], plus_b2[:],
                                  over(weight[p][:, s * HT:(s + 1) * HT], D, 2), ALU.mult).then_inc(y_done, 1)

            def steps(w, p):
                take_weights(w + p, 1 - p)
                keep_xT(w + p, 1 - p, 0)
                weigh(w, p, 0)
                keep_xT(w + p, 1 - p, 1)
                weigh(w, p, 1)

            dve.wait_ge(biases_in, 32)
            take_weights(0, 0)
            keep_xT(0, 0, 0)
            keep_xT(0, 0, 1)
            steps(0, 0)
            with dve.Fori(0, E // 2 - 1) as w:
                steps(w, 1)
                steps(w + 1, 0)
            weigh(E // 2 - 1, 1, 0)
            weigh(E // 2 - 1, 1, 1)


def stage_offset_attention(T):
    nc, t, sem = T.nc, T.t, T.sem
    NO = len(OFFS)
    BH = GB * NH
    NLOC = OFF_LOCAL + 1
    PAD = OFFS[-1]
    NPOOL = OFF_LOCAL + 1 - OFF_SPLIT
    MID = NPOOL + (NLOC - NPOOL) // 2
    POOL_RUNS = [(0, NPOOL)]
    DVE_RUNS = [(NPOOL, MID), (MID, NLOC)] + [(j, j + 1) for j in range(NLOC, NO)]
    with ExitStack() as ctx:
        def sb(name, shape, dt=F32):
            return ctx.enter_context(nc.sbuf_tensor(name, shape, dt))

        def ps(name, shape, dt=F32):
            return ctx.enter_context(nc.psum_tensor(name, shape, dt))

        w_qk = sb("oa_w_qk", [D, 2, D])
        w_vg = sb("oa_w_vg", [D, 2, D])
        w_out = sb("oa_w_out", [D, D])
        w_out_scaled = sb("oa_w_out_scaled", [D, D])
        gain = sb("oa_gain", [D, 1])
        b_qk = sb("oa_b_qk", [D, 2])
        b_vg = sb("oa_b_vg", [1, 2, D])
        b_out = sb("oa_b_out", [1, D])
        ones_row = sb("oa_ones_row", [1, L])
        shift = sb("oa_shift", [D, NO])
        sum_w = sb("oa_sum_w", [D, NO, NH])
        pos_bias = sb("oa_pos_bias", [L, NO, NH])
        cosines = sb("oa_cosines", [L, NO, NH])
        amp = sb("oa_amp", [L, NH])
        bias = sb("oa_bias", [L, NO, NH])
        stats = sb("oa_stats", [L, GB, 6])
        mv = sb("oa_mv", [L, GB, 2])
        var_eps = sb("oa_var_eps", [L, GB])
        rstd = sb("oa_rstd", [L, GB])
        z = [sb(f"oa_z{p}", [L, GB, D]) for p in range(2)]
        zT = [sb(f"oa_zT{p}", [D, GB, L]) for p in range(2)]
        q_sb = [sb(f"oa_q{p}", [D, GB, L]) for p in range(2)]
        k_sb = [sb(f"oa_k{p}", [D, PAD + GT]) for p in range(2)]
        v_ones = [sb(f"oa_v_ones{p}", [L, GB, NH, DH + 1]) for p in range(2)]
        gate = [sb(f"oa_gate{p}", [L, GB, D]) for p in range(2)]
        prod_pool = [sb(f"oa_prod_pool{i}", [D, NPOOL, L]) for i in range(2)]
        prod_dve = [sb(f"oa_prod_dve{i}", [D, NO - NPOOL, L]) for i in range(2)]
        top = [sb(f"oa_top{i}", [L, NH]) for i in range(2)]
        probs = [sb(f"oa_probs{p}", [L, NO, GB, NH]) for p in range(2)]
        dense = [sb(f"oa_dense{p}", [L, L, BH]) for p in range(2)]
        inv_sum = sb("oa_inv_sum", [L, GB, NH])
        heads_out = sb("oa_heads_out", [L, GB, D])
        gated = sb("oa_gated", [L, GB, D])
        gatedT = sb("oa_gatedT", [D, GB, L])
        p_sc = [ps(f"oa_p_sc{i}", [L, NO, NH]) for i in range(2)]
        p_zq = ps("oa_p_zq", [D, GB, L])
        p_k = ps("oa_p_k", [D, GB, L])
        p_vg = ps("oa_p_vg", [L, 2, 2, D])
        p_o = [ps(f"oa_p_o{i}", [L, 2, NH, DH + 1]) for i in range(2)]
        p_out = ps("oa_p_out", [128, 512])
        p_gatedT = p_out[:, 0:GT].rearrange("p (b l) -> p b l", b=GB)
        p_rows = p_out[0:L, :].rearrange("p (b d) -> p b d", b=GB)

        def operands(p, b, a, e, out, first):
            lo = OFFS[e - 1]
            start = PAD + b * L - OFFS[a] + lo
            k_shifted = k_sb[p][:, start:start + L - lo]
            windows = bass.AP(k_shifted.tensor, k_shifted.offset, [list(k_shifted.ap[0]), [1, e - a], [1, L - lo]])
            return out[:, a - first:e - first, lo:L], over(q_sb[p][:, b, lo:L], e - a), windows

        weights_in = sem("oa_weights_in")
        scaled = sem("oa_scaled")
        bias_steps = sem("oa_bias_steps")
        cleared = sem("oa_cleared")
        zeroed = sem("oa_zeroed")
        stats_done = sem("oa_stats_done")
        mv_done = sem("oa_mv_done")
        eps_added = sem("oa_eps_added")
        rstd_done = sem("oa_rstd_done")
        z_done = sem("oa_z_done")
        zT_made = sem("oa_zT_made")
        zT_kept = sem("oa_zT_kept")
        q_made = sem("oa_q_made")
        q_kept = sem("oa_q_kept")
        k_made = sem("oa_k_made")
        k_kept = sem("oa_k_kept")
        vg_made = sem("oa_vg_made")
        v_kept = sem("oa_v_kept")
        gate_done = sem("oa_gate_done")
        pool_prods = sem("oa_pool_prods")
        dve_prods = sem("oa_dve_prods")
        sc_made = sem("oa_sc_made")
        top_done = sem("oa_top_done")
        sub_done = sem("oa_sub_done")
        exp_done = sem("oa_exp_done")
        skewed = [sem(f"oa_skewed{p}") for p in range(2)]
        dense_in = [sem(f"oa_dense_in{p}") for p in range(2)]
        pv_done = sem("oa_pv_done")
        inv_done = sem("oa_inv_done")
        out_done = sem("oa_out_done")
        gated_done = sem("oa_gated_done")
        gatedT_made = sem("oa_gatedT_made")
        gatedT_kept = sem("oa_gatedT_kept")
        rows_made = sem("oa_rows_made")
        h_done = sem("oa_h_done")

        block = ctx.enter_context(nc.Block())

        @block.sync
        def _(sp):
            T.clear_old(sp)
            for dst, src in ((w_qk[:], t["o_wqkv"][:, 0:2 * D].rearrange("d (j e) -> d j e", j=2)),
                             (w_vg[:, 0, :], t["o_wqkv"][:, 2 * D:3 * D]), (w_vg[:, 1, :], t["o_wgate"]),
                             (w_out[:], t["o_wout"]), (gain[:], t["o_gain"].unsqueeze(1)),
                             (b_qk[:], t["o_bqk"]),
                             (b_vg[:], t["o_bvg"].rearrange("(o j d) -> o j d", o=1, j=2)),
                             (b_out[:], t["o_bout"].unsqueeze(0)), (shift[:], t["o_scale"]),
                             (pos_bias[:].rearrange("l o h -> l (o h)"), t["o_pos"].partition_broadcast(L)),
                             (cosines[:].rearrange("l o h -> l (o h)"), t["o_cos"].partition_broadcast(L)),
                             (amp[:], t["o_amp"].partition_broadcast(L))):
                sp.dma_start(dst, src).then_inc(weights_in, 16)
            sp.wait_ge(cleared, 1)
            for p in range(2):
                sp.dma_start(T.diagonals[p][PAD:PAD + L], dense[0][:]).then_inc(zeroed, 16)
            sp.wait_ge(zeroed, 32)

            def along_diagonals(g, p, w):
                row, col = L * BH, BH
                d = T.diagonals[p]
                T.wait_alone(sp, exp_done, GB * (g + 1))
                if at_least(g, 2):
                    T.wait_alone(sp, dense_in[p], 64 * w)
                sp.dma_start(bass.AP(d.tensor, (PAD - OFF_LOCAL) * row, [[row + col, L], [row, NLOC], [1, BH]]),
                             probs[p][:, 0:NLOC].rearrange("n o b h -> n o (b h)")).then_inc(skewed[p], 16)
                for j in range(NLOC, NO):
                    sp.dma_start(bass.AP(d.tensor, (PAD - OFFS[j]) * row, [[row + col, L], [1, BH]]),
                                 probs[p][:, j].rearrange("n b h -> n (b h)")).then_inc(skewed[p], 16)

            def as_matrices(g, p, w):
                T.wait_alone(sp, skewed[p], 16 * (1 + NO - NLOC) * (w + 1))
                if at_least(g, 2):
                    T.wait_alone(sp, pv_done, 2 * (g - 1))
                for m in range(0, L, 32):
                    e = min(m + 32, L)
                    sp.dma_start(dense[p][m:e, m:L, :], T.diagonals[p][PAD + m:PAD + e, m:L]).then_inc(dense_in[p], 16)

            for g in range(2):
                along_diagonals(g, g, 0)
                as_matrices(g, g, 0)
            with sp.Fori(1, NG // 2) as k:
                for p in range(2):
                    along_diagonals(2 * k + p, p, k)
                    as_matrices(2 * k + p, p, k)

        @block.gpsimd
        def _(pool):
            pool.wait_ge(bias_steps, 2)
            for i, (a, b) in enumerate([(0, NLOC)] + [(j, j + 1) for j in range(NLOC, NO)]):
                pool.affine_select(out=bias[:, a:b, :], in_=bias[:, a:b, :], compare_op=ALU.is_ge, fill=-1e30,
                                   base=-OFFS[a], pattern=[[1, b - a], [0, NH]],
                                   channel_multiplier=1).then_inc(bias_steps, 1)

            def rstd_of(g):
                pool.wait_ge(mv_done, GB * (g + 1))
                pool.tensor_tensor(var_eps[:], mv[:, :, 1], T.eps[:], ALU.add).then_inc(eps_added, 1)
                pool.wait_ge(eps_added, g + 1)
                pool.tensor_tensor(rstd[:], var_eps[:], T.neg_half[:], ALU.pow).then_inc(rstd_done, 1)

            def products_of(g, p, b):
                s = GB * g + b
                if b == 0:
                    T.wait_alone(pool, q_kept, g + 1)
                    T.wait_alone(pool, k_kept, g + 1)
                if at_least(g, 1) or b >= 2:
                    T.wait_alone(pool, sc_made, s - 1)
                for a, e in POOL_RUNS:
                    pool.tensor_tensor(*operands(p, b, a, e, prod_pool[b % 2], 0), ALU.mult).then_inc(pool_prods, 1)

            def turn(g, p):
                for b in range(GB):
                    products_of(g, p, b)
                if below(g, NG - 2):
                    rstd_of(g + 2)

            rstd_of(0)
            rstd_of(1)
            pool.wait_ge(cleared, 3)
            turn(0, 0)
            turn(1, 1)
            with pool.Fori(1, NG // 2 - 1) as k:
                turn(2 * k, 0)
                turn(2 * k + 1, 1)
            turn(NG - 2, 0)
            turn(NG - 1, 1)

        @block.tensor
        def _(pe):
            pe.wait_ge(weights_in, 16 * 12)
            pe.wait_ge(scaled, 2 + NH)
            pe.wait_ge(bias_steps, 3 + NO - NLOC)

            def z_transposes(g, p):
                T.wait_alone(pe, z_done, g + 1)
                if at_least(g, 1):
                    T.wait_alone(pe, q_kept, g)
                for b in range(GB):
                    last = pe.transpose(p_zq[:, b, :], z[p][:, b, :], T.ident[0:L, 0:L])
                last.then_inc(zT_made, 1)

            def queries_keys(g, p):
                T.wait_alone(pe, zT_kept, g + 1)
                pe.matmul(p_zq[:], w_qk[:, 0, :], zT[p][:], start=True, stop=True).then_inc(q_made, 1)
                if at_least(g, 1):
                    T.wait_alone(pe, k_kept, g)
                pe.matmul(p_k[:], w_qk[:, 1, :], zT[p][:], start=True, stop=True).then_inc(k_made, 1)

            def values_gate(g, p):
                for i in range(2):
                    if at_least(g, 1) or i == 1:
                        T.wait_alone(pe, gate_done, 2 * g + i)
                    for j in range(2):
                        b = 2 * i + j
                        pe.matmul(p_vg[:, j], zT[p][:, b, :], w_vg[:], start=True, stop=False)
                        last = pe.matmul(p_vg[:, j], ones_row[:], b_vg[:], start=False, stop=True)
                    last.then_inc(vg_made, 1)

            def scores(g, p):
                for b in range(GB):
                    s = GB * g + b
                    if at_least(g, 1) or b >= 2:
                        T.wait_alone(pe, sub_done, s - 1)
                    pe.matmul(p_sc[b % 2][:], T.ident[0:L, 0:L], bias[:], start=True, stop=False,
                              skip_group_check=True)
                    T.wait_alone(pe, dve_prods, s + 1)
                    for j in range(NPOOL, NO):
                        pe.matmul(p_sc[b % 2][:, j, :], prod_dve[b % 2][:, j - NPOOL, :], sum_w[:, j, :],
                                  start=False, stop=False, skip_group_check=True)
                    T.wait_alone(pe, pool_prods, s + 1)
                    for j in range(NPOOL):
                        last = pe.matmul(p_sc[b % 2][:, j, :], prod_pool[b % 2][:, j, :], sum_w[:, j, :],
                                         start=False, stop=(j == NPOOL - 1), skip_group_check=True)
                    last.then_inc(sc_made, 1)

            def values(g, p, w):
                T.wait_alone(pe, dense_in[p], 64 * (w + 1))
                T.wait_alone(pe, v_kept, 2 * (g + 1))
                for i in range(2):
                    if at_least(g, 1):
                        T.wait_alone(pe, out_done, 2 * g - 1 + i)
                    for j in range(2):
                        for h in range(NH):
                            b = 2 * i + j
                            last = pe.matmul(p_o[i][:, j, h, :], dense[p][:, :, b * NH + h], v_ones[p][:, b, h, :],
                                             start=True, stop=True)
                    last.then_inc(pv_done, 1)

            def gated_transposes(g):
                T.wait_alone(pe, gated_done, g + 1)
                if at_least(g, 1):
                    T.wait_alone(pe, h_done, g)
                for b in range(GB):
                    last = pe.transpose(p_gatedT[:, b, :], gated[:, b, :], T.ident[0:L, 0:L])
                last.then_inc(gatedT_made, 1)

            def project_out(g):
                T.wait_alone(pe, gatedT_kept, g + 1)
                for b in range(GB):
                    pe.matmul(p_rows[:, b, :], gatedT[:, b, :], w_out_scaled[:], start=True, stop=False)
                    last = pe.matmul(p_rows[:, b, :], ones_row[:], b_out[:], start=False, stop=True)
                last.then_inc(rows_made, 1)

            def turn(g, p, w):
                if at_least(g, 2):
                    gated_transposes(g - 2)
                if below(g, NG - 1):
                    z_transposes(g + 1, 1 - p)
                if at_least(g, 2):
                    project_out(g - 2)
                if below(g, NG - 1):
                    queries_keys(g + 1, 1 - p)
                scores(g, p)
                if at_least(g, 1):
                    values(g - 1, 1 - p, w - 1 + p)
                if below(g, NG - 1):
                    values_gate(g + 1, 1 - p)

            z_transposes(0, 0)
            queries_keys(0, 0)
            values_gate(0, 0)
            turn(0, 0, 0)
            turn(1, 1, 0)
            with pe.Fori(1, NG // 2 - 1) as k:
                turn(2 * k, 0, k)
                turn(2 * k + 1, 1, k)
            turn(NG - 2, 0, NG // 2 - 1)
            turn(NG - 1, 1, NG // 2 - 1)
            gated_transposes(NG - 2)
            project_out(NG - 2)
            values(NG - 1, 1, NG // 2 - 1)
            gated_transposes(NG - 1)
            project_out(NG - 1)

        @block.scalar
        def _(act):
            act.wait_ge(weights_in, 16 * 12)
            act.wait_ge(cleared, 3)

            def keep_qk(g, p):
                act.wait_ge(zT_made, g + 1)
                if at_least(g, 2):
                    act.wait_ge(vg_made, 2 * (g - 1))
                act.copy(zT[p][:], p_zq[:]).then_inc(zT_kept, 1)
                if at_least(g, 2):
                    act.wait_ge(sc_made, GB * (g - 1))
                act.wait_ge(q_made, g + 1)
                act.activation(q_sb[p][:], p_zq[:], ACT.Identity, bias=b_qk[:, 0:1]).then_inc(q_kept, 1)
                act.wait_ge(k_made, g + 1)
                act.activation(k_sb[p][:, PAD:PAD + GT].rearrange("p (b l) -> p b l", b=GB), p_k[:], ACT.Identity,
                               bias=b_qk[:, 1:2]).then_inc(k_kept, 1)

            def keep_vg(g, p):
                for i in range(2):
                    act.wait_ge(vg_made, 2 * g + i + 1)
                    if at_least(g, 2):
                        act.wait_ge(pv_done, 2 * (g - 1))
                        act.wait_ge(gated_done, g - 1)
                    act.copy(v_ones[p][:, 2 * i:2 * i + 2, :, 0:DH],
                             p_vg[:, :, 0, :].rearrange("l j (h d) -> l j h d", h=NH)).then_inc(v_kept, 1)
                    act.activation(gate[p][:, 2 * i:2 * i + 2, :], p_vg[:, :, 1, :], ACT.Tanh,
                                   scale=0.5).then_inc(gate_done, 1)

            def exponentials(g, p):
                for b in range(GB):
                    act.wait_ge(sub_done, GB * g + b + 1)
                    act.activation(probs[p][:, :, b, :], probs[p][:, :, b, :], ACT.Exp).then_inc(exp_done, 1)

            def keep_gatedT(g):
                act.wait_ge(gatedT_made, g + 1)
                if at_least(g, 1):
                    act.wait_ge(rows_made, g)
                act.copy(gatedT[:], p_gatedT).then_inc(gatedT_kept, 1)

            def turn(g, p):
                if at_least(g, 2):
                    keep_gatedT(g - 2)
                if below(g, NG - 1):
                    keep_qk(g + 1, 1 - p)
                exponentials(g, p)
                if below(g, NG - 1):
                    keep_vg(g + 1, 1 - p)

            keep_qk(0, 0)
            keep_vg(0, 0)
            turn(0, 0)
            turn(1, 1)
            with act.Fori(1, NG // 2 - 1) as k:
                turn(2 * k, 0)
                turn(2 * k + 1, 1)
            turn(NG - 2, 0)
            turn(NG - 1, 1)
            keep_gatedT(NG - 2)
            keep_gatedT(NG - 1)

        @block.vector
        def _(dve):
            dve.memset(dense[0][:], 0.0).then_inc(cleared, 1)
            for i in range(2):
                dve.memset(prod_pool[i][:], 0.0)
                dve.memset(prod_dve[i][:], 0.0)
                dve.memset(k_sb[i][:, 0:PAD], 0.0)
                dve.memset(v_ones[i][:], 1.0)
            dve.memset(ones_row[:], 1.0).then_inc(cleared, 1)
            dve.memset(dense[1][:], 0.0).then_inc(cleared, 1)
            dve.wait_ge(weights_in, 16 * 12)
            dve.tensor_tensor(bias[:], cosines[:], over(amp[:], NO), ALU.mult).then_inc(bias_steps, 1)
            dve.wait_ge(bias_steps, 1)
            dve.tensor_tensor(bias[:], bias[:], pos_bias[:], ALU.add).then_inc(bias_steps, 1)
            dve.tensor_scalar(shift[:], shift[:], 1.0, DH ** -0.5, ALU.add, ALU.mult).then_inc(scaled, 1)
            dve.tensor_scalar(w_out_scaled[:], w_out[:], gain[:, 0:1], 0.5, ALU.mult, ALU.mult).then_inc(scaled, 1)
            dve.wait_ge(scaled, 2)
            for h in range(NH):
                dve.tensor_scalar(sum_w[:, :, h], shift[:], T.head_mask[:, h:h + 1], None, ALU.mult).then_inc(scaled, 1)
            dve.wait_ge(zeroed, 32)

            def moments(g):
                for b in range(GB):
                    dve.bn_stats(stats[:, b, :], T.H[:, g * GB + b, :]).then_inc(stats_done, 1)
                T.wait_alone(dve, stats_done, GB * (g + 1))
                for b in range(GB):
                    dve.bn_aggr(mv[:, b, :], stats[:, b, :]).then_inc(mv_done, 1)

            def normalize(g, p):
                T.wait_alone(dve, rstd_done, g + 1)
                if at_least(g, 2):
                    T.wait_alone(dve, zT_made, g - 1)
                for b in range(GB):
                    last = dve.tensor_scalar(z[p][:, b, :], T.H[:, g * GB + b, :], mv[:, b, 0:1],
                                             rstd[:, b:b + 1], ALU.subtract, ALU.mult)
                last.then_inc(z_done, 1)

            def products_of(g, p, b):
                s = GB * g + b
                if b == 0:
                    T.wait_alone(dve, q_kept, g + 1)
                    T.wait_alone(dve, k_kept, g + 1)
                if at_least(g, 1) or b >= 2:
                    T.wait_alone(dve, sc_made, s - 1)
                for a, e in DVE_RUNS:
                    last = dve.tensor_tensor(*operands(p, b, a, e, prod_dve[b % 2], NPOOL), ALU.mult)
                last.then_inc(dve_prods, 1)

            def less_maximum(g, p, b, w):
                s = GB * g + b
                dve.wait_ge(sc_made, s + 1)
                dve.tensor_reduce(top[b % 2][:], p_sc[b % 2][:].rearrange("n o h -> n h o"), AX_X,
                                  ALU.max).then_inc(top_done, 1)
                dve.wait_ge(top_done, s + 1)
                if b == 0 and at_least(g, 2):
                    dve.wait_ge(skewed[p], 16 * (1 + NO - NLOC) * w)
                dve.tensor_tensor(probs[p][:, :, b, :], p_sc[b % 2][:], over(top[b % 2][:], NO),
                                  ALU.subtract).then_inc(sub_done, 1)

            def divide_and_gate(g, p):
                for i in range(2):
                    dve.wait_ge(pv_done, 2 * g + i + 1)
                    dve.reciprocal(inv_sum[:, 2 * i:2 * i + 2, :], p_o[i][:, :, :, DH]).then_inc(inv_done, 1)
                    dve.wait_ge(inv_done, 2 * g + i + 1)
                    dve.tensor_tensor(heads_out[:, 2 * i:2 * i + 2, :].rearrange("n b (h d) -> n b h d", h=NH),
                                      p_o[i][:, :, :, 0:DH], over(inv_sum[:, 2 * i:2 * i + 2, :], DH, 3),
                                      ALU.mult).then_inc(out_done, 1)
                dve.wait_ge(out_done, 2 * (g + 1))
                dve.wait_ge(gate_done, 2 * (g + 1))
                if at_least(g, 1):
                    dve.wait_ge(gatedT_made, g)
                dve.scalar_tensor_tensor(out=gated[:], in0=gate[p][:], scalar=1.0, in1=heads_out[:], op0=ALU.add,
                                         op1=ALU.mult).then_inc(gated_done, 1)

            def add_to_h(g):
                dve.wait_ge(rows_made, g + 1)
                rows = T.H[:, bass.ds(g * GB, GB), :]
                dve.tensor_tensor(rows, rows, p_rows, ALU.add).then_inc(h_done, 1)

            def turn(g, p, w):
                products_of(g, p, 0)
                products_of(g, p, 1)
                less_maximum(g, p, 0, w)
                products_of(g, p, 2)
                less_maximum(g, p, 1, w)
                products_of(g, p, 3)
                less_maximum(g, p, 2, w)
                if at_least(g, 2):
                    add_to_h(g - 2)
                if below(g, NG - 2):
                    moments(g + 2)
                less_maximum(g, p, 3, w)
                if below(g, NG - 2):
                    normalize(g + 2, p)
                if at_least(g, 1):
                    divide_and_gate(g - 1, 1 - p)

            for g in range(2):
                moments(g)
                normalize(g, g)
            turn(0, 0, 0)
            turn(1, 1, 0)
            with dve.Fori(1, NG // 2 - 1) as k:
                turn(2 * k, 0, k)
                turn(2 * k + 1, 1, k)
            turn(NG - 2, 0, NG // 2 - 1)
            turn(NG - 1, 1, NG // 2 - 1)
            add_to_h(NG - 2)
            divide_and_gate(NG - 1, 1)
            add_to_h(NG - 1)


def stage_dispatch(T):
    nc, t, sem = T.nc, T.t, T.sem
    with ExitStack() as ctx:
        def sb(name, shape, dt=F32):
            return ctx.enter_context(nc.sbuf_tensor(name, shape, dt))

        def ps(name, shape, dt=F32):
            return ctx.enter_context(nc.psum_tensor(name, shape, dt))

        w_gate = sb("di_w_gate", [D, E])
        b_gate = sb("di_b_gate", [1, E])
        ones_row = sb("di_ones_row", [1, L])
        earlier = sb("di_earlier", [L, L], BF16)
        all_ones = sb("di_all_ones", [L, L], BF16)
        empty = sb("di_empty", [128, ROW])
        stats = sb("di_stats", [L, GB, 6])
        mv = sb("di_mv", [L, GB, 2])
        var_eps = sb("di_var_eps", [L, GB])
        rstd = sb("di_rstd", [L, GB])
        z = [sb(f"di_z{p}", [L, GB, D]) for p in range(2)]
        zT = [sb(f"di_zT{p}", [D, GB, L]) for p in range(2)]
        rows = sb("di_rows", [L, B, ROW])
        best = sb("di_best", [L, B])
        less = sb("di_less", [L, B, E])
        preference = sb("di_preference", [L, B, E])
        preference_int = sb("di_preference_int", [L, B, E], I32)
        candidates = sb("di_candidates", [L, B, E])
        first = sb("di_first", [L, B])
        hot = sb("di_hot", [L, B, E])
        hot_bf = sb("di_hot_bf", [L, B, E], BF16)
        score_sum = sb("di_score_sum", [L, B])
        totals = sb("di_totals", [L, E, B])
        same_expert = sb("di_same_expert", [L, E, B])
        running = sb("di_running", [L, E, B])
        tiles_int = sb("di_tiles_int", [L, E], I32)
        tiles_shifted = sb("di_tiles_shifted", [L, E], I32)
        tiles = sb("di_tiles", [L, E])
        ones_e = sb("di_ones_e", [L, E])
        tile_end = sb("di_tile_end", [L, E])
        base = sb("di_base", [L, E])
        place = sb("di_place", [L, B, E])
        slot_f = sb("di_slot_f", [L, B])
        slot = sb("di_slot", [L, B], I32)
        tile_no = sb("di_tile_no", [1, NTILES])
        tile_no_int = sb("di_tile_no_int", [1, NTILES], I32)
        passed = sb("di_passed", [1, NTILES, E])
        tile_expert_f = sb("di_tile_expert_f", [1, NTILES])
        p_zT = [ps(f"di_p_zT{p}", [D, GB, L]) for p in range(2)]
        p_logits = ps("di_p_logits", [L, B, E])
        p_before = ps("di_p_before", [L, B, E])
        p_total = ps("di_p_total", [L, B, E])

        weights_in = sem("di_weights_in")
        consts = sem("di_consts")
        emptied = sem("di_emptied")
        stats_done = sem("di_stats_done")
        mv_done = sem("di_mv_done")
        eps_added = sem("di_eps_added")
        rstd_done = sem("di_rstd_done")
        z_done = sem("di_z_done")
        z_copied = sem("di_z_copied")
        h_copied = sem("di_h_copied")
        zT_made = sem("di_zT_made")
        zT_kept = sem("di_zT_kept")
        logits_made = sem("di_logits_made")
        step = sem("di_step")
        less_done = sem("di_less_done")
        exp_done = sem("di_exp_done")
        hot_done = sem("di_hot_done")
        counts_made = sem("di_counts_made")
        score_done = sem("di_score_done")
        slot_done = sem("di_slot_done")
        tile_expert_done = sem("di_tile_expert_done")
        dispatched = sem("di_dispatched")

        block = ctx.enter_context(nc.Block())

        @block.sync
        def _(sp):
            T.clear_old(sp)
            sp.dma_start(w_gate[:], t["r_w"]).then_inc(weights_in, 16)
            sp.dma_start(b_gate[:], t["r_b"].unsqueeze(0)).then_inc(weights_in, 16)
            sp.wait_ge(consts, 8)
            sp.dma_start(T.slot_rows.rearrange("(i n) c -> n i c", n=128), over(empty[:], NTILES * TILE // 128)
                         ).then_inc(emptied, 16)
            sp.wait_ge(emptied, 16)

        @block.gpsimd
        def _(pool):
            pool.memset(all_ones[:], 1.0).then_inc(consts, 1)
            pool.wait_ge(consts, 1)
            pool.affine_select(out=earlier[:], in_=all_ones[:], compare_op=ALU.is_gt, fill=0.0, base=0,
                               pattern=[[1, L]], channel_multiplier=-1).then_inc(consts, 1)
            pool.iota(preference_int[:], pattern=[[0, B], [-1, E]], base=E, channel_multiplier=0).then_inc(consts, 1)
            pool.iota(tile_no_int[:], pattern=[[1, NTILES]], base=0, channel_multiplier=0).then_inc(consts, 1)
            pool.wait_ge(consts, 4)
            pool.tensor_copy(preference[:], preference_int[:]).then_inc(consts, 1)
            pool.tensor_copy(tile_no[:], tile_no_int[:]).then_inc(consts, 1)
            pool.memset(empty[:], 0.0).then_inc(consts, 1)
            pool.wait_ge(consts, 7)
            pool.memset(empty[:, 2 * D:2 * D + 1].bitcast(I32), N).then_inc(consts, 1)
            pool.wait_ge(consts, 8)
            pool.iota(rows[:, :, 2 * D:2 * D + 1].bitcast(I32), pattern=[[L, B], [0, 1]], base=0,
                      channel_multiplier=1).then_inc(consts, 1)

            def finish(g, p):
                pool.wait_ge(mv_done, GB * (g + 1))
                pool.tensor_tensor(var_eps[:], mv[:, :, 1], T.eps[:], ALU.add).then_inc(eps_added, 1)
                pool.wait_ge(eps_added, g + 1)
                pool.tensor_tensor(rstd[:], var_eps[:], T.neg_half[:], ALU.pow).then_inc(rstd_done, 1)
                T.wait_alone(pool, z_done, g + 1)
                pool.tensor_copy(rows[:, bass.ds(g * GB, GB), 0:D], z[p][:]).then_inc(z_copied, 1)

            with pool.Fori(0, NG // 2) as k:
                finish(2 * k, 0)
                finish(2 * k + 1, 1)
            pool.wait_ge(h_copied, NG)
            pool.wait_ge(score_done, 1)
            pool.wait_ge(slot_done, 1)
            pool.wait_ge(consts, 9)
            pool.wait_ge(emptied, 16)
            pool.wait_ge(z_copied, NG)
            for b in range(B):
                pool.indirect_dma_start(out=T.slot_rows,
                                        out_offset=bass.IndirectOffsetOnAxis(ap=slot[:, b:b + 1], axis=0),
                                        in_=rows[:, b, :], in_offset=None).then_inc(dispatched, 16)
            pool.wait_ge(dispatched, 16 * B)

        @block.tensor
        def _(pe):
            pe.wait_ge(weights_in, 32)

            def transposes(g, p):
                T.wait_alone(pe, z_done, g + 1)
                if at_least(g, 2):
                    T.wait_alone(pe, zT_kept, g - 1)
                for b in range(GB):
                    last = pe.transpose(p_zT[p][:, b, :], z[p][:, b, :], T.ident[0:L, 0:L])
                last.then_inc(zT_made, 1)

            def route(g, p):
                T.wait_alone(pe, zT_kept, g + 1)
                for b in range(GB):
                    out = p_logits[:, bass.ds(g * GB + b, 1), :].rearrange("l o e -> l (o e)")
                    pe.matmul(out, zT[p][:, b, :], w_gate[:], start=True, stop=False)
                    last = pe.matmul(out, ones_row[:], b_gate[:], start=False, stop=True)
                last.then_inc(logits_made, 1)

            pe.wait_ge(step, 1)
            transposes(0, 0)
            transposes(1, 1)
            route(0, 0)
            with pe.Fori(1, NG // 2) as k:
                transposes(2 * k, 0)
                route(2 * k - 1, 1)
                transposes(2 * k + 1, 1)
                route(2 * k, 0)
            route(NG - 1, 1)
            pe.wait_ge(hot_done, 1)
            pe.wait_ge(consts, 2)
            pe.matmul(p_total[:], all_ones[:], hot_bf[:], start=True, stop=True).then_inc(counts_made, 1)
            pe.matmul(p_before[:], earlier[:], hot_bf[:], start=True, stop=True).then_inc(counts_made, 1)

        @block.scalar
        def _(act):
            with act.Fori(0, NG // 2) as k:
                for p in range(2):
                    g = 2 * k + p
                    act.wait_ge(zT_made, g + 1)
                    act.wait_ge(logits_made, g + 1)
                    act.copy(zT[p][:], p_zT[p][:]).then_inc(zT_kept, 1)
                    act.copy(rows[:, bass.ds(g * GB, GB), D:2 * D], T.H[:, bass.ds(g * GB, GB), :]).then_inc(h_copied, 1)
            act.wait_ge(less_done, 1)
            act.activation(less[:], less[:], ACT.Exp).then_inc(exp_done, 1)

        @block.vector
        def _(dve):
            dve.sem_inc(logits_made, 2)
            dve.memset(ones_row[:], 1.0)
            dve.memset(ones_e[:], 1.0)
            dve.memset(same_expert[:], 1.0).then_inc(step, 1)
            dve.wait_ge(step, 1)
            dve.memset(same_expert[:, :, 0:1], 0.0).then_inc(step, 1)

            def norm(g, p):
                for b in range(GB):
                    dve.bn_stats(stats[:, b, :], T.H[:, g * GB + b, :]).then_inc(stats_done, 1)
                T.wait_alone(dve, stats_done, GB * (g + 1))
                for b in range(GB):
                    dve.bn_aggr(mv[:, b, :], stats[:, b, :]).then_inc(mv_done, 1)
                T.wait_alone(dve, rstd_done, g + 1)
                if at_least(g, 2):
                    T.wait_alone(dve, zT_made, g - 1)
                    T.wait_alone(dve, z_copied, g - 1)
                for b in range(GB):
                    last = dve.tensor_scalar(z[p][:, b, :], T.H[:, g * GB + b, :], mv[:, b, 0:1],
                                             rstd[:, b:b + 1], ALU.subtract, ALU.mult)
                last.then_inc(z_done, 1)

            norm(0, 0)
            norm(1, 1)
            with dve.Fori(1, NG // 2) as k:
                norm(2 * k, 0)
                norm(2 * k + 1, 1)

            dve.wait_ge(logits_made, NG + 2)
            dve.tensor_reduce(best[:], p_logits[:], AX_X, ALU.max).then_inc(step, 1)
            dve.wait_ge(step, 3)
            dve.tensor_tensor(less[:], p_logits[:], over(best[:], E, 2), ALU.subtract).then_inc(less_done, 1)
            dve.wait_ge(consts, 6)
            dve.tensor_tensor(candidates[:], p_logits[:], over(best[:], E, 2), ALU.is_equal).then_inc(step, 1)
            dve.wait_ge(step, 4)
            dve.tensor_tensor(candidates[:], candidates[:], preference[:], ALU.mult).then_inc(step, 1)
            dve.wait_ge(step, 5)
            dve.tensor_reduce(first[:], candidates[:], AX_X, ALU.max).then_inc(step, 1)
            dve.wait_ge(step, 6)
            dve.tensor_tensor(hot_bf[:], candidates[:], over(first[:], E, 2), ALU.is_equal).then_inc(hot_done, 1)
            dve.tensor_tensor(hot[:], candidates[:], over(first[:], E, 2), ALU.is_equal).then_inc(step, 1)
            dve.wait_ge(exp_done, 1)
            dve.tensor_reduce(score_sum[:], less[:], AX_X, ALU.add).then_inc(step, 1)
            dve.wait_ge(step, 8)
            dve.reciprocal(rows[:, :, 2 * D + 1:2 * D + 2].rearrange("l b o -> l (b o)"), score_sum[:]
                           ).then_inc(score_done, 1)
            dve.wait_ge(counts_made, 2)
            dve.tensor_copy(totals[:].rearrange("l e b -> l b e"), p_total[:]).then_inc(step, 1)
            dve.wait_ge(step, 9)
            dve.tensor_tensor_scan(running[:].rearrange("l e b -> l (e b)"),
                                   same_expert[:].rearrange("l e b -> l (e b)"),
                                   totals[:].rearrange("l e b -> l (e b)"), 0.0, ALU.mult, ALU.add).then_inc(step, 1)
            dve.wait_ge(step, 10)
            dve.tensor_scalar(tiles_int[:], running[:, :, B - 1], float(TILE - 1), None, ALU.add).then_inc(step, 1)
            dve.wait_ge(step, 11)
            dve.tensor_scalar(tiles_shifted[:], tiles_int[:], TILE.bit_length() - 1, None,
                              ALU.arith_shift_right).then_inc(step, 1)
            dve.wait_ge(step, 12)
            dve.tensor_copy(tiles[:], tiles_shifted[:]).then_inc(step, 1)
            dve.wait_ge(step, 13)
            dve.tensor_tensor_scan(tile_end[:], ones_e[:], tiles[:], 0.0, ALU.mult, ALU.add).then_inc(step, 1)
            dve.wait_ge(step, 14)
            dve.tensor_tensor(base[:], tile_end[:], tiles[:], ALU.subtract).then_inc(step, 1)
            dve.wait_ge(step, 15)
            dve.tensor_scalar(base[:], base[:], float(TILE), None, ALU.mult).then_inc(step, 1)
            dve.tensor_tensor(running[:], running[:], totals[:], ALU.subtract).then_inc(step, 1)
            dve.wait_ge(step, 17)
            dve.tensor_tensor(running[:], running[:], over(base[:], B, 2), ALU.add).then_inc(step, 1)
            dve.wait_ge(step, 18)
            dve.tensor_tensor(place[:], p_before[:], running[:].rearrange("l e b -> l b e"), ALU.add).then_inc(step, 1)
            dve.wait_ge(step, 19)
            dve.tensor_tensor(place[:], place[:], hot[:], ALU.mult).then_inc(step, 1)
            dve.wait_ge(step, 20)
            dve.tensor_reduce(slot_f[:], place[:], AX_X, ALU.add).then_inc(step, 1)
            dve.wait_ge(step, 21)
            dve.tensor_copy(slot[:], slot_f[:]).then_inc(slot_done, 1)
            dve.tensor_tensor(passed[:], over(tile_end[0:1, :], NTILES), over(tile_no[:], E, 2),
                              ALU.is_le).then_inc(step, 1)
            dve.wait_ge(step, 22)
            dve.tensor_reduce(tile_expert_f[:], passed[:], AX_X, ALU.add).then_inc(step, 1)
            dve.wait_ge(step, 23)
            dve.tensor_scalar(T.tile_expert[:], tile_expert_f[:], float(E - 1), None, ALU.min
                              ).then_inc(tile_expert_done, 1)


def stage_top1(T):
    nc, t, sem = T.nc, T.t, T.sem
    S = TILE // 128
    FC = F // 128
    W1, W2, B1 = 0, F, F + FC * D
    PACK = B1 + FC
    with ExitStack() as ctx:
        def sb(name, shape, dt=F32):
            return ctx.enter_context(nc.sbuf_tensor(name, shape, dt))

        def ps(name, shape, dt=F32):
            return ctx.enter_context(nc.psum_tensor(name, shape, dt))

        experts = sb("tp_experts", [128, E, PACK])
        b2 = sb("tp_b2", [128, E, D])
        now = [sb(f"tp_now{p}", [128, PACK]) for p in range(2)]
        rows = [sb(f"tp_rows{p}", [128, S, ROW]) for p in range(2)]
        xT = [sb(f"tp_xT{p}", [D, TILE]) for p in range(2)]
        hidden = [sb(f"tp_hidden{p}", [128, FC, TILE]) for p in range(2)]
        plus_b2 = [sb(f"tp_plus_b2{p}", [128, S, D]) for p in range(2)]
        result = [sb(f"tp_result{p}", [128, S, D]) for p in range(2)]
        token = [sb(f"tp_token{p}", [128, S], I32) for p in range(2)]
        BANK = 512
        p_xT = [ps(f"tp_p_xT{p}", [D, BANK]) for p in range(2)]
        p_hidden = [ps(f"tp_p_hidden{c}", [128, BANK]) for c in range(FC)]
        p_y = [ps(f"tp_p_y{p}", [128, BANK // D, D]) for p in range(2)]

        experts_in = sem("tp_experts_in")
        rows_in = [sem(f"tp_rows_in{p}") for p in range(2)]
        now_done = sem("tp_now_done")
        xT_made = sem("tp_xT_made")
        xT_kept = sem("tp_xT_kept")
        hidden_made = sem("tp_hidden_made")
        relu_done = sem("tp_relu_done")
        y_made = sem("tp_y_made")
        b2_added = sem("tp_b2_added")
        result_done = sem("tp_result_done")
        stored = [sem(f"tp_stored{p}") for p in range(2)]

        block = ctx.enter_context(nc.Block())


        @block.sync
        def _(sp):
            T.clear_old(sp)
            sp.dma_start(experts[:], t["m_pack"]).then_inc(experts_in, 16)
            sp.dma_start(b2[:], t["m_b2"].rearrange("e d -> (e d)").partition_broadcast(128)).then_inc(experts_in, 16)

            def load(w, p):
                i = 2 * w + p
                sp.dma_start(rows[p][:], T.slot_rows[bass.ds(i * TILE, TILE), :].rearrange("(s n) c -> n s c", n=128)
                             ).then_inc(rows_in[p], 16)

            load(0, 0)
            load(0, 1)
            with sp.Fori(1, NTILES // 2) as w:
                for p in range(2):
                    sp.wait_ge(result_done, 2 * w + p - 1)
                    load(w, p)

        @block.gpsimd
        def _(pool):
            def store(w, p):
                T.wait_alone(pool, result_done, 2 * w + p + 1)
                for s in range(S):
                    pool.indirect_dma_start(out=T.out_rows,
                                            out_offset=bass.IndirectOffsetOnAxis(ap=token[p][:, s:s + 1], axis=0),
                                            in_=result[p][:, s, :], in_offset=None, bounds_check=N - 1,
                                            oob_is_err=False).then_inc(stored[p], 16)

            with pool.Fori(0, NTILES // 2) as w:
                store(w, 0)
                store(w, 1)
            for p in range(2):
                pool.wait_ge(stored[p], 16 * S * NTILES // 2)

        @block.tensor
        def _(pe):
            def transposes(w, p):
                i = 2 * w + p
                T.wait_alone(pe, rows_in[p], 16 * (w + 1))
                if at_least(w, 1):
                    T.wait_alone(pe, xT_kept, i - 1)
                for s in range(S):
                    last = pe.transpose(p_xT[p][:, s * 128:(s + 1) * 128], rows[p][:, s, 0:D], T.ident[:])
                last.then_inc(xT_made, 1)

            def into_hidden(w, p):
                i = 2 * w + p
                T.wait_alone(pe, now_done, i + 1)
                T.wait_alone(pe, xT_kept, i + 1)
                for c in range(FC):
                    if at_least(w, 1) or p == 1:
                        T.wait_alone(pe, relu_done, FC * (i - 1) + c + 1)
                    pe.matmul(p_hidden[c][:, 0:TILE], now[p][:, W1 + c * 128:W1 + (c + 1) * 128], xT[p][:],
                              start=True, stop=True).then_inc(hidden_made, 1)

            def out_of_hidden(w, p):
                i = 2 * w + p
                T.wait_alone(pe, relu_done, FC * (i + 1))
                if at_least(w, 1):
                    T.wait_alone(pe, b2_added, i - 1)
                for s in range(S):
                    for c in range(FC):
                        last = pe.matmul(p_y[p][:, s, :], hidden[p][:, c, s * 128:(s + 1) * 128],
                                         now[p][:, W2 + c * D:W2 + (c + 1) * D], start=(c == 0), stop=(c == FC - 1))
                last.then_inc(y_made, 1)

            transposes(0, 0)
            into_hidden(0, 0)
            transposes(0, 1)
            into_hidden(0, 1)
            out_of_hidden(0, 0)
            with pe.Fori(1, NTILES // 2) as w:
                transposes(w, 0)
                into_hidden(w, 0)
                out_of_hidden(w - 1, 1)
                transposes(w, 1)
                into_hidden(w, 1)
                out_of_hidden(w, 0)
            out_of_hidden(NTILES // 2 - 1, 1)

        @block.scalar
        def _(act):
            def tile(w, p):
                i = 2 * w + p
                T.wait_alone(act, xT_made, i + 1)
                if at_least(w, 1):
                    T.wait_alone(act, y_made, i - 1)
                act.copy(xT[p][:], p_xT[p][:, 0:TILE]).then_inc(xT_kept, 1)
                for c in range(FC):
                    act.wait_ge(hidden_made, FC * i + c + 1)
                    act.activation(hidden[p][:, c, :], p_hidden[c][:, 0:TILE], ACT.Relu,
                                   bias=now[p][:, B1 + c:B1 + c + 1]).then_inc(relu_done, 1)

            tile(0, 0)
            tile(0, 1)
            with act.Fori(1, NTILES // 2) as w:
                tile(w, 0)
                tile(w, 1)

        @block.vector
        def _(dve):
            dve.wait_ge(experts_in, 32)

            def bring(w, p):
                i = 2 * w + p
                if at_least(w, 1):
                    T.wait_alone(dve, y_made, i - 1)
                e = dve.value_load(T.tile_expert[0:1, bass.ds(i, 1)], min_val=0, max_val=E - 1)
                dve.tensor_copy(now[p][:], experts[:, bass.ds(e, 1), :].rearrange("k o n -> k (o n)")
                                ).then_inc(now_done, 1)

            def finish(w, p):
                i = 2 * w + p
                T.wait_alone(dve, y_made, i + 1)
                e = dve.value_load(T.tile_expert[0:1, bass.ds(i, 1)], min_val=0, max_val=E - 1)
                dve.tensor_tensor(plus_b2[p][:], p_y[p][:, 0:S, :],
                                  over(b2[:, bass.ds(e, 1), :].rearrange("n o d -> n (o d)"), S),
                                  ALU.add).then_inc(b2_added, 1)
                T.wait_alone(dve, b2_added, i + 1)
                if at_least(w, 1):
                    T.wait_alone(dve, stored[p], 16 * S * w)
                dve.tensor_copy(token[p][:], rows[p][:, :, 2 * D].bitcast(I32))
                for s in range(S):
                    last = dve.scalar_tensor_tensor(out=result[p][:, s, :], in0=plus_b2[p][:, s, :],
                                                    scalar=rows[p][:, s, 2 * D + 1:2 * D + 2],
                                                    in1=rows[p][:, s, D:2 * D], op0=ALU.mult, op1=ALU.add)
                last.then_inc(result_done, 1)

            bring(0, 0)
            bring(0, 1)
            finish(0, 0)
            with dve.Fori(1, NTILES // 2) as w:
                bring(w, 0)
                finish(w - 1, 1)
                bring(w, 1)
                finish(w, 0)
            finish(NTILES // 2 - 1, 1)


STAGES = [stage_tokenizer, stage_attention, stage_router_logits, stage_choose, stage_expert_choice,
          stage_offset_attention, stage_dispatch, stage_top1]


def build(nc, t, out):
    with ExitStack() as ctx:
        T = Tower(nc, ctx, t, out)
        for stage in STAGES:
            T.next_stage()
            stage(T)


def layouts(v):
    import numpy as np
    a = {
        "x": v["x"], "w_proj": v["L0_tok_W_proj"], "w_pwT": v["L0_tok_W_pw"].T, "w_dw": v["L0_tok_W_dw"],
        "b_proj": v["L0_tok_b_proj"], "b_dw": v["L0_tok_b_dw"], "b_pw": v["L0_tok_b_pw"],
        "gamma": v["L0_tok_gamma"], "beta": v["L0_tok_beta"],
        "w_qkvT": v["L0_attn_w_qkv"].T, "w_aggT": v["L0_attn_w_agg"].T, "b_agg": v["L0_attn_b_agg"],
        "w_router": v["L0_ffn_Wr"], "e_w1": v["L0_ffn_W1"].reshape(E * D, F), "e_w2": v["L0_ffn_W2"].reshape(E * F, D),
        "e_b1": v["L0_ffn_b1"].reshape(E, F // 128, 128).transpose(2, 0, 1), "e_b2": v["L0_ffn_b2"],
    }
    tables = list(range(OFF_LOCAL, -1, -1)) + list(range(OFF_LOCAL + 1, len(OFFS)))
    omega = np.array([0.0, 0.0, 1.0, 1.0, 4.0, 4.0, 6.0, 6.0]) * np.pi / np.log(1.0 + 4096.0)
    cosines = np.cos(omega[None, :] * np.log(1.0 + np.array(OFFS, np.float64))[:, None]) * (omega > 0.0)
    a.update({
        "o_wqkv": v["L1_attn_W_qkv"], "o_wgate": v["L1_attn_W_gate"], "o_wout": v["L1_attn_W_out"],
        "o_gain": np.repeat(v["L1_attn_if_gain"], DH), "o_bqk": v["L1_attn_b_qkv"][0:2 * D].reshape(2, D).T,
        "o_bvg": np.concatenate([v["L1_attn_b_qkv"][2 * D:], v["L1_attn_b_gate"]]), "o_bout": v["L1_attn_b_out"],
        "o_scale": np.tile(v["L1_attn_scale_embed"][tables].T, (NH, 1)),
        "o_pos": v["L1_attn_pos_bias"][tables].reshape(-1), "o_cos": cosines.astype(np.float32).reshape(-1),
        "o_amp": v["L1_attn_disp_amp"],
        "r_w": v["L1_ffn_Wg"], "r_b": v["L1_ffn_bg"], "m_b2": v["L1_ffn_b2"],
        "m_pack": np.concatenate([
            v["L1_ffn_W1"].transpose(1, 0, 2),
            v["L1_ffn_W2"].reshape(E, F // 128, 128, D).transpose(2, 0, 1, 3).reshape(128, E, F // 128 * D),
            v["L1_ffn_b1"].reshape(E, F // 128, 128).transpose(2, 0, 1)], axis=2),
    })
    return {k: np.ascontiguousarray(x) for k, x in a.items()}


def kernel(**inputs):
    import numpy as _np
    import concourse.bacc as _bacc
    from concourse import mybir as _mybir
    from concourse.bass_utils import run_bass_kernel_spmd as _run

    nc = _bacc.Bacc("TRN2", target_bir_lowering=False, num_devices=1)
    arrays, aps = {}, {}
    for name, a in layouts({k: _np.asarray(v) for k, v in inputs.items()}).items():
        arrays[f"in_{name}_dram"] = a
        aps[name] = nc.dram_tensor(f"in_{name}_dram", a.shape, _mybir.dt.from_np(a.dtype), kind="ExternalInput").ap()
    out = nc.dram_tensor("out_dram", (B, L, D), F32, kind="ExternalOutput").ap()
    build(nc, aps, out)
    r = _run(nc, [arrays], core_ids=[0])
    return r.results[0]["out_dram"]
```

```python
from contextlib import ExitStack

import concourse.bass as bass
from concourse import mybir

F32 = mybir.dt.float32
BF16 = mybir.dt.bfloat16
I32 = mybir.dt.int32
U32 = mybir.dt.uint32
ALU = mybir.AluOpType
ACT = mybir.ActivationFunctionType
AX_X = mybir.AxisListType.X

B, CIN, L, D = 64, 64, 125, 128
GB = 4
NG = B // GB
GT = GB * L
N = B * L
NH, DH = 8, 16
EPS = 1e-5
E, F, CAP = 8, 512, 1024
OFF_LOCAL = 32
OFFS = list(range(OFF_LOCAL, -1, -1)) + [o for o in (48, 64, 96, 128, 192, 256, 384, 512, 768, 1024) if o < L]
TILE = 256
NTILES = (N + E * (TILE - 1)) // TILE
NTILES += -NTILES % 4
ROW = 2 * D + 2


class Tower:

    def __init__(self, nc, ctx, t, out):
        self.nc, self.ctx, self.t, self.out = nc, ctx, t, out
        self.H = self.sb("H", [L, B, D])
        self.ident = self.sb("ident", [128, 128])
        self.ident_bf = self.sb("ident_bf", [128, 128], BF16)
        self.chosen = self.sb("chosen", [128, E * CAP // 128], I32)
        self.head_mask = self.sb("head_mask", [D, NH])
        self.h_rows = self.dram("h_rows", [N, D])
        self.z_rows = self.dram("z_rows", [N, D + E])
        self.logits = self.dram("logits", [E, N])
        self.diagonals = [self.dram(f"diagonals{p}", [OFFS[-1] + L, L, GB * NH]) for p in range(2)]
        self.slot_rows = self.dram("slot_rows", [NTILES * TILE, ROW])
        self.tile_expert = self.sb("tile_expert", [1, NTILES], I32)
        self.out_rows = out.rearrange("b l d -> (b l) d")
        self.chosen_rows = self.dram("chosen_rows", [E * CAP])
        self.neg_half = self.sb("neg_half", [L, GB])
        self.consts_done = ctx.enter_context(nc.semaphore("consts_done"))
        self.waited = ctx.enter_context(nc.semaphore("waited"))
        self.old_ctx, self.stage_ctx, self.stage_sems = ExitStack(), ExitStack(), []
        self.eps = self.sb("eps", [L, GB])

    def dram(self, name, shape, dt=F32):
        return self.nc.dram_tensor(name, shape, dt, kind="Internal").ap()

    def sb(self, name, shape, dt=F32):
        return self.ctx.enter_context(self.nc.sbuf_tensor(name, shape, dt))

    def wait_alone(self, eng, sem, value):
        eng.wait_ge(sem, value)
        if not isinstance(value, int):
            eng.sem_inc(self.waited, 1)

    def sem(self, name):
        s = self.stage_ctx.enter_context(self.nc.semaphore(name))
        self.stage_sems.append(s)
        return s

    def next_stage(self):
        self.old_ctx.close()
        self.old_ctx, self.old_sems = self.stage_ctx, self.stage_sems
        self.stage_ctx, self.stage_sems = self.ctx.enter_context(ExitStack()), []

    def clear_old(self, sp):
        for s in self.old_sems:
            sp.sem_clear(s)


def at_least(g, n):
    return not isinstance(g, int) or g >= n


def here(g):
    return not isinstance(g, int) or 0 <= g < NG


def below(g, n):
    return not isinstance(g, int) or g < n


def over(ap, n, axis=1):
    shape = list(ap.shape)
    return ap.unsqueeze(axis).broadcast_to(shape[:axis] + [n] + shape[axis:])


def stage_tokenizer(T):
    nc, t, sem = T.nc, T.t, T.sem
    with ExitStack() as ctx:
        def sb(name, shape, dt=F32):
            return ctx.enter_context(nc.sbuf_tensor(name, shape, dt))

        def ps(name, shape, dt=F32):
            return ctx.enter_context(nc.psum_tensor(name, shape, dt))

        w_proj = sb("tk_w_proj", [D, CIN])
        w_pwT = sb("tk_w_pwT", [D, D])
        w_pw_taps = sb("tk_w_pw_taps", [D, 3, D])
        w_dw = sb("tk_w_dw", [D, 3])
        b_proj = sb("tk_b_proj", [D, 1])
        b_dw = sb("tk_b_dw", [D, 1])
        b_pw = sb("tk_b_pw", [L, D])
        gamma = sb("tk_gamma", [L, D])
        beta = sb("tk_beta", [L, D])
        taps02 = sb("tk_taps02", [2 * CIN, D])
        tap1 = sb("tk_tap1", [CIN, D])
        edge = sb("tk_edge", [D, 3])
        conv_bias = sb("tk_conv_bias", [D, L])
        bias_tok = sb("tk_bias_tok", [L, D])
        x_in = [sb(f"tk_x{p}", [2 * CIN, GB, L + 2]) for p in range(2)]
        pre = [sb(f"tk_pre{p}", [L, GB, D]) for p in range(2)]
        y = [sb(f"tk_y{p}", [L, GB, D]) for p in range(2)]
        z = [sb(f"tk_z{p}", [L, GB, D]) for p in range(2)]
        stats = [sb(f"tk_stats{p}", [L, GB, 6]) for p in range(2)]
        mv = [sb(f"tk_mv{p}", [L, GB, 2]) for p in range(2)]
        var_eps = [sb(f"tk_var_eps{p}", [L, GB]) for p in range(2)]
        rstd = [sb(f"tk_rstd{p}", [L, GB]) for p in range(2)]
        p_w = ps("tk_p_w", [128, 2, D])
        p_bias = ps("tk_p_bias", [L, D])
        p_y = [ps(f"tk_p_y{p}", [L, GB, D]) for p in range(2)]

        weights_in = sem("tk_weights_in")
        ident_zero = sem("tk_ident_zero")
        padded = sem("tk_padded")
        taps_scaled = sem("tk_taps_scaled")
        bias_col = sem("tk_bias_col")
        joined = sem("tk_joined")
        joined_sb = sem("tk_joined_sb")
        x_ready = [sem(f"tk_x_ready{p}") for p in range(2)]
        mm_done = sem("tk_mm_done")
        pre_ready = sem("tk_pre_ready")
        silu_done = sem("tk_silu_done")
        stats_done = sem("tk_stats_done")
        mv_done = sem("tk_mv_done")
        eps_added = sem("tk_eps_added")
        rstd_done = sem("tk_rstd_done")
        z_done = sem("tk_z_done")
        scaled = sem("tk_scaled")
        h_done = sem("tk_h_done")

        block = ctx.enter_context(nc.Block())

        @block.sync
        def _(sp):
            T.clear_old(sp)
            for dst, src in ((w_proj[:], t["w_proj"]), (w_pwT[:], t["w_pwT"]), (w_dw[:], t["w_dw"]),
                             (b_proj[:], t["b_proj"].unsqueeze(1)), (b_dw[:], t["b_dw"].unsqueeze(1)),
                             (b_pw[:], t["b_pw"].partition_broadcast(L)),
                             (gamma[:], t["gamma"].partition_broadcast(L)),
                             (beta[:], t["beta"].partition_broadcast(L))):
                sp.dma_start(dst, src).then_inc(weights_in, 16)

            def load(k, p):
                src = t["x"][bass.ds((2 * k + p) * GB, GB), :, :].rearrange("b c l -> c b l")
                sp.dma_start(x_in[p][0:CIN, :, 1:L + 1], src).then_inc(x_ready[p], 16)
                sp.dma_start(x_in[p][CIN:2 * CIN, :, 0:L - 1], src[:, :, 1:L]).then_inc(x_ready[p], 16)

            sp.wait_ge(padded, 4)
            load(0, 0)
            load(0, 1)
            with sp.Fori(1, NG // 2) as k:
                for p in range(2):
                    sp.wait_ge(mm_done, 2 * k + p - 1)
                    load(k, p)

        @block.gpsimd
        def _(pool):
            pool.memset(T.neg_half[:], -0.5)
            pool.memset(T.eps[:], EPS).then_inc(T.consts_done, 1)
            pool.memset(T.ident[:], 0.0).then_inc(ident_zero, 1)
            pool.wait_ge(ident_zero, 1)
            pool.affine_select(out=T.ident[:], in_=T.ident[:], compare_op=ALU.not_equal, fill=1.0,
                               base=0, pattern=[[-1, 128]], channel_multiplier=1).then_inc(T.consts_done, 1)
            pool.wait_ge(T.consts_done, 2)
            pool.tensor_copy(T.ident_bf[:], T.ident[:]).then_inc(T.consts_done, 1)
            pool.wait_ge(weights_in, 128)

            def finish(k, p):
                g = 2 * k + p
                pool.wait_ge(mv_done, GB * (g + 1))
                pool.tensor_tensor(var_eps[p][:], mv[p][:, :, 1], T.eps[:], ALU.add).then_inc(eps_added, 1)
                pool.wait_ge(eps_added, g + 1)
                pool.tensor_tensor(rstd[p][:], var_eps[p][:], T.neg_half[:], ALU.pow).then_inc(rstd_done, 1)
                pool.wait_ge(z_done, g + 3)
                pool.tensor_tensor(z[p][:], z[p][:], over(gamma[:], GB), ALU.mult).then_inc(scaled, 1)
                pool.wait_ge(scaled, g + 1)
                pool.tensor_tensor(T.H[:, bass.ds(g * GB, GB), :], z[p][:], over(beta[:], GB),
                                   ALU.add).then_inc(h_done, 1)

            with pool.Fori(0, NG // 2) as k:
                for p in range(2):
                    finish(k, p)

        @block.tensor
        def _(pe):
            pe.wait_ge(weights_in, 128)
            pe.wait_ge(taps_scaled, 3)
            pe.matmul(p_w[0:CIN, 0, :], w_proj[:], w_pw_taps[:, 0, :], start=True, stop=True)
            pe.matmul(p_w[CIN:2 * CIN, 0, :], w_proj[:], w_pw_taps[:, 2, :], start=True, stop=True)
            pe.matmul(p_w[0:CIN, 1, :], w_proj[:], w_pw_taps[:, 1, :], start=True, stop=True)
            pe.wait_ge(bias_col, 4)
            pe.matmul(p_bias[:], conv_bias[:], w_pwT[:], start=True, stop=True).then_inc(joined, 1)
            pe.wait_ge(joined_sb, 3)
            with pe.Fori(0, NG // 2) as k:
                for p in range(2):
                    pe.wait_ge(x_ready[p], 32 * k + 32)
                    pe.wait_ge(pre_ready, 2 * k + p + 1)
                    for b in range(GB):
                        pe.matmul(p_y[p][:, b, :], x_in[p][:, b, 0:L], taps02[:], start=True, stop=False)
                        last = pe.matmul(p_y[p][:, b, :], x_in[p][0:CIN, b, 1:L + 1], tap1[:],
                                         start=False, stop=True)
                    last.then_inc(mm_done, 1)

        @block.scalar
        def _(act):
            with act.Fori(0, NG // 2) as k:
                for p in range(2):
                    act.wait_ge(pre_ready, 2 * k + p + 3)
                    act.wait_ge(z_done, 2 * k + p + 1)
                    act.activation(y[p][:], pre[p][:], ACT.Silu).then_inc(silu_done, 1)

        @block.vector
        def _(dve):
            for p in range(2):
                dve.memset(x_in[p][0:CIN, :, 0:1], 0.0)
                dve.memset(x_in[p][0:CIN, :, L + 1:L + 2], 0.0).then_inc(padded, 1)
                dve.memset(x_in[p][CIN:2 * CIN, :, L - 1:L + 2], 0.0).then_inc(padded, 1)
            dve.sem_inc(pre_ready, 2)
            dve.sem_inc(z_done, 2)
            dve.sem_inc(h_done, 2)
            dve.wait_ge(weights_in, 128)
            for j in range(3):
                dve.tensor_scalar(w_pw_taps[:, j, :], w_pwT[:], w_dw[:, j:j + 1], None,
                                  ALU.mult).then_inc(taps_scaled, 1)
            dve.tensor_scalar(edge[:, 0:3], w_dw[:], b_proj[:, 0:1], None, ALU.mult).then_inc(bias_col, 1)
            dve.wait_ge(bias_col, 1)
            dve.tensor_scalar(conv_bias[:], edge[:, 1:2].broadcast_to([D, L]), b_dw[:, 0:1], edge[:, 0:1],
                              ALU.add, ALU.add).then_inc(bias_col, 1)
            dve.wait_ge(bias_col, 2)
            dve.tensor_scalar(conv_bias[:, 0:1], conv_bias[:, 1:2], edge[:, 0:1], None,
                              ALU.subtract).then_inc(bias_col, 1)
            dve.wait_ge(bias_col, 3)
            dve.tensor_scalar(conv_bias[:, 0:L - 1], conv_bias[:, 0:L - 1], edge[:, 2:3], None,
                              ALU.add).then_inc(bias_col, 1)
            dve.wait_ge(joined, 1)
            dve.tensor_copy(taps02[:], p_w[:, 0, :]).then_inc(joined_sb, 1)
            dve.tensor_copy(tap1[:], p_w[0:CIN, 1, :]).then_inc(joined_sb, 1)
            dve.tensor_tensor(bias_tok[:], p_bias[:], b_pw[:], ALU.add).then_inc(joined_sb, 1)
            dve.wait_ge(joined_sb, 3)

            def add_bias(k, p):
                dve.wait_ge(mm_done, 2 * k + p + 1)
                dve.tensor_tensor(pre[p][:], p_y[p][:], over(bias_tok[:], GB), ALU.add).then_inc(pre_ready, 1)

            def moments(k, p):
                g = 2 * k + p
                dve.wait_ge(silu_done, g + 1)
                for b in range(GB):
                    dve.bn_stats(stats[p][:, b, :], y[p][:, b, :]).then_inc(stats_done, 1)
                T.wait_alone(dve, stats_done, GB * (g + 1))
                for b in range(GB):
                    dve.bn_aggr(mv[p][:, b, :], stats[p][:, b, :]).then_inc(mv_done, 1)

            def normalize(k, p):
                g = 2 * k + p
                dve.wait_ge(rstd_done, g + 1)
                dve.wait_ge(h_done, g + 1)
                for b in range(GB):
                    last = dve.tensor_scalar(z[p][:, b, :], y[p][:, b, :], mv[p][:, b, 0:1],
                                             rstd[p][:, b:b + 1], ALU.subtract, ALU.mult)
                last.then_inc(z_done, 1)

            add_bias(0, 0)
            with dve.Fori(0, NG // 2 - 1) as k:
                for p in range(2):
                    moments(k, p)
                    add_bias(k + p, 1 - p)
                    normalize(k, p)
            moments(NG // 2 - 1, 0)
            add_bias(NG // 2 - 1, 1)
            normalize(NG // 2 - 1, 0)
            moments(NG // 2 - 1, 1)
            normalize(NG // 2 - 1, 1)


def stage_attention(T):
    nc, t, sem = T.nc, T.t, T.sem
    HALF = NH // 2
    NHF = 2 * GB
    with ExitStack() as ctx:
        def sb(name, shape, dt=F32):
            return ctx.enter_context(nc.sbuf_tensor(name, shape, dt))

        def ps(name, shape, dt=F32):
            return ctx.enter_context(nc.psum_tensor(name, shape, dt))

        w_qkvT = sb("at_w_qkvT", [D, 3, D])
        w_aggT = sb("at_w_aggT", [D, D])
        b_agg = sb("at_b_agg", [L, D])
        head_mask = T.head_mask
        pick = sb("at_pick", [GB * 2 * NH, GB, NH, L], BF16)
        stats = sb("at_stats", [L, GB, 6])
        mv = sb("at_mv", [L, GB, 2])
        var_eps = sb("at_var_eps", [L, GB])
        rstd = sb("at_rstd", [L, GB])
        z = [sb(f"at_z{p}", [L, GB, D]) for p in range(2)]
        zT = [sb(f"at_zT{p}", [D, GB, L]) for p in range(2)]
        q_sb = [sb(f"at_q{p}", [D, GB, L]) for p in range(2)]
        k_sb = sb("at_k", [D, GB, L])
        k_heads = [sb(f"at_k_heads{p}", [D, NH, GB, L]) for p in range(2)]
        v_ones = [sb(f"at_v_ones{p}", [L, GB, NH, DH + 1]) for p in range(2)]
        top = sb("at_top", [L, GB, NH])
        neg_top = sb("at_neg_top", [L, GB, 2, NH], BF16)
        neg_topT = sb("at_neg_topT", [GB * 2 * NH, L], BF16)
        probsT = [sb(f"at_probsT{i}", [L, HALF, L]) for i in range(2)]
        inv_sum = sb("at_inv_sum", [L, GB, NH])
        heads_out = sb("at_heads_out", [L, GB, D])
        heads_outT = sb("at_heads_outT", [D, GB, L])
        p_s = [ps(f"at_p_s{i}", [128, 512]) for i in range(2)]
        p_st = [ps(f"at_p_st{i}", [L, HALF, L]) for i in range(2)]
        p_o = [ps(f"at_p_o{i}", [L, 2, NH, DH + 1]) for i in range(2)]
        p_agg = ps("at_p_agg", [128, 512])
        p_q = ps("at_p_q", [128, 512])

        def tokens(bank, rows=L):
            return bank[0:rows, :].rearrange("p (b d) -> p b d", b=GB)

        def features(bank):
            return bank[:, 0:GT].rearrange("p (b l) -> p b l", b=GB)

        neg_topT_ps = p_s[0][:, :].bitcast(BF16)[0:GB * 2 * NH, 0:L]

        weights_in = sem("at_weights_in")
        pool_consts = sem("at_pool_consts")
        stats_done = sem("at_stats_done")
        mv_done = sem("at_mv_done")
        eps_added = sem("at_eps_added")
        rstd_done = sem("at_rstd_done")
        z_done = sem("at_z_done")
        zT_made = sem("at_zT_made")
        zT_kept = sem("at_zT_kept")
        q_made = sem("at_q_made")
        k_made = sem("at_k_made")
        v_made = sem("at_v_made")
        q_kept = sem("at_q_kept")
        k_kept = sem("at_k_kept")
        v_kept = sem("at_v_kept")
        k_masked = sem("at_k_masked")
        bias_added = sem("at_bias_added")
        s_made = sem("at_s_made")
        top_done = sem("at_top_done")
        neg_hi = sem("at_neg_hi")
        neg_lo = sem("at_neg_lo")
        negT_made = sem("at_negT_made")
        negT_kept = sem("at_negT_kept")
        st_made = sem("at_st_made")
        exp_done = sem("at_exp_done")
        pv_done = sem("at_pv_done")
        inv_done = sem("at_inv_done")
        out_done = sem("at_out_done")
        outT_made = sem("at_outT_made")
        outT_kept = sem("at_outT_kept")
        agg_made = sem("at_agg_made")
        h_done = sem("at_h_done")

        block = ctx.enter_context(nc.Block())

        @block.sync
        def _(sp):
            T.clear_old(sp)
            sp.dma_start(w_qkvT[:], t["w_qkvT"].rearrange("d (j e) -> d j e", j=3)).then_inc(weights_in, 16)
            sp.dma_start(w_aggT[:], t["w_aggT"]).then_inc(weights_in, 16)
            sp.dma_start(b_agg[:], t["b_agg"].partition_broadcast(L)).then_inc(weights_in, 16)

        @block.gpsimd
        def _(pool):
            pool.memset(head_mask[:], 1.0).then_inc(pool_consts, 1)
            pool.memset(pick[:], 0.0).then_inc(pool_consts, 1)
            pool.wait_ge(pool_consts, 2)
            pool.affine_select(out=head_mask[:], in_=head_mask[:], compare_op=ALU.is_ge, fill=0.0,
                               base=0, pattern=[[-DH, NH]], channel_multiplier=1).then_inc(pool_consts, 1)
            pool.wait_ge(pool_consts, 3)
            pool.affine_select(out=head_mask[:], in_=head_mask[:], compare_op=ALU.is_ge, fill=0.0,
                               base=DH - 1, pattern=[[DH, NH]], channel_multiplier=-1).then_inc(pool_consts, 1)
            for part in range(2):
                pool.wait_ge(pool_consts, 4 + part)
                pool.affine_select(out=pick[:], in_=pick[:], compare_op=ALU.not_equal, fill=1.0,
                                   base=-NH * part, pattern=[[-2 * NH, GB], [-1, NH], [0, L]],
                                   channel_multiplier=1).then_inc(pool_consts, 1)
            pool.wait_ge(pool_consts, 6)

            def rstd_of(g):
                pool.wait_ge(mv_done, GB * (g + 1))
                pool.tensor_tensor(var_eps[:], mv[:, :, 1], T.eps[:], ALU.add).then_inc(eps_added, 1)
                pool.wait_ge(eps_added, g + 1)
                pool.tensor_tensor(rstd[:], var_eps[:], T.neg_half[:], ALU.pow).then_inc(rstd_done, 1)

            def mask_k(g, p):
                T.wait_alone(pool, k_kept, g + 1)
                if at_least(g, 2):
                    T.wait_alone(pool, st_made, NHF * (g - 1))
                for h in range(NH):
                    last = pool.tensor_scalar(k_heads[p][:, h], k_sb[:], head_mask[:, h:h + 1], 1.0, ALU.mult,
                                              ALU.mult)
                last.then_inc(k_masked, 1)

            def add_b_agg(g):
                rows = T.H[:, bass.ds(g * GB, GB), :]
                pool.wait_ge(z_done, g + 1)
                pool.tensor_tensor(rows, rows, over(b_agg[:], GB), ALU.add).then_inc(bias_added, 1)

            pool.wait_ge(weights_in, 48)
            rstd_of(0)
            rstd_of(1)
            mask_k(0, 0)
            add_b_agg(0)

            def turn(g, p):
                if below(g, NG - 2):
                    rstd_of(g + 2)
                if below(g, NG - 1):
                    mask_k(g + 1, 1 - p)
                    add_b_agg(g + 1)

            turn(0, 0)
            with pool.Fori(0, NG // 2 - 2) as k:
                turn(2 * k + 1, 1)
                turn(2 * k + 2, 0)
            turn(NG - 3, 1)
            turn(NG - 2, 0)
            turn(NG - 1, 1)

        @block.tensor
        def _(pe):
            pe.wait_ge(weights_in, 48)
            pe.wait_ge(pool_consts, 6)

            def z_transposes(g, p):
                T.wait_alone(pe, z_done, g + 1)
                if at_least(g, 1):
                    T.wait_alone(pe, q_kept, g)
                for b in range(GB):
                    last = pe.transpose(features(p_q)[:, b, :], z[p][:, b, :], T.ident[0:L, 0:L])
                last.then_inc(zT_made, 1)

            def qkv(g, p):
                pe.wait_ge(zT_kept, g + 1)
                pe.matmul(features(p_q), w_qkvT[:, 0, :], zT[p][:], start=True, stop=True).then_inc(q_made, 1)
                pe.matmul(features(p_s[1]), w_qkvT[:, 1, :], zT[p][:], start=True, stop=True).then_inc(k_made, 1)
                if at_least(g, 1):
                    pe.wait_ge(negT_kept, g)
                for b in range(GB):
                    last = pe.matmul(tokens(p_s[0])[:, b, :], zT[p][:, b, :], w_qkvT[:, 2, :],
                                     start=True, stop=True)
                last.then_inc(v_made, 1)

            def scores(g, p):
                pe.wait_ge(k_masked, g + 1)
                pe.wait_ge(q_kept, g + 1)
                pe.wait_ge(v_kept, g + 1)
                for f in range(NHF):
                    b, half = f // 2, f % 2
                    if f >= 2:
                        pe.wait_ge(top_done, NHF * g + f - 1)
                    pe.matmul(p_s[half][0:L, 0:HALF * L].rearrange("n (h m) -> n h m", h=HALF),
                              q_sb[p][:, b, :], k_heads[p][:, half * HALF:(half + 1) * HALF, b, :],
                              start=True, stop=True).then_inc(s_made, 1)

            def maxima_transpose(g):
                T.wait_alone(pe, neg_lo, g + 1)
                pe.transpose(neg_topT_ps, neg_top[:].rearrange("n b s h -> n (b s h)"),
                             T.ident_bf[0:L, 0:L]).then_inc(negT_made, 1)

            def scoresT_and_values(g, p):
                pe.wait_ge(negT_kept, g + 1)
                if at_least(g, 1):
                    pe.wait_ge(out_done, 2 * g)
                for f in range(NHF + 1):
                    if f < NHF:
                        b, half = f // 2, f % 2
                        if at_least(g, 1) or f >= 2:
                            pe.wait_ge(exp_done, NHF * g + f - 1)
                        for j in range(HALF):
                            h = half * HALF + j
                            pe.matmul(p_st[half][:, j, :], k_heads[p][:, h, b, :], q_sb[p][:, b, :],
                                      start=True, stop=False)
                            last = pe.matmul(p_st[half][:, j, :], pick[:, b, h, :], neg_topT[:],
                                             start=False, stop=True)
                        last.then_inc(st_made, 1)
                    if f >= 1:
                        b, half = (f - 1) // 2, (f - 1) % 2
                        pe.wait_ge(exp_done, NHF * g + f)
                        for j in range(HALF):
                            h = half * HALF + j
                            last = pe.matmul(p_o[b // 2][:, b % 2, h, :], probsT[half][:, j, :],
                                             v_ones[p][:, b, h, :], start=True, stop=True)
                        last.then_inc(pv_done, 1)

            def out_transposes(g):
                T.wait_alone(pe, out_done, 2 * (g + 1))
                if at_least(g, 1):
                    T.wait_alone(pe, h_done, g)
                for b in range(GB):
                    last = pe.transpose(features(p_agg)[:, b, :], heads_out[:, b, :], T.ident[0:L, 0:L])
                last.then_inc(outT_made, 1)

            def aggregate(g):
                pe.wait_ge(outT_kept, g + 1)
                for b in range(GB):
                    last = pe.matmul(tokens(p_agg)[:, b, :], heads_outT[:, b, :], w_aggT[:],
                                     start=True, stop=True)
                last.then_inc(agg_made, 1)

            def turn(g, p):
                first, final = not at_least(g, 1), not below(g, NG - 1)
                scores(g, p)
                if not first:
                    out_transposes(g - 1)
                if not final:
                    z_transposes(g + 1, 1 - p)
                maxima_transpose(g)
                if not first:
                    aggregate(g - 1)
                if not final:
                    qkv(g + 1, 1 - p)
                scoresT_and_values(g, p)

            z_transposes(0, 0)
            qkv(0, 0)
            turn(0, 0)
            with pe.Fori(0, NG // 2 - 1) as k:
                turn(2 * k + 1, 1)
                turn(2 * k + 2, 0)
            turn(NG - 1, 1)
            out_transposes(NG - 1)
            aggregate(NG - 1)

        @block.scalar
        def _(act):
            def keep_qk(g, p):
                act.wait_ge(zT_made, g + 1)
                if at_least(g, 2):
                    act.wait_ge(v_made, g - 1)
                act.copy(zT[p][:], features(p_q)).then_inc(zT_kept, 1)
                act.wait_ge(q_made, g + 1)
                if at_least(g, 2):
                    act.wait_ge(st_made, NHF * (g - 1))
                act.mul(q_sb[p][:], features(p_q), DH ** -0.5).then_inc(q_kept, 1)
                act.wait_ge(k_made, g + 1)
                if at_least(g, 1):
                    act.wait_ge(k_masked, g)
                act.copy(k_sb[:], features(p_s[1])).then_inc(k_kept, 1)

            def keep_outT(g):
                act.wait_ge(outT_made, g + 1)
                if at_least(g, 1):
                    act.wait_ge(agg_made, g)
                act.copy(heads_outT[:], features(p_agg)).then_inc(outT_kept, 1)

            def exponentials(g):
                for f in range(NHF):
                    act.wait_ge(st_made, NHF * g + f + 1)
                    if at_least(g, 1) or f >= 2:
                        act.wait_ge(pv_done, NHF * g + f - 1)
                    act.activation(probsT[f % 2][:], p_st[f % 2][:], ACT.Exp).then_inc(exp_done, 1)

            def turn(g, p):
                if at_least(g, 1):
                    keep_outT(g - 1)
                if below(g, NG - 1):
                    keep_qk(g + 1, 1 - p)
                exponentials(g)

            keep_qk(0, 0)
            turn(0, 0)
            with act.Fori(0, NG // 2 - 1) as k:
                turn(2 * k + 1, 1)
                turn(2 * k + 2, 0)
            turn(NG - 1, 1)
            keep_outT(NG - 1)

        @block.vector
        def _(dve):
            for p in range(2):
                dve.memset(v_ones[p][:], 1.0)

            def norm_in(g, p):
                for b in range(GB):
                    dve.bn_stats(stats[:, b, :], T.H[:, g * GB + b, :]).then_inc(stats_done, 1)
                T.wait_alone(dve, stats_done, GB * (g + 1))
                for b in range(GB):
                    dve.bn_aggr(mv[:, b, :], stats[:, b, :]).then_inc(mv_done, 1)
                T.wait_alone(dve, rstd_done, g + 1)
                if at_least(g, 2):
                    T.wait_alone(dve, zT_made, g - 1)
                for b in range(GB):
                    last = dve.tensor_scalar(z[p][:, b, :], T.H[:, g * GB + b, :], mv[:, b, 0:1],
                                             rstd[:, b:b + 1], ALU.subtract, ALU.mult)
                last.then_inc(z_done, 1)

            def keep_v(g, p):
                dve.wait_ge(v_made, g + 1)
                if at_least(g, 2):
                    dve.wait_ge(pv_done, NHF * (g - 1))
                dve.tensor_copy(v_ones[p][:, :, :, 0:DH],
                                p_s[0][0:L, :].rearrange("p (b h d) -> p b h d", b=GB, h=NH)).then_inc(v_kept, 1)

            def maxima(g):
                for f in range(NHF):
                    b, half = f // 2, f % 2
                    dve.wait_ge(s_made, NHF * g + f + 1)
                    dve.tensor_reduce(top[:, b, half * HALF:(half + 1) * HALF],
                                      p_s[half][0:L, 0:HALF * L].rearrange("n (h m) -> n h m", h=HALF),
                                      AX_X, ALU.max).then_inc(top_done, 1)
                dve.wait_ge(top_done, NHF * (g + 1))
                dve.tensor_scalar(neg_top[:, :, 0, :], top[:], -1.0, None, ALU.mult).then_inc(neg_hi, 1)
                dve.wait_ge(neg_hi, g + 1)
                dve.scalar_tensor_tensor(out=neg_top[:, :, 1, :], in0=top[:], scalar=-1.0,
                                         in1=neg_top[:, :, 0, :], op0=ALU.mult,
                                         op1=ALU.subtract).then_inc(neg_lo, 1)

            def keep_maxima(g):
                dve.wait_ge(negT_made, g + 1)
                dve.tensor_copy(neg_topT[:], neg_topT_ps).then_inc(negT_kept, 1)

            def divide(g):
                for i in range(2):
                    dve.wait_ge(pv_done, NHF * g + 4 * (i + 1))
                    dve.reciprocal(inv_sum[:, 2 * i:2 * i + 2, :], p_o[i][:, :, :, DH]).then_inc(inv_done, 1)
                    dve.wait_ge(inv_done, 2 * g + i + 1)
                    if at_least(g, 1):
                        dve.wait_ge(outT_made, g)
                    dve.tensor_tensor(heads_out[:, 2 * i:2 * i + 2, :].rearrange("n b (h d) -> n b h d", h=NH),
                                      p_o[i][:, :, :, 0:DH], over(inv_sum[:, 2 * i:2 * i + 2, :], DH, 3),
                                      ALU.mult).then_inc(out_done, 1)

            def add_to_h(g):
                dve.wait_ge(agg_made, g + 1)
                dve.wait_ge(bias_added, g + 1)
                rows = T.H[:, bass.ds(g * GB, GB), :]
                dve.tensor_tensor(rows, rows, tokens(p_agg), ALU.add).then_inc(h_done, 1)

            def turn(g, p):
                first, final = not at_least(g, 1), not below(g, NG - 1)
                if not first:
                    divide(g - 1)
                maxima(g)
                keep_maxima(g)
                if not first:
                    add_to_h(g - 1)
                if not final:
                    keep_v(g + 1, 1 - p)
                if below(g, NG - 2):
                    norm_in(g + 2, p)

            norm_in(0, 0)
            norm_in(1, 1)
            keep_v(0, 0)
            turn(0, 0)
            with dve.Fori(0, NG // 2 - 2) as k:
                turn(2 * k + 1, 1)
                turn(2 * k + 2, 0)
            turn(NG - 3, 1)
            turn(NG - 2, 0)
            turn(NG - 1, 1)
            divide(NG - 1)
            add_to_h(NG - 1)


def stage_router_logits(T):
    nc, t, sem = T.nc, T.t, T.sem
    with ExitStack() as ctx:
        def sb(name, shape, dt=F32):
            return ctx.enter_context(nc.sbuf_tensor(name, shape, dt))

        def ps(name, shape, dt=F32):
            return ctx.enter_context(nc.psum_tensor(name, shape, dt))

        w_router = sb("rl_w_router", [D, E])
        stats = sb("rl_stats", [L, GB, 6])
        mv = sb("rl_mv", [L, GB, 2])
        var_eps = sb("rl_var_eps", [L, GB])
        rstd = sb("rl_rstd", [L, GB])
        z = [sb(f"rl_z{p}", [L, GB, D]) for p in range(2)]
        zT = [sb(f"rl_zT{p}", [D, GB, L]) for p in range(2)]
        logits = [sb(f"rl_logits{p}", [E, GT]) for p in range(2)]
        p_zT = [ps(f"rl_p_zT{p}", [D, GB, L]) for p in range(2)]
        p_logits = [ps(f"rl_p_logits{p}", [E, GT]) for p in range(2)]

        weights_in = sem("rl_weights_in")
        stats_done = sem("rl_stats_done")
        mv_done = sem("rl_mv_done")
        eps_added = sem("rl_eps_added")
        rstd_done = sem("rl_rstd_done")
        z_done = sem("rl_z_done")
        z_stored = [sem(f"rl_z_stored{p}") for p in range(2)]
        zT_made = sem("rl_zT_made")
        zT_kept = sem("rl_zT_kept")
        logits_made = sem("rl_logits_made")
        logits_kept = sem("rl_logits_kept")
        logits_stored = [sem(f"rl_logits_stored{p}") for p in range(2)]
        h_stored = sem("rl_h_stored")

        block = ctx.enter_context(nc.Block())

        @block.sync
        def _(sp):
            T.clear_old(sp)
            sp.dma_start(w_router[:], t["w_router"]).then_inc(weights_in, 16)
            sp.dma_start(T.h_rows.rearrange("(b l) d -> l b d", l=L), T.H[:]).then_inc(h_stored, 16)
            z_rows = T.z_rows.rearrange("(b l) c -> l b c", l=L)
            with sp.Fori(0, NG // 2) as k:
                for p in range(2):
                    g = 2 * k + p
                    sp.wait_ge(z_done, g + 1)
                    sp.dma_start(z_rows[:, bass.ds(g * GB, GB), 0:D], z[p][:]).then_inc(z_stored[p], 16)
                    sp.wait_ge(logits_kept, g + 1)
                    sp.dma_start(T.logits[:, bass.ds(g * GT, GT)], logits[p][:]).then_inc(logits_stored[p], 16)
            sp.wait_ge(h_stored, 16)
            for p in range(2):
                sp.wait_ge(z_stored[p], 16 * (NG // 2))
                sp.wait_ge(logits_stored[p], 16 * (NG // 2))

        @block.gpsimd
        def _(pool):
            with pool.Fori(0, NG) as g:
                pool.wait_ge(mv_done, GB * (g + 1))
                pool.tensor_tensor(var_eps[:], mv[:, :, 1], T.eps[:], ALU.add).then_inc(eps_added, 1)
                pool.wait_ge(eps_added, g + 1)
                pool.tensor_tensor(rstd[:], var_eps[:], T.neg_half[:], ALU.pow).then_inc(rstd_done, 1)

        @block.tensor
        def _(pe):
            pe.wait_ge(weights_in, 16)

            def transposes(g, p):
                T.wait_alone(pe, z_done, g + 1)
                if at_least(g, 2):
                    T.wait_alone(pe, zT_kept, g - 1)
                for b in range(GB):
                    last = pe.transpose(p_zT[p][:, b, :], z[p][:, b, :], T.ident[0:L, 0:L])
                last.then_inc(zT_made, 1)

            def route(g, p):
                T.wait_alone(pe, zT_kept, g + 1)
                if at_least(g, 2):
                    T.wait_alone(pe, logits_kept, g - 1)
                pe.matmul(p_logits[p][:], w_router[:], zT[p][:], start=True, stop=True).then_inc(logits_made, 1)

            transposes(0, 0)
            transposes(1, 1)
            route(0, 0)
            with pe.Fori(1, NG // 2) as k:
                transposes(2 * k, 0)
                route(2 * k - 1, 1)
                transposes(2 * k + 1, 1)
                route(2 * k, 0)
            route(NG - 1, 1)

        @block.scalar
        def _(act):
            with act.Fori(0, NG // 2) as k:
                for p in range(2):
                    act.wait_ge(zT_made, 2 * k + p + 1)
                    act.wait_ge(logits_made, 2 * k + p + 1)
                    act.copy(zT[p][:], p_zT[p][:]).then_inc(zT_kept, 1)

        @block.vector
        def _(dve):
            dve.sem_inc(logits_made, 2)

            def norm(g, p, w):
                for b in range(GB):
                    dve.bn_stats(stats[:, b, :], T.H[:, g * GB + b, :]).then_inc(stats_done, 1)
                T.wait_alone(dve, stats_done, GB * (g + 1))
                for b in range(GB):
                    dve.bn_aggr(mv[:, b, :], stats[:, b, :]).then_inc(mv_done, 1)
                T.wait_alone(dve, rstd_done, g + 1)
                if at_least(g, 2):
                    T.wait_alone(dve, zT_made, g - 1)
                    T.wait_alone(dve, z_stored[p], 16 * w)
                for b in range(GB):
                    last = dve.tensor_scalar(z[p][:, b, :], T.H[:, g * GB + b, :], mv[:, b, 0:1],
                                             rstd[:, b:b + 1], ALU.subtract, ALU.mult)
                last.then_inc(z_done, 1)

            def keep_logits(g, p, w):
                dve.wait_ge(logits_made, g + 3)
                if at_least(g, 2):
                    dve.wait_ge(logits_stored[p], 16 * w)
                dve.tensor_copy(logits[p][:], p_logits[p][:]).then_inc(logits_kept, 1)

            norm(0, 0, 0)
            norm(1, 1, 0)
            keep_logits(0, 0, 0)
            norm(2, 0, 1)
            keep_logits(1, 1, 0)
            norm(3, 1, 1)
            with dve.Fori(2, NG // 2) as k:
                keep_logits(2 * k - 2, 0, k - 1)
                norm(2 * k, 0, k)
                keep_logits(2 * k - 1, 1, k - 1)
                norm(2 * k + 1, 1, k)
            keep_logits(NG - 2, 0, NG // 2 - 1)
            keep_logits(NG - 1, 1, NG // 2 - 1)


def stage_choose(T):
    nc, t, sem = T.nc, T.t, T.sem
    R = 128 // E
    C = N // R
    assert C == GT
    LO = 32
    HI = CAP // LO
    tiles = E * CAP // 128
    PB = 8
    NCH = B // PB
    with ExitStack() as ctx:
        def sb(name, shape, dt=F32):
            return ctx.enter_context(nc.sbuf_tensor(name, shape, dt))

        def ps(name, shape, dt=F32):
            return ctx.enter_context(nc.psum_tensor(name, shape, dt))

        logit = sb("ch_logit", [128, C])
        u = sb("ch_u", [128, C])
        weight = sb("ch_weight", [128, C])
        same = sb("ch_same", [128, 128])
        before = sb("ch_before", [128, 128])
        ones = sb("ch_ones", [128, C])
        scratch = sb("ch_scratch", [128, C])
        lower = sb("ch_lower", [128, C])
        equal = sb("ch_equal", [128, C])
        tied = sb("ch_tied", [128, C])
        taken = sb("ch_taken", [128, C])
        count = sb("ch_count", [128, C])
        slot = sb("ch_slot", [128, C])
        row_max = sb("ch_row_max", [128, 1])
        max_e = sb("ch_max_e", [1, E])
        max_row = sb("ch_max_row", [1, E, R])
        top = sb("ch_top", [128, 1])
        row_sum = sb("ch_row_sum", [128, 1])
        inv_sum = sb("ch_inv_sum", [128, 1])
        kth = sb("ch_kth", [128, 1], I32)
        bit = sb("ch_bit", [128, 1])
        bit_int = sb("ch_bit_int", [128, 1], I32)
        trial = sb("ch_trial", [128, 1], I32)
        gain = sb("ch_gain", [128, 1], I32)
        row_count = sb("ch_row_count", [128, 1])
        tie_room = sb("ch_tie_room", [128, 1])
        ahead = sb("ch_ahead", [128, 2])
        weightT = sb("ch_weightT", [L, B, E])
        slot_int = sb("ch_slot_int", [L, GB, 128], I32)
        hi_int = sb("ch_hi_int", [L, GB, 128], I32)
        lo_int = sb("ch_lo_int", [L, GB, 128], I32)
        hi = sb("ch_hi", [L, B, E], BF16)
        lo = sb("ch_lo", [L, B, E], BF16)
        iota = sb("ch_iota", [L, LO], BF16)
        iota_int = sb("ch_iota_int", [L, LO], I32)
        seq_no = sb("ch_seq_no", [L, B, E], BF16)
        seq_no_int = sb("ch_seq_no_int", [L, B, E], I32)
        tok_no = sb("ch_tok_no", [L, 1])
        tok_no_int = sb("ch_tok_no_int", [L, 1], I32)
        hot_hi = [sb(f"ch_hot_hi{p}", [L, PB * E, HI], BF16) for p in range(2)]
        hot_lo = [sb(f"ch_hot_lo{p}", [L, PB * E, LO], BF16) for p in range(2)]
        numbers = [sb(f"ch_numbers{p}", [L, PB * E, 2, LO], BF16) for p in range(2)]
        zeros = sb("ch_zeros", [L, 2 * LO], BF16)
        rows_f = sb("ch_rows_f", [128, E // 4, LO])
        rows_t = sb("ch_rows_t", [tiles, 128])
        p_small = ps("ch_p_small", [128, 512])
        p_tot = ps("ch_p_tot", [128, 1])
        p_slot = ps("ch_p_slot", [L, GB, 128])
        p_weight = ps("ch_p_weight", [L, GB, 128])
        p_chosen = ps("ch_p_chosen", [128, tiles])
        p_rows = [ps(f"ch_p_rows{i}", [128, 2, LO]) for i in range(E // 4)]

        loaded = sem("ch_loaded")
        consts = sem("ch_consts")
        small = sem("ch_small")
        max_made = sem("ch_max_made")
        max_spread = sem("ch_max_spread")
        u_done = sem("ch_u_done")
        exp_done = sem("ch_exp_done")
        sum_made = sem("ch_sum_made")
        weight_done = sem("ch_weight_done")
        trial_done = sem("ch_trial_done")
        counted = sem("ch_counted")
        total_made = sem("ch_total_made")
        gain_done = sem("ch_gain_done")
        kth_done = sem("ch_kth_done")
        bit_done = sem("ch_bit_done")
        marked = sem("ch_marked")
        offsets_made = sem("ch_offsets_made")
        slot_done = sem("ch_slot_done")
        turned = sem("ch_turned")
        weightT_kept = sem("ch_weightT_kept")
        parts_done = sem("ch_parts_done")
        hot_done = sem("ch_hot_done")
        lo_hot_done = sem("ch_lo_hot_done")
        tok_numbered = sem("ch_tok_numbered")
        seq_numbered = sem("ch_seq_numbered")
        chunk_used = sem("ch_chunk_used")
        rows_made = sem("ch_rows_made")
        rows_out = sem("ch_rows_out")
        rows_back = sem("ch_rows_back")
        rows_turned = sem("ch_rows_turned")
        chosen_done = sem("ch_chosen_done")
        weights_stored = sem("ch_weights_stored")

        block = ctx.enter_context(nc.Block())

        @block.sync
        def _(sp):
            T.clear_old(sp)
            sp.dma_start(logit[:], T.logits.rearrange("e (r c) -> (e r) c", r=R)).then_inc(loaded, 16)
            sp.wait_ge(weightT_kept, 1)
            sp.dma_start(T.z_rows.rearrange("(b l) c -> l b c", l=L)[:, :, D:D + E],
                         weightT[:]).then_inc(weights_stored, 16)
            sp.wait_ge(slot_done, 1 + E // 4)
            sp.dma_start(T.chosen_rows.rearrange("(g p c) -> p g c", p=128, c=LO), rows_f[:]).then_inc(rows_out, 16)
            sp.wait_ge(rows_out, 16)
            sp.dma_start(rows_t[:], T.chosen_rows.rearrange("(t p) -> t p", p=128)).then_inc(rows_back, 16)
            sp.wait_ge(weights_stored, 16)

        @block.gpsimd
        def _(pool):
            pool.memset(same[:], 1.0).then_inc(consts, 1)
            pool.wait_ge(consts, 1)
            sameb = same[:].rearrange("p (e r) -> p e r", e=E)
            pool.affine_select(out=sameb, in_=sameb, compare_op=ALU.is_ge, fill=0.0, base=0,
                               pattern=[[-R, E], [0, R]], channel_multiplier=1).then_inc(consts, 1)
            pool.wait_ge(consts, 2)
            pool.affine_select(out=sameb, in_=sameb, compare_op=ALU.is_ge, fill=0.0, base=R - 1,
                               pattern=[[R, E], [0, R]], channel_multiplier=-1).then_inc(consts, 1)
            pool.wait_ge(consts, 3)
            pool.affine_select(out=before[:], in_=same[:], compare_op=ALU.is_gt, fill=0.0, base=0,
                               pattern=[[1, 128]], channel_multiplier=-1).then_inc(consts, 1)
            pool.iota(iota_int[:], pattern=[[1, LO]], base=0, channel_multiplier=0).then_inc(consts, 1)
            pool.iota(seq_no_int[:], pattern=[[1, B], [0, E]], base=0, channel_multiplier=0).then_inc(consts, 1)
            pool.iota(tok_no_int[:], pattern=[[0, 1]], base=0, channel_multiplier=1).then_inc(consts, 1)
            pool.memset(zeros[:], 0.0)
            pool.wait_ge(consts, 7)
            pool.tensor_copy(iota[:], iota_int[:]).then_inc(consts, 1)
            pool.tensor_copy(seq_no[:], seq_no_int[:]).then_inc(consts, 1)
            pool.tensor_copy(tok_no[:], tok_no_int[:]).then_inc(consts, 1)
            pool.wait_ge(consts, 10)

            def number_sequences(c, p):
                T.wait_alone(pool, lo_hot_done, c + 1)
                T.wait_alone(pool, chunk_used, c + 1)
                pool.tensor_tensor(numbers[p][:, :, 1, :], hot_lo[p][:],
                                   over(seq_no[:, bass.ds(c * PB, PB), :].rearrange("l b e -> l (b e)"), LO, 2),
                                   ALU.mult).then_inc(seq_numbered, 1)

            with pool.Fori(0, NCH // 2) as k:
                for p in range(2):
                    number_sequences(2 * k + p, p)

        @block.tensor
        def _(pe):
            pe.wait_ge(small, 1)
            pe.matmul(p_small[0:1, 0:128], row_max[:], T.ident[:], start=True, stop=True).then_inc(max_made, 1)
            pe.wait_ge(small, 3)
            pe.matmul(p_small[:, 128:129], max_row[:].rearrange("o e r -> o (e r)"), ones[0:1, 0:1],
                      start=True, stop=True).then_inc(max_spread, 1)
            pe.wait_ge(consts, 10)
            pe.wait_ge(exp_done, 1)
            pe.matmul(p_small[:, 129:130], same[:], row_sum[:], start=True, stop=True).then_inc(sum_made, 1)
            with pe.Fori(0, 31) as i:
                T.wait_alone(pe, counted, i + 1)
                pe.matmul(p_tot[:], same[:], row_count[:], start=True, stop=True).then_inc(total_made, 1)
            pe.wait_ge(marked, 1)
            pe.matmul(p_tot[:], same[:], row_count[:], start=True, stop=True).then_inc(offsets_made, 1)
            pe.wait_ge(marked, 3)
            pe.matmul(p_small[:, 130:131], before[:], count[:, C - 1:C], start=True, stop=True).then_inc(offsets_made, 1)
            pe.wait_ge(weight_done, 1)
            for i in range(GB):
                last = pe.transpose(p_weight[:, i, :], weight[:, i * L:(i + 1) * L], T.ident[:])
            last.then_inc(turned, 1)
            pe.wait_ge(marked, 6)
            pe.matmul(p_small[:, 131:132], before[:], count[:, C - 1:C], start=True, stop=True).then_inc(offsets_made, 1)
            pe.wait_ge(slot_done, 1)
            for i in range(GB):
                last = pe.transpose(p_slot[:, i, :], slot[:, i * L:(i + 1) * L], T.ident[:])
            last.then_inc(turned, 1)

            def sums(lhsT, rhs, e, **flags):
                q = e % 4
                return pe.matmul(p_rows[e // 4][HI * q:HI * (q + 1), :, :].rearrange("h s c -> h (s c)"), lhsT, rhs,
                                 skip_group_check=True, **flags)

            for e in range(E):
                sums(zeros[:, 0:HI], zeros[:], e, start=True, stop=False)
            with pe.Fori(0, NCH // 2) as k:
                for p in range(2):
                    c = 2 * k + p
                    T.wait_alone(pe, hot_done, c + 1)
                    T.wait_alone(pe, tok_numbered, c + 1)
                    T.wait_alone(pe, seq_numbered, c + 1)
                    for b in range(PB):
                        for e in range(E):
                            i = b * E + e
                            last = sums(hot_hi[p][:, i, :], numbers[p][:, i, :, :].rearrange("l s c -> l (s c)"), e,
                                        start=False, stop=False)
                    last.then_inc(chunk_used, 1)
            for e in range(E):
                last = sums(zeros[:, 0:HI], zeros[:], e, start=False, stop=True)
            last.then_inc(rows_made, 1)
            pe.wait_ge(rows_back, 16)
            pe.transpose(p_chosen[:], rows_t[:], T.ident[0:tiles, 0:tiles]).then_inc(rows_turned, 1)

        @block.scalar
        def _(act):
            act.wait_ge(u_done, 1)
            act.activation(weight[:], u[:], ACT.Exp, scale=-1.0, accum_out=row_sum[:]).then_inc(exp_done, 1)
            act.wait_ge(consts, 10)

            def number_tokens(c, p):
                act.wait_ge(lo_hot_done, c + 1)
                act.wait_ge(chunk_used, c + 1)
                act.activation(numbers[p][:, :, 0, :], hot_lo[p][:], ACT.Copy, scale=tok_no[:, 0:1]).then_inc(tok_numbered, 1)

            with act.Fori(0, NCH // 2) as k:
                for p in range(2):
                    number_tokens(2 * k + p, p)

        @block.vector
        def _(dve):
            dve.sem_inc(chunk_used, 2)
            dve.memset(ones[:], 1.0).then_inc(bit_done, 1)
            dve.memset(kth[:], 0).then_inc(kth_done, 1)
            dve.memset(bit[:], float(2 ** 30)).then_inc(bit_done, 1)
            dve.wait_ge(bit_done, 2)
            dve.tensor_copy(bit_int[:], bit[:]).then_inc(bit_done, 1)
            dve.wait_ge(loaded, 16)
            dve.tensor_reduce(row_max[:], logit[:], AX_X, ALU.max).then_inc(small, 1)
            dve.wait_ge(max_made, 1)
            dve.tensor_reduce(max_e[:], p_small[0:1, 0:128].rearrange("o (e r) -> o e r", e=E), AX_X,
                              ALU.max).then_inc(small, 1)
            dve.wait_ge(small, 2)
            dve.tensor_copy(max_row[:], over(max_e[:], R, 2)).then_inc(small, 1)
            dve.wait_ge(max_spread, 1)
            dve.tensor_copy(top[:], p_small[:, 128:129]).then_inc(small, 1)
            dve.wait_ge(small, 4)
            dve.tensor_scalar(u[:], logit[:], -1.0, top[:, 0:1], ALU.mult, ALU.add).then_inc(u_done, 1)
            dve.wait_ge(sum_made, 1)
            dve.reciprocal(inv_sum[:], p_small[:, 129:130]).then_inc(small, 1)
            dve.wait_ge(small, 5)
            dve.tensor_scalar(weight[:], weight[:], inv_sum[:, 0:1], None, ALU.mult).then_inc(weight_done, 1)

            with dve.Fori(0, 31) as i:
                dve.wait_ge(bit_done, 2 * i + 3)
                dve.wait_ge(kth_done, i + 1)
                dve.tensor_tensor(trial[:], kth[:], bit_int[:], ALU.bitwise_or).then_inc(trial_done, 1)
                T.wait_alone(dve, trial_done, i + 1)
                dve.tensor_scalar(scratch[:], u[:], trial[:].bitcast(F32), None, ALU.is_lt, ALU.add,
                                  accum_out=row_count[:]).then_inc(counted, 1)
                dve.wait_ge(total_made, i + 1)
                dve.tensor_scalar(gain[:], p_tot[:], CAP - 0.5, bit[:, 0:1], ALU.is_lt, ALU.mult).then_inc(gain_done, 1)
                dve.wait_ge(gain_done, i + 1)
                dve.tensor_tensor(kth[:], kth[:], gain[:], ALU.bitwise_or).then_inc(kth_done, 1)
                dve.tensor_scalar(bit[:], bit[:], 0.5, None, ALU.mult).then_inc(bit_done, 1)
                dve.wait_ge(bit_done, 2 * i + 4)
                dve.tensor_copy(bit_int[:], bit[:]).then_inc(bit_done, 1)

            dve.wait_ge(kth_done, 32)
            kth_f = kth[:].bitcast(F32)
            dve.tensor_scalar(lower[:], u[:], kth_f, None, ALU.is_lt, ALU.add, accum_out=row_count[:]).then_inc(marked, 1)
            dve.tensor_scalar(equal[:], u[:], kth_f, None, ALU.is_equal).then_inc(marked, 1)
            dve.wait_ge(marked, 2)
            dve.tensor_tensor_scan(count[:], ones[:], equal[:], 0.0, ALU.mult, ALU.add).then_inc(marked, 1)
            dve.wait_ge(offsets_made, 2)
            dve.tensor_copy(ahead[:, 0:1], p_small[:, 130:131]).then_inc(marked, 1)
            dve.wait_ge(marked, 4)
            dve.tensor_tensor(tie_room[:], p_tot[:], ahead[:, 0:1], ALU.add).then_inc(small, 1)
            dve.wait_ge(small, 6)
            dve.tensor_scalar(tie_room[:], tie_room[:], -1.0, float(CAP), ALU.mult, ALU.add).then_inc(small, 1)
            dve.wait_ge(small, 7)
            dve.scalar_tensor_tensor(out=tied[:], in0=count[:], scalar=tie_room[:, 0:1], in1=equal[:],
                                     op0=ALU.is_le, op1=ALU.mult).then_inc(small, 1)
            dve.wait_ge(small, 8)
            dve.tensor_tensor(taken[:], lower[:], tied[:], ALU.add).then_inc(marked, 1)
            dve.wait_ge(marked, 5)
            dve.tensor_tensor_scan(count[:], ones[:], taken[:], 0.0, ALU.mult, ALU.add).then_inc(marked, 1)
            dve.wait_ge(offsets_made, 3)
            dve.tensor_copy(ahead[:, 1:2], p_small[:, 131:132]).then_inc(marked, 1)
            dve.wait_ge(marked, 7)
            dve.scalar_tensor_tensor(out=slot[:], in0=count[:], scalar=ahead[:, 1:2], in1=taken[:],
                                     op0=ALU.add, op1=ALU.mult).then_inc(marked, 1)
            dve.wait_ge(marked, 8)
            dve.tensor_scalar(slot[:], slot[:], -1.0, None, ALU.add).then_inc(slot_done, 1)
            dve.wait_ge(turned, 1)

            def by_sequence(tile):
                return tile[:].rearrange("l (r i) e -> l i e r", i=GB)

            def by_group(tile):
                return tile.rearrange("l i (e r) -> l i e r", e=E)

            dve.tensor_copy(by_sequence(weightT), by_group(p_weight[:])).then_inc(weightT_kept, 1)
            dve.wait_ge(turned, 2)
            dve.tensor_copy(slot_int[:], p_slot[:]).then_inc(parts_done, 1)
            dve.wait_ge(parts_done, 1)
            dve.tensor_scalar(hi_int[:], slot_int[:], 5, None, ALU.arith_shift_right).then_inc(parts_done, 1)
            dve.tensor_scalar(lo_int[:], slot_int[:], LO - 1, None, ALU.bitwise_and).then_inc(parts_done, 1)
            dve.wait_ge(parts_done, 3)
            dve.tensor_copy(by_sequence(hi), by_group(hi_int[:])).then_inc(parts_done, 1)
            dve.tensor_copy(by_sequence(lo), by_group(lo_int[:])).then_inc(parts_done, 1)
            dve.wait_ge(parts_done, 5)
            dve.wait_ge(consts, 10)

            def one_hot(c, p):
                T.wait_alone(dve, chunk_used, c + 1)
                pairs = PB * E

                def of(x):
                    return over(x[:, bass.ds(c * PB, PB), :].rearrange("l b e -> l (b e)"), LO, 2)

                dve.tensor_tensor(hot_lo[p][:], over(iota[:], pairs), of(lo), ALU.is_equal).then_inc(lo_hot_done, 1)
                dve.tensor_tensor(hot_hi[p][:], over(iota[:], pairs), of(hi), ALU.is_equal).then_inc(hot_done, 1)

            with dve.Fori(0, NCH // 2) as k:
                for p in range(2):
                    one_hot(2 * k + p, p)
            dve.wait_ge(rows_made, 1)
            for i in range(E // 4):
                dve.tensor_copy(rows_f[:, i, :], p_rows[i][:, 0, :]).then_inc(marked, 1)
                dve.wait_ge(marked, 9 + i)
                dve.scalar_tensor_tensor(out=rows_f[:, i, :], in0=p_rows[i][:, 1, :], scalar=float(L),
                                         in1=rows_f[:, i, :], op0=ALU.mult, op1=ALU.add).then_inc(slot_done, 1)
            dve.wait_ge(rows_turned, 1)
            dve.tensor_copy(T.chosen[:], p_chosen[:]).then_inc(chosen_done, 1)


def stage_expert_choice(T):
    nc, t, sem = T.nc, T.t, T.sem
    ET = CAP // 128
    HT = ET // 2
    FC = F // 128
    HS = HT * 128
    with ExitStack() as ctx:
        def sb(name, shape, dt=F32):
            return ctx.enter_context(nc.sbuf_tensor(name, shape, dt))

        def ps(name, shape, dt=F32):
            return ctx.enter_context(nc.psum_tensor(name, shape, dt))

        w1 = [sb(f"ec_w1{p}", [D, F]) for p in range(2)]
        w2 = [sb(f"ec_w2{p}", [128, FC, D]) for p in range(2)]
        b1 = sb("ec_b1", [128, E, FC])
        b1_now = [sb(f"ec_b1_now{p}", [128, FC]) for p in range(2)]
        b2 = sb("ec_b2", [128, E, D])
        rows_in = [sb(f"ec_rows_in{p}", [128, ET], I32) for p in range(2)]
        rows_out = sb("ec_rows_out", [128, ET], I32)
        x = [sb(f"ec_x{p}", [128, ET, D + E]) for p in range(2)]
        weight = [sb(f"ec_weight{p}", [128, ET]) for p in range(2)]
        xT = [sb(f"ec_xT{s}", [D, HT, 128]) for s in range(2)]
        hidden = [sb(f"ec_hidden{s}", [128, FC, HS]) for s in range(2)]
        plus_b2 = sb("ec_plus_b2", [128, HT, D])
        y = [sb(f"ec_y{p}", [128, ET, D]) for p in range(2)]
        p_xT = ps("ec_p_xT", [D, HT, 128])
        p_hidden = [ps(f"ec_p_hidden{c}", [128, HS]) for c in range(FC)]
        p_y = [ps(f"ec_p_y{s}", [128, HT, D]) for s in range(2)]

        biases_in = sem("ec_biases_in")
        weights_in = [sem(f"ec_weights_in{p}") for p in range(2)]
        rows_in_set = sem("ec_rows_in_set")
        rows_out_set = sem("ec_rows_out_set")
        gathered = [sem(f"ec_gathered{p}") for p in range(2)]
        weight_set = sem("ec_weight_set")
        xT_made = sem("ec_xT_made")
        xT_kept = sem("ec_xT_kept")
        hidden_made = sem("ec_hidden_made")
        gelu_done = sem("ec_gelu_done")
        y_made = sem("ec_y_made")
        b2_added = sem("ec_b2_added")
        y_done = sem("ec_y_done")
        added = [sem(f"ec_added{p}") for p in range(2)]
        h_back = sem("ec_h_back")

        block = ctx.enter_context(nc.Block())


        @block.sync
        def _(sp):
            T.clear_old(sp)
            sp.dma_start(b1[:], t["e_b1"]).then_inc(biases_in, 16)
            sp.dma_start(b2[:], t["e_b2"].rearrange("e d -> (e d)").partition_broadcast(128)).then_inc(biases_in, 16)

            def load(w, p):
                e = 2 * w + p
                sp.dma_start(w1[p][:], t["e_w1"][bass.ds(e * D, D), :]).then_inc(weights_in[p], 16)
                sp.dma_start(w2[p][:], t["e_w2"][bass.ds(e * F, F), :].rearrange("(c k) d -> k c d", k=128)
                             ).then_inc(weights_in[p], 16)

            load(0, 0)
            load(0, 1)
            with sp.Fori(1, E // 2) as w:
                for p in range(2):
                    sp.wait_ge(y_made, 2 * (2 * w + p - 1))
                    load(w, p)
            for p in range(2):
                sp.wait_ge(added[p], 16 * ET * (E // 2))
            sp.dma_start(T.H[:], T.h_rows.rearrange("(b l) d -> l b d", l=L)).then_inc(h_back, 16)
            sp.wait_ge(h_back, 16)

        @block.gpsimd
        def _(pool):
            def gather(w, p):
                e = 2 * w + p
                if at_least(w, 1):
                    T.wait_alone(pool, xT_made, 2 * (e - 1))
                    T.wait_alone(pool, weight_set, e - 1)
                pool.tensor_copy(rows_in[p][:], T.chosen[:, bass.ds(e * ET, ET)]).then_inc(rows_in_set, 1)
                T.wait_alone(pool, rows_in_set, e + 1)
                for s in range(ET):
                    pool.indirect_dma_start(out=x[p][:, s, :], out_offset=None, in_=T.z_rows,
                                            in_offset=bass.IndirectOffsetOnAxis(ap=rows_in[p][:, s:s + 1], axis=0)
                                            ).then_inc(gathered[p], 16)

            def add(w, p):
                e = 2 * w + p
                T.wait_alone(pool, y_done, 2 * e + 2)
                if at_least(w, 1) or p == 1:
                    T.wait_alone(pool, added[1 - p], 16 * ET * (w + p))
                pool.tensor_copy(rows_out[:], T.chosen[:, bass.ds(e * ET, ET)]).then_inc(rows_out_set, 1)
                T.wait_alone(pool, rows_out_set, e + 1)
                for s in range(ET):
                    pool.indirect_dma_start(out=T.h_rows,
                                            out_offset=bass.IndirectOffsetOnAxis(ap=rows_out[:, s:s + 1], axis=0),
                                            in_=y[p][:, s, :], in_offset=None,
                                            compute_op=ALU.add).then_inc(added[p], 16)

            gather(0, 0)
            gather(0, 1)
            with pool.Fori(0, E // 2 - 1) as w:
                for p in range(2):
                    gather(w + 1, p)
                    add(w, p)
            add(E // 2 - 1, 0)
            add(E // 2 - 1, 1)

        @block.tensor
        def _(pe):
            def transposes(w, p, s):
                u = 4 * w + 2 * p + s
                T.wait_alone(pe, gathered[p], 16 * ET * (w + 1))
                if at_least(w, 1) or p + s > 0:
                    T.wait_alone(pe, xT_kept, u)
                for i in range(HT):
                    last = pe.transpose(p_xT[:, i, :], x[p][:, s * HT + i, 0:D], T.ident[:])
                last.then_inc(xT_made, 1)

            def into_hidden(w, p, s):
                u = 4 * w + 2 * p + s
                T.wait_alone(pe, weights_in[p], 32 * (w + 1))
                T.wait_alone(pe, xT_kept, u + 1)
                for c in range(FC):
                    if at_least(w, 1) or p + s > 0:
                        pe.wait_ge(gelu_done, FC * (u - 1) + c + 1)
                    pe.matmul(p_hidden[c][:], w1[p][:, c * 128:(c + 1) * 128],
                              xT[s][:].rearrange("d i n -> d (i n)"), start=True, stop=True).then_inc(hidden_made, 1)

            def out_of_hidden(w, p, s):
                u = 4 * w + 2 * p + s
                T.wait_alone(pe, gelu_done, FC * (u + 1))
                if at_least(w, 1) or p > 0:
                    T.wait_alone(pe, b2_added, u - 1)
                for i in range(HT):
                    for c in range(FC):
                        last = pe.matmul(p_y[s][:, i, :], hidden[s][:, c, i * 128:(i + 1) * 128], w2[p][:, c, :],
                                         start=(c == 0), stop=(c == FC - 1))
                last.then_inc(y_made, 1)

            transposes(0, 0, 0)
            transposes(0, 0, 1)
            into_hidden(0, 0, 0)

            def steps(w, p):
                transposes(w + p, 1 - p, 0)
                into_hidden(w, p, 1)
                out_of_hidden(w, p, 0)
                transposes(w + p, 1 - p, 1)
                into_hidden(w + p, 1 - p, 0)
                out_of_hidden(w, p, 1)

            steps(0, 0)
            with pe.Fori(0, E // 2 - 1) as w:
                steps(w, 1)
                steps(w + 1, 0)
            into_hidden(E // 2 - 1, 1, 1)
            out_of_hidden(E // 2 - 1, 1, 0)
            out_of_hidden(E // 2 - 1, 1, 1)

        @block.scalar
        def _(act):
            def gelus(w, p, s):
                u = 4 * w + 2 * p + s
                if at_least(w, 1) or p > 0:
                    T.wait_alone(act, y_made, u - 1)
                for c in range(FC):
                    act.wait_ge(hidden_made, FC * u + c + 1)
                    act.activation(hidden[s][:, c, :], p_hidden[c][:], ACT.Gelu,
                                   bias=b1_now[p][:, c:c + 1]).then_inc(gelu_done, 1)

            def expert(w, p):
                T.wait_alone(act, weight_set, 2 * w + p + 1)
                gelus(w, p, 0)
                gelus(w, p, 1)

            expert(0, 0)
            expert(0, 1)
            with act.Fori(1, E // 2) as w:
                expert(w, 0)
                expert(w, 1)

        @block.vector
        def _(dve):
            def take_weights(w, p):
                e = 2 * w + p
                T.wait_alone(dve, gathered[p], 16 * ET * (w + 1))
                if at_least(w, 1):
                    T.wait_alone(dve, gelu_done, 2 * FC * (e - 1))
                    T.wait_alone(dve, y_done, 2 * (e - 1))
                dve.tensor_copy(weight[p][:], x[p][:, :, bass.ds(D + e, 1)].rearrange("n s o -> n (s o)"))
                dve.tensor_copy(b1_now[p][:], b1[:, bass.ds(e, 1), :].rearrange("n o c -> n (o c)")
                                ).then_inc(weight_set, 1)

            def keep_xT(w, p, s):
                u = 4 * w + 2 * p + s
                T.wait_alone(dve, xT_made, u + 1)
                if at_least(w, 1) or p > 0:
                    T.wait_alone(dve, hidden_made, FC * (u - 1))
                dve.tensor_copy(xT[s][:], p_xT[:]).then_inc(xT_kept, 1)

            def weigh(w, p, s):
                e, u = 2 * w + p, 4 * w + 2 * p + s
                T.wait_alone(dve, y_made, u + 1)
                if at_least(w, 1) or p + s > 0:
                    T.wait_alone(dve, y_done, u)
                if at_least(w, 1):
                    T.wait_alone(dve, added[p], 16 * ET * w)
                dve.tensor_tensor(plus_b2[:], p_y[s][:],
                                  over(b2[:, bass.ds(e, 1), :].rearrange("n o d -> n (o d)"), HT),
                                  ALU.add).then_inc(b2_added, 1)
                T.wait_alone(dve, b2_added, u + 1)
                dve.tensor_tensor(y[p][:, s * HT:(s + 1) * HT, :], plus_b2[:],
                                  over(weight[p][:, s * HT:(s + 1) * HT], D, 2), ALU.mult).then_inc(y_done, 1)

            def steps(w, p):
                take_weights(w + p, 1 - p)
                keep_xT(w + p, 1 - p, 0)
                weigh(w, p, 0)
                keep_xT(w + p, 1 - p, 1)
                weigh(w, p, 1)

            dve.wait_ge(biases_in, 32)
            take_weights(0, 0)
            keep_xT(0, 0, 0)
            keep_xT(0, 0, 1)
            steps(0, 0)
            with dve.Fori(0, E // 2 - 1) as w:
                steps(w, 1)
                steps(w + 1, 0)
            weigh(E // 2 - 1, 1, 0)
            weigh(E // 2 - 1, 1, 1)


def stage_offset_attention(T):
    nc, t, sem = T.nc, T.t, T.sem
    NO = len(OFFS)
    BH = GB * NH
    NLOC = OFF_LOCAL + 1
    PAD = OFFS[-1]
    CHUNK = 16
    NCH = (NO + CHUNK - 1) // CHUNK
    LAST = NO - CHUNK * (NCH - 1)
    UNITS = [("dve", 0, 0), ("dve", 0, 1), ("dve", 0, 2), ("pool", 0, 3),
             ("dve", 1, 0), ("dve", 1, 1), ("pool", 1, 2), ("pool", 1, 3), ("pool", 2, 0)]
    NU = len(UNITS)
    SLOT = {u: sum(v[0] == UNITS[u][0] for v in UNITS[:u]) for u in range(NU)}
    NDVE, NPOOL = (sum(v[0] == who for v in UNITS) for who in ("dve", "pool"))
    with ExitStack() as ctx:
        def sb(name, shape, dt=F32):
            return ctx.enter_context(nc.sbuf_tensor(name, shape, dt))

        def ps(name, shape, dt=F32):
            return ctx.enter_context(nc.psum_tensor(name, shape, dt))

        w_qk = sb("oa_w_qk", [D, 2, D])
        w_vg = sb("oa_w_vg", [D, 2, D])
        w_out = sb("oa_w_out", [D, D])
        w_out_scaled = sb("oa_w_out_scaled", [D, D])
        gain = sb("oa_gain", [D, 1])
        b_qk = sb("oa_b_qk", [D, 2])
        b_vg = sb("oa_b_vg", [1, 2, D])
        b_out = sb("oa_b_out", [1, D])
        ones_row = sb("oa_ones_row", [1, L])
        shift = sb("oa_shift", [D, NO])
        sum_w = sb("oa_sum_w", [D, NO, 4 * NH])
        pos_bias = sb("oa_pos_bias", [128, NCH])
        cosines = sb("oa_cosines", [128, NCH])
        amp = sb("oa_amp", [128, 1])
        bias_col = sb("oa_bias_col", [128, NCH])
        bias = sb("oa_bias", [128, NCH, L])
        stats = sb("oa_stats", [L, GB, 6])
        mv = sb("oa_mv", [L, GB, 2])
        var_eps = sb("oa_var_eps", [L, GB])
        rstd = sb("oa_rstd", [L, GB])
        z = [sb(f"oa_z{p}", [L, GB, D]) for p in range(2)]
        zT = [sb(f"oa_zT{p}", [D, GB, L]) for p in range(2)]
        q_sb = [sb(f"oa_q{p}", [D, GB, L]) for p in range(2)]
        k_sb = [sb(f"oa_k{p}", [D, PAD + GT]) for p in range(2)]
        v_ones = [sb(f"oa_v_ones{p}", [L, GB, NH, DH + 1]) for p in range(2)]
        gate = [sb(f"oa_gate{p}", [L, GB, D]) for p in range(2)]
        prod_dve = [sb(f"oa_prod_dve{i}", [D, 4, GB, L]) for i in range(NDVE)]
        prod_pool = [sb(f"oa_prod_pool{i}", [D, 4, GB, L]) for i in range(NPOOL)]
        biased = sb("oa_biased", [128, NCH, GB, L])
        top = [sb(f"oa_top{i}", [L, NH]) for i in range(2)]
        probs = [sb(f"oa_probs{p}", [L, NO, GB, NH]) for p in range(2)]
        dense = [sb(f"oa_dense{p}", [L, L, BH]) for p in range(2)]
        inv_sum = sb("oa_inv_sum", [L, GB, NH])
        heads_out = sb("oa_heads_out", [L, GB, D])
        gated = sb("oa_gated", [L, GB, D])
        gatedT = sb("oa_gatedT", [D, GB, L])
        p_sc = [ps(f"oa_p_sc{i}", [128, 512]) for i in range(2)]
        p_turned = [ps(f"oa_p_turned{i}", [128, 512]) for i in range(2)]
        p_qk = ps("oa_p_qk", [D, GB, L])
        p_vg = ps("oa_p_vg", [L, 2, 2, D])
        p_o = ps("oa_p_o", [L, 2, NH, DH + 1])
        p_out = ps("oa_p_out", [128, 512])
        p_gatedT = p_out[:, 0:GT].rearrange("p (b l) -> p b l", b=GB)
        p_rows = p_out[0:L, :].rearrange("p (b d) -> p b d", b=GB)

        def sc_of(p, c):
            return p_sc[(NCH * p + c) % 2]

        def turned(b):
            return p_turned[b % 2][0:L, 0:NO * NH].rearrange("n (o h) -> n o h", h=NH)

        def products(eng, p, u, done):
            who, c, place = UNITS[u]
            buf = (prod_dve if who == "dve" else prod_pool)[SLOT[u]]
            js = [CHUNK * c + 4 * i + place for i in range(4)] if c < NCH - 1 else list(range(CHUNK * c, NO))
            runs = [(0, 4)] if c < NCH - 1 else [(i, i + 1) for i in range(LAST)]
            for a, e in runs:
                lo = OFFS[js[e - 1]]
                n = e - a
                k0 = k_sb[p][:, PAD - OFFS[js[a]] + lo:PAD - OFFS[js[a]] + lo + 1]
                q0 = q_sb[p][:, 0, lo:lo + 1]
                k_win = bass.AP(k0.tensor, k0.offset, [list(k0.ap[0]), [4, n], [L, GB], [1, L - lo]])
                q_win = bass.AP(q0.tensor, q0.offset, [list(q0.ap[0]), [0, n], [L, GB], [1, L - lo]])
                last = eng.tensor_tensor(buf[:, a:e, :, lo:L], q_win, k_win, ALU.mult)
            last.then_inc(done, 1)

        weights_in = sem("oa_weights_in")
        scaled = sem("oa_scaled")
        bias_steps = sem("oa_bias_steps")
        masked = sem("oa_masked")
        cleared = sem("oa_cleared")
        zeroed = sem("oa_zeroed")
        stats_done = sem("oa_stats_done")
        mv_done = sem("oa_mv_done")
        eps_added = sem("oa_eps_added")
        rstd_done = sem("oa_rstd_done")
        z_done = sem("oa_z_done")
        zT_made = sem("oa_zT_made")
        zT_kept = sem("oa_zT_kept")
        q_made = sem("oa_q_made")
        q_kept = sem("oa_q_kept")
        k_made = sem("oa_k_made")
        k_kept = sem("oa_k_kept")
        vg_made = sem("oa_vg_made")
        v_kept = sem("oa_v_kept")
        gate_done = sem("oa_gate_done")
        pool_prods = sem("oa_pool_prods")
        dve_prods = sem("oa_dve_prods")
        summed = sem("oa_summed")
        chunk_made = sem("oa_chunk_made")
        bias_added = sem("oa_bias_added")
        turned_made = sem("oa_turned_made")
        top_done = sem("oa_top_done")
        sub_done = sem("oa_sub_done")
        exp_done = sem("oa_exp_done")
        skewed = [sem(f"oa_skewed{p}") for p in range(2)]
        dense_in = [sem(f"oa_dense_in{p}") for p in range(2)]
        pv_done = sem("oa_pv_done")
        inv_done = sem("oa_inv_done")
        out_done = sem("oa_out_done")
        gated_done = sem("oa_gated_done")
        gatedT_made = sem("oa_gatedT_made")
        gatedT_kept = sem("oa_gatedT_kept")
        rows_made = sem("oa_rows_made")
        h_done = sem("oa_h_done")

        block = ctx.enter_context(nc.Block())

        @block.sync
        def _(sp):
            T.clear_old(sp)
            for dst, src in ((w_qk[:], t["o_wqkv"][:, 0:2 * D].rearrange("d (j e) -> d j e", j=2)),
                             (w_vg[:, 0, :], t["o_wqkv"][:, 2 * D:3 * D]), (w_vg[:, 1, :], t["o_wgate"]),
                             (w_out[:], t["o_wout"]), (gain[:], t["o_gain"].unsqueeze(1)),
                             (b_qk[:], t["o_bqk"]),
                             (b_vg[:], t["o_bvg"].rearrange("(o j d) -> o j d", o=1, j=2)),
                             (b_out[:], t["o_bout"].unsqueeze(0)), (shift[:], t["o_scale"]),
                             (pos_bias[:], t["o_pos"]),
                             (cosines[:], t["o_cos"]),
                             (amp[:], t["o_amp"].unsqueeze(1))):
                sp.dma_start(dst, src).then_inc(weights_in, 16)
            sp.wait_ge(cleared, 1)
            for p in range(2):
                sp.dma_start(T.diagonals[p][PAD:PAD + L], dense[0][:]).then_inc(zeroed, 16)
            sp.wait_ge(zeroed, 32)

            def along_diagonals(g, p, w):
                row, col = L * BH, BH
                d = T.diagonals[p]
                T.wait_alone(sp, exp_done, GB * (g + 1))
                if at_least(g, 2):
                    T.wait_alone(sp, dense_in[p], 64 * w)
                sp.dma_start(bass.AP(d.tensor, (PAD - OFF_LOCAL) * row, [[row + col, L], [row, NLOC], [1, BH]]),
                             probs[p][:, 0:NLOC].rearrange("n o b h -> n o (b h)")).then_inc(skewed[p], 16)
                for j in range(NLOC, NO):
                    sp.dma_start(bass.AP(d.tensor, (PAD - OFFS[j]) * row, [[row + col, L], [1, BH]]),
                                 probs[p][:, j].rearrange("n b h -> n (b h)")).then_inc(skewed[p], 16)

            def as_matrices(g, p, w):
                T.wait_alone(sp, skewed[p], 16 * (1 + NO - NLOC) * (w + 1))
                if at_least(g, 2):
                    T.wait_alone(sp, pv_done, 2 * (g - 1))
                for m in range(0, L, 32):
                    e = min(m + 32, L)
                    sp.dma_start(dense[p][m:e, m:L, :], T.diagonals[p][PAD + m:PAD + e, m:L]).then_inc(dense_in[p], 16)

            for g in range(2):
                along_diagonals(g, g, 0)
                as_matrices(g, g, 0)
            with sp.Fori(1, NG // 2) as k:
                for p in range(2):
                    along_diagonals(2 * k + p, p, k)
                    as_matrices(2 * k + p, p, k)

        @block.gpsimd
        def _(pool):
            pool.wait_ge(bias_steps, 1)
            for c in range(NCH - 1):
                pool.affine_select(out=bias[:, c, :], in_=bias[:, c, :], compare_op=ALU.is_ge, fill=-1e30,
                                   base=NH * (CHUNK * c - OFF_LOCAL), pattern=[[NH, L]],
                                   channel_multiplier=1).then_inc(masked, 1)
            for i in range(1, LAST):
                rows, far = slice(32 * i, 32 * i + 32), OFFS[CHUNK * (NCH - 1) + i]
                pool.wait_ge(masked, NCH - 2 + i)
                pool.affine_select(out=bias[rows, NCH - 1, :], in_=bias[rows, NCH - 1, :], compare_op=ALU.is_ge,
                                   fill=-1e30, base=-far, pattern=[[1, L]], channel_multiplier=0).then_inc(masked, 1)

            def rstd_of(g):
                pool.wait_ge(mv_done, GB * (g + 1))
                pool.tensor_tensor(var_eps[:], mv[:, :, 1], T.eps[:], ALU.add).then_inc(eps_added, 1)
                pool.wait_ge(eps_added, g + 1)
                pool.tensor_tensor(rstd[:], var_eps[:], T.neg_half[:], ALU.pow).then_inc(rstd_done, 1)

            def turn(g, p):
                for u in range(NU):
                    if UNITS[u][0] == "pool":
                        if SLOT[u] == 0:
                            T.wait_alone(pool, k_kept, g + 1)
                        if at_least(g, 1):
                            T.wait_alone(pool, summed, NU * (g - 1) + u + 1)
                        products(pool, p, u, pool_prods)
                        if SLOT[u] == 1 and below(g, NG - 2):
                            rstd_of(g + 2)

            rstd_of(0)
            rstd_of(1)
            pool.wait_ge(cleared, 3)
            for g in range(4):
                turn(g, g % 2)
            with pool.Fori(2, NG // 2 - 1) as k:
                turn(2 * k, 0)
                turn(2 * k + 1, 1)
            turn(NG - 2, 0)
            turn(NG - 1, 1)

        @block.tensor
        def _(pe):
            pe.wait_ge(weights_in, 16 * 12)
            pe.wait_ge(scaled, 7)

            def z_transposes(g, p):
                T.wait_alone(pe, z_done, g + 1)
                if at_least(g, 1):
                    T.wait_alone(pe, k_kept, g)
                for b in range(GB):
                    last = pe.transpose(p_qk[:, b, :], z[p][:, b, :], T.ident[0:L, 0:L])
                last.then_inc(zT_made, 1)

            def queries(g, p):
                T.wait_alone(pe, zT_kept, g + 1)
                pe.matmul(p_qk[:], w_qk[:, 0, :], zT[p][:], start=True, stop=True).then_inc(q_made, 1)

            def keys(g, p):
                T.wait_alone(pe, q_kept, g + 1)
                pe.matmul(p_qk[:], w_qk[:, 1, :], zT[p][:], start=True, stop=True).then_inc(k_made, 1)

            def values_gate(g, p, i):
                if at_least(g, 1) or i == 1:
                    T.wait_alone(pe, gate_done, 2 * g + i)
                for j in range(2):
                    b = 2 * i + j
                    pe.matmul(p_vg[:, j], zT[p][:, b, :], w_vg[:], start=True, stop=False)
                    last = pe.matmul(p_vg[:, j], ones_row[:], b_vg[:], start=False, stop=True)
                last.then_inc(vg_made, 1)

            def sums(g, p, u):
                who, c, place = UNITS[u]
                if u == 0 or UNITS[u - 1][1] != c:
                    if at_least(g, 1) or c >= 2:
                        T.wait_alone(pe, bias_added, NCH * g + c - 1)
                if who == "dve":
                    T.wait_alone(pe, dve_prods, NDVE * g + SLOT[u] + 1)
                    buf = prod_dve[SLOT[u]]
                else:
                    T.wait_alone(pe, pool_prods, NPOOL * g + SLOT[u] + 1)
                    buf = prod_pool[SLOT[u]]
                for i in range(4):
                    j = CHUNK * c + (4 * i + place if c < NCH - 1 else i)
                    last = pe.matmul(sc_of(p, c)[32 * i:32 * i + 32, 0:GT], sum_w[:, j, :],
                                     buf[:, i].rearrange("d b l -> d (b l)"), start=(place == 0),
                                     stop=(place == 3 or c == NCH - 1), skip_group_check=True)
                last.then_inc(summed, 1)
                if u == NU - 1 or UNITS[u + 1][1] != c:
                    pe.wait_ge(summed, NU * g + u + 1)
                    pe.sem_inc(chunk_made, 1)

            def turn_scores(g, b):
                s = GB * g + b
                T.wait_alone(pe, bias_added, NCH * (g + 1))
                if at_least(g, 1) or b >= 2:
                    T.wait_alone(pe, sub_done, s - 1)
                for c in range(NCH - 1):
                    pe.transpose(p_turned[b % 2][0:L, c * 128:(c + 1) * 128], biased[:, c, b, :], T.ident[:])
                pe.matmul(p_turned[b % 2][0:L, (NCH - 1) * 128:NO * NH], biased[:, NCH - 1, b, :],
                          T.ident[:].rearrange("r (i m) -> r i m", i=LAST)[:, :, 0:NH], start=True, stop=True
                          ).then_inc(turned_made, 1)

            def values(g, p, w, i):
                if i == 0:
                    T.wait_alone(pe, dense_in[p], 64 * (w + 1))
                    T.wait_alone(pe, v_kept, 2 * (g + 1))
                if at_least(g, 1) or i == 1:
                    T.wait_alone(pe, out_done, 2 * g + i)
                for j in range(2):
                    for h in range(NH):
                        b = 2 * i + j
                        last = pe.matmul(p_o[:, j, h, :], dense[p][:, :, b * NH + h], v_ones[p][:, b, h, :],
                                         start=True, stop=True)
                last.then_inc(pv_done, 1)

            def gated_transposes(g):
                T.wait_alone(pe, gated_done, g + 1)
                if at_least(g, 1):
                    T.wait_alone(pe, h_done, g)
                for b in range(GB):
                    last = pe.transpose(p_gatedT[:, b, :], gated[:, b, :], T.ident[0:L, 0:L])
                last.then_inc(gatedT_made, 1)

            def project_out(g):
                T.wait_alone(pe, gatedT_kept, g + 1)
                for b in range(GB):
                    pe.matmul(p_rows[:, b, :], gatedT[:, b, :], w_out_scaled[:], start=True, stop=False)
                    last = pe.matmul(p_rows[:, b, :], ones_row[:], b_out[:], start=False, stop=True)
                last.then_inc(rows_made, 1)

            def turn(g, p, w):
                if here(g - 1):
                    values_gate(g - 1, 1 - p, 0)
                if here(g):
                    sums(g, p, 0)
                if here(g - 1):
                    values_gate(g - 1, 1 - p, 1)
                if here(g + 1):
                    z_transposes(g + 1, 1 - p)
                if here(g):
                    sums(g, p, 1)
                if here(g + 1):
                    queries(g + 1, 1 - p)
                if here(g):
                    sums(g, p, 2)
                if here(g + 1):
                    keys(g + 1, 1 - p)
                if here(g - 1):
                    turn_scores(g - 1, 0)
                    turn_scores(g - 1, 1)
                if here(g - 2):
                    values(g - 2, p, w - 1, 0)
                if here(g - 1):
                    turn_scores(g - 1, 2)
                    turn_scores(g - 1, 3)
                if here(g):
                    sums(g, p, 3)
                if here(g - 2):
                    values(g - 2, p, w - 1, 1)
                if here(g):
                    sums(g, p, 4)
                if here(g - 3):
                    gated_transposes(g - 3)
                if here(g):
                    sums(g, p, 5)
                    sums(g, p, 6)
                if here(g - 3):
                    project_out(g - 3)
                if here(g):
                    sums(g, p, 7)
                    sums(g, p, 8)

            z_transposes(0, 0)
            queries(0, 0)
            keys(0, 0)
            for g in range(4):
                turn(g, g % 2, g // 2)
            with pe.Fori(2, NG // 2 - 1) as k:
                turn(2 * k, 0, k)
                turn(2 * k + 1, 1, k)
            for g in range(NG - 2, NG + 4):
                turn(g, g % 2, g // 2)

        @block.scalar
        def _(act):
            act.wait_ge(weights_in, 16 * 12)
            act.wait_ge(cleared, 3)

            def keep_zT(g, p):
                act.wait_ge(zT_made, g + 1)
                if at_least(g, 2):
                    act.wait_ge(vg_made, 2 * (g - 1))
                act.copy(zT[p][:], p_qk[:]).then_inc(zT_kept, 1)

            def keep_qk(g, p):
                act.wait_ge(q_made, g + 1)
                if at_least(g, 2):
                    act.wait_ge(dve_prods, NDVE * (g - 1))
                    act.wait_ge(pool_prods, NPOOL * (g - 1))
                act.activation(q_sb[p][:], p_qk[:], ACT.Identity, bias=b_qk[:, 0:1]).then_inc(q_kept, 1)
                act.wait_ge(k_made, g + 1)
                act.activation(k_sb[p][:, PAD:PAD + GT].rearrange("p (b l) -> p b l", b=GB), p_qk[:], ACT.Identity,
                               bias=b_qk[:, 1:2]).then_inc(k_kept, 1)

            def keep_vg(g, p, i):
                act.wait_ge(vg_made, 2 * g + i + 1)
                if at_least(g, 2):
                    act.wait_ge(pv_done, 2 * (g - 1))
                    act.wait_ge(gated_done, g - 1)
                act.copy(v_ones[p][:, 2 * i:2 * i + 2, :, 0:DH],
                         p_vg[:, :, 0, :].rearrange("l j (h d) -> l j h d", h=NH)).then_inc(v_kept, 1)
                act.activation(gate[p][:, 2 * i:2 * i + 2, :], p_vg[:, :, 1, :], ACT.Tanh,
                               scale=0.5).then_inc(gate_done, 1)

            def exponential(g, p, b):
                act.wait_ge(sub_done, GB * g + b + 1)
                act.activation(probs[p][:, :, b, :], probs[p][:, :, b, :], ACT.Exp).then_inc(exp_done, 1)

            def keep_gatedT(g):
                act.wait_ge(gatedT_made, g + 1)
                if at_least(g, 1):
                    act.wait_ge(rows_made, g)
                act.copy(gatedT[:], p_gatedT).then_inc(gatedT_kept, 1)

            def turn(g, p):
                if here(g - 1):
                    keep_vg(g - 1, 1 - p, 0)
                    keep_vg(g - 1, 1 - p, 1)
                if here(g + 1):
                    keep_zT(g + 1, 1 - p)
                    keep_qk(g + 1, 1 - p)
                if here(g - 1):
                    for b in range(GB):
                        exponential(g - 1, 1 - p, b)
                if here(g - 3):
                    keep_gatedT(g - 3)

            keep_zT(0, 0)
            keep_qk(0, 0)
            for g in range(4):
                turn(g, g % 2)
            with act.Fori(2, NG // 2 - 1) as k:
                turn(2 * k, 0)
                turn(2 * k + 1, 1)
            for g in range(NG - 2, NG + 4):
                turn(g, g % 2)

        @block.vector
        def _(dve):
            dve.memset(dense[0][:], 0.0).then_inc(cleared, 1)
            for buf in prod_pool + prod_dve:
                dve.memset(buf[:], 0.0)
            for i in range(2):
                dve.memset(k_sb[i][:, 0:PAD], 0.0)
                dve.memset(v_ones[i][:], 1.0)
            dve.memset(sum_w[:], 0.0)
            dve.memset(bias[:], 0.0).then_inc(bias_steps, 1)
            dve.memset(ones_row[:], 1.0).then_inc(cleared, 1)
            dve.memset(dense[1][:], 0.0).then_inc(cleared, 1)
            dve.wait_ge(weights_in, 16 * 12)
            dve.tensor_scalar(bias_col[:], cosines[:], amp[:, 0:1], None, ALU.mult).then_inc(bias_steps, 1)
            dve.tensor_scalar(shift[:], shift[:], 1.0, DH ** -0.5, ALU.add, ALU.mult).then_inc(scaled, 1)
            dve.tensor_scalar(w_out_scaled[:], w_out[:], gain[:, 0:1], 0.5, ALU.mult, ALU.mult).then_inc(scaled, 1)
            dve.wait_ge(scaled, 2)
            near = CHUNK * (NCH - 1)
            for place in range(4):
                dve.tensor_tensor(sum_w[:, place:near:4, NH * place:NH * (place + 1)], over(shift[:, place:near:4], NH, 2),
                                  over(T.head_mask[:], near // 4), ALU.mult).then_inc(scaled, 1)
            dve.tensor_tensor(sum_w[:, near:NO, 0:NH], over(shift[:, near:NO], NH, 2),
                              over(T.head_mask[:], LAST), ALU.mult).then_inc(scaled, 1)
            dve.wait_ge(bias_steps, 2)
            dve.tensor_tensor(bias_col[:], bias_col[:], pos_bias[:], ALU.add).then_inc(bias_steps, 1)
            dve.wait_ge(bias_steps, 3)
            dve.wait_ge(masked, NCH - 1 + LAST - 1)
            dve.tensor_tensor(bias[:], bias[:], over(bias_col[:], L, 2), ALU.add).then_inc(bias_steps, 1)
            dve.wait_ge(zeroed, 32)

            def moments(g):
                for b in range(GB):
                    dve.bn_stats(stats[:, b, :], T.H[:, g * GB + b, :]).then_inc(stats_done, 1)
                T.wait_alone(dve, stats_done, GB * (g + 1))
                for b in range(GB):
                    dve.bn_aggr(mv[:, b, :], stats[:, b, :]).then_inc(mv_done, 1)

            def normalize(g, p):
                T.wait_alone(dve, rstd_done, g + 1)
                if at_least(g, 2):
                    T.wait_alone(dve, zT_made, g - 1)
                for b in range(GB):
                    last = dve.tensor_scalar(z[p][:, b, :], T.H[:, g * GB + b, :], mv[:, b, 0:1],
                                             rstd[:, b:b + 1], ALU.subtract, ALU.mult)
                last.then_inc(z_done, 1)

            def products_of(g, p, u):
                if u == 0:
                    T.wait_alone(dve, k_kept, g + 1)
                if at_least(g, 1):
                    T.wait_alone(dve, summed, NU * (g - 1) + u + 1)
                products(dve, p, u, dve_prods)

            def add_bias(g, p, c):
                dve.wait_ge(chunk_made, NCH * g + c + 1)
                if at_least(g, 1):
                    dve.wait_ge(turned_made, GB * g)
                dve.tensor_tensor(biased[:, c], sc_of(p, c)[:, 0:GT].rearrange("r (b l) -> r b l", b=GB),
                                  over(bias[:, c], GB), ALU.add).then_inc(bias_added, 1)

            def less_maximum(g, p, b, w):
                s = GB * g + b
                dve.wait_ge(turned_made, s + 1)
                dve.tensor_reduce(top[b % 2][:], turned(b).rearrange("n o h -> n h o"), AX_X,
                                  ALU.max).then_inc(top_done, 1)
                dve.wait_ge(top_done, s + 1)
                if b == 0 and at_least(g, 2):
                    dve.wait_ge(skewed[p], 16 * (1 + NO - NLOC) * w)
                dve.tensor_tensor(probs[p][:, :, b, :], turned(b), over(top[b % 2][:], NO),
                                  ALU.subtract).then_inc(sub_done, 1)

            def divide(g, i):
                dve.wait_ge(pv_done, 2 * g + i + 1)
                dve.reciprocal(inv_sum[:, 2 * i:2 * i + 2, :], p_o[:, :, :, DH]).then_inc(inv_done, 1)
                dve.wait_ge(inv_done, 2 * g + i + 1)
                dve.tensor_tensor(heads_out[:, 2 * i:2 * i + 2, :].rearrange("n b (h d) -> n b h d", h=NH),
                                  p_o[:, :, :, 0:DH], over(inv_sum[:, 2 * i:2 * i + 2, :], DH, 3),
                                  ALU.mult).then_inc(out_done, 1)

            def apply_gate(g, p):
                dve.wait_ge(out_done, 2 * (g + 1))
                dve.wait_ge(gate_done, 2 * (g + 1))
                if at_least(g, 1):
                    dve.wait_ge(gatedT_made, g)
                dve.scalar_tensor_tensor(out=gated[:], in0=gate[p][:], scalar=1.0, in1=heads_out[:], op0=ALU.add,
                                         op1=ALU.mult).then_inc(gated_done, 1)

            def add_to_h(g):
                dve.wait_ge(rows_made, g + 1)
                rows = T.H[:, bass.ds(g * GB, GB), :]
                dve.tensor_tensor(rows, rows, p_rows, ALU.add).then_inc(h_done, 1)

            def turn(g, p, w):
                if here(g):
                    products_of(g, p, 0)
                if here(g + 2):
                    moments(g + 2)
                if here(g - 1):
                    add_bias(g - 1, 1 - p, 1)
                if here(g):
                    products_of(g, p, 1)
                if here(g - 4):
                    add_to_h(g - 4)
                if here(g - 1):
                    add_bias(g - 1, 1 - p, 2)
                if here(g):
                    products_of(g, p, 2)
                if here(g - 1):
                    less_maximum(g - 1, 1 - p, 0, w - 1 + p)
                    less_maximum(g - 1, 1 - p, 1, w - 1 + p)
                if here(g):
                    products_of(g, p, 4)
                if here(g - 1):
                    less_maximum(g - 1, 1 - p, 2, w - 1 + p)
                    less_maximum(g - 1, 1 - p, 3, w - 1 + p)
                if here(g - 2):
                    divide(g - 2, 0)
                if here(g):
                    products_of(g, p, 5)
                    add_bias(g, p, 0)
                if here(g + 2):
                    normalize(g + 2, p)
                if here(g - 2):
                    divide(g - 2, 1)
                    apply_gate(g - 2, p)

            for g in range(2):
                moments(g)
                normalize(g, g)
            for g in range(4):
                turn(g, g % 2, g // 2)
            with dve.Fori(2, NG // 2 - 1) as k:
                turn(2 * k, 0, k)
                turn(2 * k + 1, 1, k)
            for g in range(NG - 2, NG + 4):
                turn(g, g % 2, g // 2)


def stage_dispatch(T):
    nc, t, sem = T.nc, T.t, T.sem
    with ExitStack() as ctx:
        def sb(name, shape, dt=F32):
            return ctx.enter_context(nc.sbuf_tensor(name, shape, dt))

        def ps(name, shape, dt=F32):
            return ctx.enter_context(nc.psum_tensor(name, shape, dt))

        w_gate = sb("di_w_gate", [D, E])
        b_gate = sb("di_b_gate", [1, E])
        ones_row = sb("di_ones_row", [1, L])
        earlier = sb("di_earlier", [L, L], BF16)
        all_ones = sb("di_all_ones", [L, L], BF16)
        empty = sb("di_empty", [128, ROW])
        stats = sb("di_stats", [L, GB, 6])
        mv = sb("di_mv", [L, GB, 2])
        var_eps = sb("di_var_eps", [L, GB])
        rstd = sb("di_rstd", [L, GB])
        z = [sb(f"di_z{p}", [L, GB, D]) for p in range(2)]
        zT = [sb(f"di_zT{p}", [D, GB, L]) for p in range(2)]
        rows = sb("di_rows", [L, B, ROW])
        best = sb("di_best", [L, B])
        less = sb("di_less", [L, B, E])
        preference = sb("di_preference", [L, B, E])
        preference_int = sb("di_preference_int", [L, B, E], I32)
        candidates = sb("di_candidates", [L, B, E])
        first = sb("di_first", [L, B])
        hot = sb("di_hot", [L, B, E])
        hot_bf = sb("di_hot_bf", [L, B, E], BF16)
        score_sum = sb("di_score_sum", [L, B])
        totals = sb("di_totals", [L, E, B])
        same_expert = sb("di_same_expert", [L, E, B])
        running = sb("di_running", [L, E, B])
        tiles_int = sb("di_tiles_int", [L, E], I32)
        tiles_shifted = sb("di_tiles_shifted", [L, E], I32)
        tiles = sb("di_tiles", [L, E])
        ones_e = sb("di_ones_e", [L, E])
        tile_end = sb("di_tile_end", [L, E])
        base = sb("di_base", [L, E])
        place = sb("di_place", [L, B, E])
        slot_f = sb("di_slot_f", [L, B])
        slot = sb("di_slot", [L, B], I32)
        tile_no = sb("di_tile_no", [1, NTILES])
        tile_no_int = sb("di_tile_no_int", [1, NTILES], I32)
        passed = sb("di_passed", [1, NTILES, E])
        tile_expert_f = sb("di_tile_expert_f", [1, NTILES])
        p_zT = [ps(f"di_p_zT{p}", [D, GB, L]) for p in range(2)]
        p_logits = ps("di_p_logits", [L, B, E])
        p_before = ps("di_p_before", [L, B, E])
        p_total = ps("di_p_total", [L, B, E])

        weights_in = sem("di_weights_in")
        consts = sem("di_consts")
        emptied = sem("di_emptied")
        stats_done = sem("di_stats_done")
        mv_done = sem("di_mv_done")
        eps_added = sem("di_eps_added")
        rstd_done = sem("di_rstd_done")
        z_done = sem("di_z_done")
        z_copied = sem("di_z_copied")
        h_copied = sem("di_h_copied")
        zT_made = sem("di_zT_made")
        zT_kept = sem("di_zT_kept")
        logits_made = sem("di_logits_made")
        step = sem("di_step")
        less_done = sem("di_less_done")
        exp_done = sem("di_exp_done")
        hot_done = sem("di_hot_done")
        counts_made = sem("di_counts_made")
        score_done = sem("di_score_done")
        slot_done = sem("di_slot_done")
        tile_expert_done = sem("di_tile_expert_done")
        dispatched = sem("di_dispatched")

        block = ctx.enter_context(nc.Block())

        @block.sync
        def _(sp):
            T.clear_old(sp)
            sp.dma_start(w_gate[:], t["r_w"]).then_inc(weights_in, 16)
            sp.dma_start(b_gate[:], t["r_b"].unsqueeze(0)).then_inc(weights_in, 16)
            sp.wait_ge(consts, 8)
            sp.dma_start(T.slot_rows.rearrange("(i n) c -> n i c", n=128), over(empty[:], NTILES * TILE // 128)
                         ).then_inc(emptied, 16)
            sp.wait_ge(emptied, 16)

        @block.gpsimd
        def _(pool):
            pool.memset(all_ones[:], 1.0).then_inc(consts, 1)
            pool.wait_ge(consts, 1)
            pool.affine_select(out=earlier[:], in_=all_ones[:], compare_op=ALU.is_gt, fill=0.0, base=0,
                               pattern=[[1, L]], channel_multiplier=-1).then_inc(consts, 1)
            pool.iota(preference_int[:], pattern=[[0, B], [-1, E]], base=E, channel_multiplier=0).then_inc(consts, 1)
            pool.iota(tile_no_int[:], pattern=[[1, NTILES]], base=0, channel_multiplier=0).then_inc(consts, 1)
            pool.wait_ge(consts, 4)
            pool.tensor_copy(preference[:], preference_int[:]).then_inc(consts, 1)
            pool.tensor_copy(tile_no[:], tile_no_int[:]).then_inc(consts, 1)
            pool.memset(empty[:], 0.0).then_inc(consts, 1)
            pool.wait_ge(consts, 7)
            pool.memset(empty[:, 2 * D:2 * D + 1].bitcast(I32), N).then_inc(consts, 1)
            pool.wait_ge(consts, 8)
            pool.iota(rows[:, :, 2 * D:2 * D + 1].bitcast(I32), pattern=[[L, B], [0, 1]], base=0,
                      channel_multiplier=1).then_inc(consts, 1)

            def finish(g, p):
                pool.wait_ge(mv_done, GB * (g + 1))
                pool.tensor_tensor(var_eps[:], mv[:, :, 1], T.eps[:], ALU.add).then_inc(eps_added, 1)
                pool.wait_ge(eps_added, g + 1)
                pool.tensor_tensor(rstd[:], var_eps[:], T.neg_half[:], ALU.pow).then_inc(rstd_done, 1)
                T.wait_alone(pool, z_done, g + 1)
                pool.tensor_copy(rows[:, bass.ds(g * GB, GB), 0:D], z[p][:]).then_inc(z_copied, 1)

            with pool.Fori(0, NG // 2) as k:
                finish(2 * k, 0)
                finish(2 * k + 1, 1)
            pool.wait_ge(h_copied, NG)
            pool.wait_ge(score_done, 1)
            pool.wait_ge(slot_done, 1)
            pool.wait_ge(consts, 9)
            pool.wait_ge(emptied, 16)
            pool.wait_ge(z_copied, NG)
            for b in range(B):
                pool.indirect_dma_start(out=T.slot_rows,
                                        out_offset=bass.IndirectOffsetOnAxis(ap=slot[:, b:b + 1], axis=0),
                                        in_=rows[:, b, :], in_offset=None).then_inc(dispatched, 16)
            pool.wait_ge(dispatched, 16 * B)

        @block.tensor
        def _(pe):
            pe.wait_ge(weights_in, 32)

            def transposes(g, p):
                T.wait_alone(pe, z_done, g + 1)
                if at_least(g, 2):
                    T.wait_alone(pe, zT_kept, g - 1)
                for b in range(GB):
                    last = pe.transpose(p_zT[p][:, b, :], z[p][:, b, :], T.ident[0:L, 0:L])
                last.then_inc(zT_made, 1)

            def route(g, p):
                T.wait_alone(pe, zT_kept, g + 1)
                for b in range(GB):
                    out = p_logits[:, bass.ds(g * GB + b, 1), :].rearrange("l o e -> l (o e)")
                    pe.matmul(out, zT[p][:, b, :], w_gate[:], start=True, stop=False)
                    last = pe.matmul(out, ones_row[:], b_gate[:], start=False, stop=True)
                last.then_inc(logits_made, 1)

            pe.wait_ge(step, 1)
            transposes(0, 0)
            transposes(1, 1)
            route(0, 0)
            with pe.Fori(1, NG // 2) as k:
                transposes(2 * k, 0)
                route(2 * k - 1, 1)
                transposes(2 * k + 1, 1)
                route(2 * k, 0)
            route(NG - 1, 1)
            pe.wait_ge(hot_done, 1)
            pe.wait_ge(consts, 2)
            pe.matmul(p_total[:], all_ones[:], hot_bf[:], start=True, stop=True).then_inc(counts_made, 1)
            pe.matmul(p_before[:], earlier[:], hot_bf[:], start=True, stop=True).then_inc(counts_made, 1)

        @block.scalar
        def _(act):
            with act.Fori(0, NG // 2) as k:
                for p in range(2):
                    g = 2 * k + p
                    act.wait_ge(zT_made, g + 1)
                    act.wait_ge(logits_made, g + 1)
                    act.copy(zT[p][:], p_zT[p][:]).then_inc(zT_kept, 1)
                    act.copy(rows[:, bass.ds(g * GB, GB), D:2 * D], T.H[:, bass.ds(g * GB, GB), :]).then_inc(h_copied, 1)
            act.wait_ge(less_done, 1)
            act.activation(less[:], less[:], ACT.Exp).then_inc(exp_done, 1)

        @block.vector
        def _(dve):
            dve.sem_inc(logits_made, 2)
            dve.memset(ones_row[:], 1.0)
            dve.memset(ones_e[:], 1.0)
            dve.memset(same_expert[:], 1.0).then_inc(step, 1)
            dve.wait_ge(step, 1)
            dve.memset(same_expert[:, :, 0:1], 0.0).then_inc(step, 1)

            def norm(g, p):
                for b in range(GB):
                    dve.bn_stats(stats[:, b, :], T.H[:, g * GB + b, :]).then_inc(stats_done, 1)
                T.wait_alone(dve, stats_done, GB * (g + 1))
                for b in range(GB):
                    dve.bn_aggr(mv[:, b, :], stats[:, b, :]).then_inc(mv_done, 1)
                T.wait_alone(dve, rstd_done, g + 1)
                if at_least(g, 2):
                    T.wait_alone(dve, zT_made, g - 1)
                    T.wait_alone(dve, z_copied, g - 1)
                for b in range(GB):
                    last = dve.tensor_scalar(z[p][:, b, :], T.H[:, g * GB + b, :], mv[:, b, 0:1],
                                             rstd[:, b:b + 1], ALU.subtract, ALU.mult)
                last.then_inc(z_done, 1)

            norm(0, 0)
            norm(1, 1)
            with dve.Fori(1, NG // 2) as k:
                norm(2 * k, 0)
                norm(2 * k + 1, 1)

            dve.wait_ge(logits_made, NG + 2)
            dve.tensor_reduce(best[:], p_logits[:], AX_X, ALU.max).then_inc(step, 1)
            dve.wait_ge(step, 3)
            dve.tensor_tensor(less[:], p_logits[:], over(best[:], E, 2), ALU.subtract).then_inc(less_done, 1)
            dve.wait_ge(consts, 6)
            dve.tensor_tensor(candidates[:], p_logits[:], over(best[:], E, 2), ALU.is_equal).then_inc(step, 1)
            dve.wait_ge(step, 4)
            dve.tensor_tensor(candidates[:], candidates[:], preference[:], ALU.mult).then_inc(step, 1)
            dve.wait_ge(step, 5)
            dve.tensor_reduce(first[:], candidates[:], AX_X, ALU.max).then_inc(step, 1)
            dve.wait_ge(step, 6)
            dve.tensor_tensor(hot_bf[:], candidates[:], over(first[:], E, 2), ALU.is_equal).then_inc(hot_done, 1)
            dve.tensor_tensor(hot[:], candidates[:], over(first[:], E, 2), ALU.is_equal).then_inc(step, 1)
            dve.wait_ge(exp_done, 1)
            dve.tensor_reduce(score_sum[:], less[:], AX_X, ALU.add).then_inc(step, 1)
            dve.wait_ge(step, 8)
            dve.reciprocal(rows[:, :, 2 * D + 1:2 * D + 2].rearrange("l b o -> l (b o)"), score_sum[:]
                           ).then_inc(score_done, 1)
            dve.wait_ge(counts_made, 2)
            dve.tensor_copy(totals[:].rearrange("l e b -> l b e"), p_total[:]).then_inc(step, 1)
            dve.wait_ge(step, 9)
            dve.tensor_tensor_scan(running[:].rearrange("l e b -> l (e b)"),
                                   same_expert[:].rearrange("l e b -> l (e b)"),
                                   totals[:].rearrange("l e b -> l (e b)"), 0.0, ALU.mult, ALU.add).then_inc(step, 1)
            dve.wait_ge(step, 10)
            dve.tensor_scalar(tiles_int[:], running[:, :, B - 1], float(TILE - 1), None, ALU.add).then_inc(step, 1)
            dve.wait_ge(step, 11)
            dve.tensor_scalar(tiles_shifted[:], tiles_int[:], TILE.bit_length() - 1, None,
                              ALU.arith_shift_right).then_inc(step, 1)
            dve.wait_ge(step, 12)
            dve.tensor_copy(tiles[:], tiles_shifted[:]).then_inc(step, 1)
            dve.wait_ge(step, 13)
            dve.tensor_tensor_scan(tile_end[:], ones_e[:], tiles[:], 0.0, ALU.mult, ALU.add).then_inc(step, 1)
            dve.wait_ge(step, 14)
            dve.tensor_tensor(base[:], tile_end[:], tiles[:], ALU.subtract).then_inc(step, 1)
            dve.wait_ge(step, 15)
            dve.tensor_scalar(base[:], base[:], float(TILE), None, ALU.mult).then_inc(step, 1)
            dve.tensor_tensor(running[:], running[:], totals[:], ALU.subtract).then_inc(step, 1)
            dve.wait_ge(step, 17)
            dve.tensor_tensor(running[:], running[:], over(base[:], B, 2), ALU.add).then_inc(step, 1)
            dve.wait_ge(step, 18)
            dve.tensor_tensor(place[:], p_before[:], running[:].rearrange("l e b -> l b e"), ALU.add).then_inc(step, 1)
            dve.wait_ge(step, 19)
            dve.tensor_tensor(place[:], place[:], hot[:], ALU.mult).then_inc(step, 1)
            dve.wait_ge(step, 20)
            dve.tensor_reduce(slot_f[:], place[:], AX_X, ALU.add).then_inc(step, 1)
            dve.wait_ge(step, 21)
            dve.tensor_copy(slot[:], slot_f[:]).then_inc(slot_done, 1)
            dve.tensor_tensor(passed[:], over(tile_end[0:1, :], NTILES), over(tile_no[:], E, 2),
                              ALU.is_le).then_inc(step, 1)
            dve.wait_ge(step, 22)
            dve.tensor_reduce(tile_expert_f[:], passed[:], AX_X, ALU.add).then_inc(step, 1)
            dve.wait_ge(step, 23)
            dve.tensor_scalar(T.tile_expert[:], tile_expert_f[:], float(E - 1), None, ALU.min
                              ).then_inc(tile_expert_done, 1)


def stage_top1(T):
    nc, t, sem = T.nc, T.t, T.sem
    S = TILE // 128
    FC = F // 128
    W1, W2, B1 = 0, F, F + FC * D
    PACK = B1 + FC
    with ExitStack() as ctx:
        def sb(name, shape, dt=F32):
            return ctx.enter_context(nc.sbuf_tensor(name, shape, dt))

        def ps(name, shape, dt=F32):
            return ctx.enter_context(nc.psum_tensor(name, shape, dt))

        experts = sb("tp_experts", [128, E, PACK])
        b2 = sb("tp_b2", [128, E, D])
        now = [sb(f"tp_now{p}", [128, PACK]) for p in range(2)]
        rows = [sb(f"tp_rows{a}", [128, S, ROW]) for a in range(4)]
        xT = [sb(f"tp_xT{p}", [D, TILE]) for p in range(2)]
        hidden = [sb(f"tp_hidden{p}", [128, FC, TILE]) for p in range(2)]
        plus_b2 = [sb(f"tp_plus_b2{p}", [128, S, D]) for p in range(2)]
        result = [sb(f"tp_result{a}", [128, S, D]) for a in range(4)]
        token = [sb(f"tp_token{a}", [128, S], I32) for a in range(4)]
        BANK = 512
        p_xT = [ps(f"tp_p_xT{p}", [D, BANK]) for p in range(2)]
        p_hidden = [ps(f"tp_p_hidden{c}", [128, BANK]) for c in range(FC)]
        p_y = [ps(f"tp_p_y{p}", [128, BANK // D, D]) for p in range(2)]

        experts_in = sem("tp_experts_in")
        rows_in = [sem(f"tp_rows_in{a}") for a in range(4)]
        now_done = sem("tp_now_done")
        xT_made = sem("tp_xT_made")
        xT_kept = sem("tp_xT_kept")
        hidden_made = sem("tp_hidden_made")
        relu_done = sem("tp_relu_done")
        y_made = sem("tp_y_made")
        b2_added = sem("tp_b2_added")
        result_done = sem("tp_result_done")
        stored = [sem(f"tp_stored{a}") for a in range(4)]

        block = ctx.enter_context(nc.Block())


        @block.sync
        def _(sp):
            T.clear_old(sp)
            sp.dma_start(experts[:], t["m_pack"]).then_inc(experts_in, 16)
            sp.dma_start(b2[:], t["m_b2"].rearrange("e d -> (e d)").partition_broadcast(128)).then_inc(experts_in, 16)

            def load(w, a):
                i = 4 * w + a
                sp.dma_start(rows[a][:], T.slot_rows[bass.ds(i * TILE, TILE), :].rearrange("(s n) c -> n s c", n=128)
                             ).then_inc(rows_in[a], 16)

            for a in range(4):
                load(0, a)
            with sp.Fori(1, NTILES // 4) as w:
                for a in range(4):
                    sp.wait_ge(result_done, 4 * w + a - 3)
                    load(w, a)

        @block.gpsimd
        def _(pool):
            with pool.Fori(0, NTILES // 4) as w:
                for a in range(4):
                    T.wait_alone(pool, result_done, 4 * w + a + 1)
                    for s in range(S):
                        pool.indirect_dma_start(out=T.out_rows,
                                                out_offset=bass.IndirectOffsetOnAxis(ap=token[a][:, s:s + 1], axis=0),
                                                in_=result[a][:, s, :], in_offset=None, bounds_check=N - 1,
                                                oob_is_err=False).then_inc(stored[a], 16)
            for a in range(4):
                pool.wait_ge(stored[a], 16 * S * NTILES // 4)

        @block.tensor
        def _(pe):
            def transposes(w, a):
                i, p = 4 * w + a, a % 2
                T.wait_alone(pe, rows_in[a], 16 * (w + 1))
                if at_least(i, 2):
                    T.wait_alone(pe, xT_kept, i - 1)
                for s in range(S):
                    last = pe.transpose(p_xT[p][:, s * 128:(s + 1) * 128], rows[a][:, s, 0:D], T.ident[:])
                last.then_inc(xT_made, 1)

            def into_hidden(w, a):
                i, p = 4 * w + a, a % 2
                T.wait_alone(pe, now_done, i + 1)
                T.wait_alone(pe, xT_kept, i + 1)
                for c in range(FC):
                    if at_least(i, 1):
                        T.wait_alone(pe, relu_done, FC * (i - 1) + c + 1)
                    pe.matmul(p_hidden[c][:, 0:TILE], now[p][:, W1 + c * 128:W1 + (c + 1) * 128], xT[p][:],
                              start=True, stop=True).then_inc(hidden_made, 1)

            def out_of_hidden(i, p):
                T.wait_alone(pe, relu_done, FC * (i + 1))
                if at_least(i, 2):
                    T.wait_alone(pe, b2_added, i - 1)
                for s in range(S):
                    for c in range(FC):
                        last = pe.matmul(p_y[p][:, s, :], hidden[p][:, c, s * 128:(s + 1) * 128],
                                         now[p][:, W2 + c * D:W2 + (c + 1) * D], start=(c == 0), stop=(c == FC - 1))
                last.then_inc(y_made, 1)

            def tile(w, a):
                transposes(w, a)
                if at_least(4 * w + a, 1):
                    out_of_hidden(4 * w + a - 1, (a + 1) % 2)
                into_hidden(w, a)

            for a in range(4):
                tile(0, a)
            with pe.Fori(1, NTILES // 4) as w:
                for a in range(4):
                    tile(w, a)
            out_of_hidden(NTILES - 1, 1)

        @block.scalar
        def _(act):
            def tile(w, a):
                i, p = 4 * w + a, a % 2
                T.wait_alone(act, xT_made, i + 1)
                if at_least(i, 2):
                    T.wait_alone(act, y_made, i - 1)
                act.copy(xT[p][:], p_xT[p][:, 0:TILE]).then_inc(xT_kept, 1)
                for c in range(FC):
                    act.wait_ge(hidden_made, FC * i + c + 1)
                    act.activation(hidden[p][:, c, :], p_hidden[c][:, 0:TILE], ACT.Relu,
                                   bias=now[p][:, B1 + c:B1 + c + 1]).then_inc(relu_done, 1)

            for a in range(4):
                tile(0, a)
            with act.Fori(1, NTILES // 4) as w:
                for a in range(4):
                    tile(w, a)

        @block.vector
        def _(dve):
            dve.wait_ge(experts_in, 32)

            def bring(i, p):
                if at_least(i, 2):
                    T.wait_alone(dve, y_made, i - 1)
                e = dve.value_load(T.tile_expert[0:1, bass.ds(i, 1)], min_val=0, max_val=E - 1)
                dve.tensor_copy(now[p][:], experts[:, bass.ds(e, 1), :].rearrange("k o n -> k (o n)")
                                ).then_inc(now_done, 1)

            def finish(i, a, w):
                p = a % 2
                T.wait_alone(dve, y_made, i + 1)
                e = dve.value_load(T.tile_expert[0:1, bass.ds(i, 1)], min_val=0, max_val=E - 1)
                dve.tensor_tensor(plus_b2[p][:], p_y[p][:, 0:S, :],
                                  over(b2[:, bass.ds(e, 1), :].rearrange("n o d -> n (o d)"), S),
                                  ALU.add).then_inc(b2_added, 1)
                T.wait_alone(dve, b2_added, i + 1)
                if at_least(i, 4):
                    T.wait_alone(dve, stored[a], 16 * S * w)
                dve.tensor_copy(token[a][:], rows[a][:, :, 2 * D].bitcast(I32))
                for s in range(S):
                    last = dve.scalar_tensor_tensor(out=result[a][:, s, :], in0=plus_b2[p][:, s, :],
                                                    scalar=rows[a][:, s, 2 * D + 1:2 * D + 2],
                                                    in1=rows[a][:, s, D:2 * D], op0=ALU.mult, op1=ALU.add)
                last.then_inc(result_done, 1)

            bring(0, 0)
            for i in range(1, 5):
                bring(i, i % 2)
                finish(i - 1, i - 1, 0)
            with dve.Fori(1, NTILES // 4 - 1) as w:
                for a in range(4):
                    bring(4 * w + a + 1, (a + 1) % 2)
                    finish(4 * w + a, a, w)
            for a in range(4):
                if a < 3:
                    bring(NTILES - 3 + a, (a + 1) % 2)
                finish(NTILES - 4 + a, a, NTILES // 4 - 1)


STAGES = [stage_tokenizer, stage_attention, stage_router_logits, stage_choose, stage_expert_choice,
          stage_offset_attention, stage_dispatch, stage_top1]


def build(nc, t, out):
    with ExitStack() as ctx:
        T = Tower(nc, ctx, t, out)
        for stage in STAGES:
            T.next_stage()
            stage(T)


def layouts(v):
    import numpy as np
    a = {
        "x": v["x"], "w_proj": v["L0_tok_W_proj"], "w_pwT": v["L0_tok_W_pw"].T, "w_dw": v["L0_tok_W_dw"],
        "b_proj": v["L0_tok_b_proj"], "b_dw": v["L0_tok_b_dw"], "b_pw": v["L0_tok_b_pw"],
        "gamma": v["L0_tok_gamma"], "beta": v["L0_tok_beta"],
        "w_qkvT": v["L0_attn_w_qkv"].T, "w_aggT": v["L0_attn_w_agg"].T, "b_agg": v["L0_attn_b_agg"],
        "w_router": v["L0_ffn_Wr"], "e_w1": v["L0_ffn_W1"].reshape(E * D, F), "e_w2": v["L0_ffn_W2"].reshape(E * F, D),
        "e_b1": v["L0_ffn_b1"].reshape(E, F // 128, 128).transpose(2, 0, 1), "e_b2": v["L0_ffn_b2"],
    }
    tables = list(range(OFF_LOCAL, -1, -1)) + list(range(OFF_LOCAL + 1, len(OFFS)))
    omega = np.array([0.0, 0.0, 1.0, 1.0, 4.0, 4.0, 6.0, 6.0]) * np.pi / np.log(1.0 + 4096.0)
    cosines = np.cos(omega[None, :] * np.log(1.0 + np.array(OFFS, np.float64))[:, None]) * (omega > 0.0)

    def chunked(table):
        out = np.zeros((128, 3), np.float32)
        out[:, 0:2] = table[0:32].reshape(2, 128).T
        out.reshape(4, 32, 3)[:, 0:NH, 2] = table[32:36]
        return out

    a.update({
        "o_wqkv": v["L1_attn_W_qkv"], "o_wgate": v["L1_attn_W_gate"], "o_wout": v["L1_attn_W_out"],
        "o_gain": np.repeat(v["L1_attn_if_gain"], DH), "o_bqk": v["L1_attn_b_qkv"][0:2 * D].reshape(2, D).T,
        "o_bvg": np.concatenate([v["L1_attn_b_qkv"][2 * D:], v["L1_attn_b_gate"]]), "o_bout": v["L1_attn_b_out"],
        "o_scale": np.tile(v["L1_attn_scale_embed"][tables].T, (NH, 1)),
        "o_pos": chunked(v["L1_attn_pos_bias"][tables]), "o_cos": chunked(cosines.astype(np.float32)),
        "o_amp": np.tile(v["L1_attn_disp_amp"], 128 // NH),
        "r_w": v["L1_ffn_Wg"], "r_b": v["L1_ffn_bg"], "m_b2": v["L1_ffn_b2"],
        "m_pack": np.concatenate([
            v["L1_ffn_W1"].transpose(1, 0, 2),
            v["L1_ffn_W2"].reshape(E, F // 128, 128, D).transpose(2, 0, 1, 3).reshape(128, E, F // 128 * D),
            v["L1_ffn_b1"].reshape(E, F // 128, 128).transpose(2, 0, 1)], axis=2),
    })
    return {k: np.ascontiguousarray(x) for k, x in a.items()}


def kernel(**inputs):
    import numpy as _np
    import concourse.bacc as _bacc
    from concourse import mybir as _mybir
    from concourse.bass_utils import run_bass_kernel_spmd as _run

    nc = _bacc.Bacc("TRN2", target_bir_lowering=False, num_devices=1)
    arrays, aps = {}, {}
    for name, a in layouts({k: _np.asarray(v) for k, v in inputs.items()}).items():
        arrays[f"in_{name}_dram"] = a
        aps[name] = nc.dram_tensor(f"in_{name}_dram", a.shape, _mybir.dt.from_np(a.dtype), kind="ExternalInput").ap()
    out = nc.dram_tensor("out_dram", (B, L, D), F32, kind="ExternalOutput").ap()
    build(nc, aps, out)
    r = _run(nc, [arrays], core_ids=[0])
    return r.results[0]["out_dram"]
```

```python
from contextlib import ExitStack

import concourse.bass as bass
from concourse import mybir

F32 = mybir.dt.float32
BF16 = mybir.dt.bfloat16
I32 = mybir.dt.int32
U32 = mybir.dt.uint32
ALU = mybir.AluOpType
ACT = mybir.ActivationFunctionType
AX_X = mybir.AxisListType.X

B, CIN, L, D = 64, 64, 125, 128
GB = 4
NG = B // GB
GT = GB * L
N = B * L
NH, DH = 8, 16
EPS = 1e-5
E, F, CAP = 8, 512, 1024
OFF_LOCAL = 32
OFFS = list(range(OFF_LOCAL, -1, -1)) + [o for o in (48, 64, 96, 128, 192, 256, 384, 512, 768, 1024) if o < L]
TILE = 256
NTILES = (N + E * (TILE - 1)) // TILE
NTILES += -NTILES % 4
ROW = 2 * D + 2


class Tower:

    def __init__(self, nc, ctx, t, out):
        self.nc, self.ctx, self.t, self.out = nc, ctx, t, out
        self.H = self.sb("H", [L, B, D])
        self.ident = self.sb("ident", [128, 128])
        self.chosen = self.sb("chosen", [128, E * CAP // 128], I32)
        self.head_mask = self.sb("head_mask", [D, NH])
        self.h_rows = self.dram("h_rows", [N, D])
        self.z_rows = self.dram("z_rows", [N, D + E])
        self.logits = self.dram("logits", [E, N])
        self.diagonals = [self.dram(f"diagonals{p}", [OFFS[-1] + L, L, GB * NH]) for p in range(2)]
        self.slot_rows = self.dram("slot_rows", [NTILES * TILE, ROW])
        self.tile_expert = self.sb("tile_expert", [1, NTILES], I32)
        self.out_rows = out.rearrange("b l d -> (b l) d")
        self.chosen_rows = self.dram("chosen_rows", [E * CAP])
        self.neg_half = self.sb("neg_half", [L, GB])
        self.consts_done = ctx.enter_context(nc.semaphore("consts_done"))
        self.waited = ctx.enter_context(nc.semaphore("waited"))
        self.old_ctx, self.stage_ctx, self.stage_sems = ExitStack(), ExitStack(), []
        self.eps = self.sb("eps", [L, GB])

    def dram(self, name, shape, dt=F32):
        return self.nc.dram_tensor(name, shape, dt, kind="Internal").ap()

    def sb(self, name, shape, dt=F32):
        return self.ctx.enter_context(self.nc.sbuf_tensor(name, shape, dt))

    def wait_alone(self, eng, sem, value):
        eng.wait_ge(sem, value)
        if not isinstance(value, int):
            eng.sem_inc(self.waited, 1)

    def sem(self, name):
        s = self.stage_ctx.enter_context(self.nc.semaphore(name))
        self.stage_sems.append(s)
        return s

    def next_stage(self):
        self.old_ctx.close()
        self.old_ctx, self.old_sems = self.stage_ctx, self.stage_sems
        self.stage_ctx, self.stage_sems = self.ctx.enter_context(ExitStack()), []

    def clear_old(self, sp):
        for s in self.old_sems:
            sp.sem_clear(s)


def at_least(g, n):
    return not isinstance(g, int) or g >= n


def here(g):
    return not isinstance(g, int) or 0 <= g < NG


def below(g, n):
    return not isinstance(g, int) or g < n


def over(ap, n, axis=1):
    shape = list(ap.shape)
    return ap.unsqueeze(axis).broadcast_to(shape[:axis] + [n] + shape[axis:])


def stage_tokenizer(T):
    nc, t, sem = T.nc, T.t, T.sem
    with ExitStack() as ctx:
        def sb(name, shape, dt=F32):
            return ctx.enter_context(nc.sbuf_tensor(name, shape, dt))

        def ps(name, shape, dt=F32):
            return ctx.enter_context(nc.psum_tensor(name, shape, dt))

        w_proj = sb("tk_w_proj", [D, CIN])
        w_pwT = sb("tk_w_pwT", [D, D])
        w_pw_taps = sb("tk_w_pw_taps", [D, 3, D])
        w_dw = sb("tk_w_dw", [D, 3])
        b_proj = sb("tk_b_proj", [D, 1])
        b_dw = sb("tk_b_dw", [D, 1])
        b_pw = sb("tk_b_pw", [L, D])
        gamma = sb("tk_gamma", [L, D])
        beta = sb("tk_beta", [L, D])
        taps02 = sb("tk_taps02", [2 * CIN, D])
        tap1 = sb("tk_tap1", [CIN, D])
        edge = sb("tk_edge", [D, 3])
        conv_bias = sb("tk_conv_bias", [D, L])
        bias_tok = sb("tk_bias_tok", [L, D])
        x_in = [sb(f"tk_x{p}", [2 * CIN, GB, L + 2]) for p in range(2)]
        pre = [sb(f"tk_pre{p}", [L, GB, D]) for p in range(2)]
        y = [sb(f"tk_y{p}", [L, GB, D]) for p in range(2)]
        z = [sb(f"tk_z{p}", [L, GB, D]) for p in range(2)]
        stats = [sb(f"tk_stats{p}", [L, GB, 6]) for p in range(2)]
        mv = [sb(f"tk_mv{p}", [L, GB, 2]) for p in range(2)]
        var_eps = [sb(f"tk_var_eps{p}", [L, GB]) for p in range(2)]
        rstd = [sb(f"tk_rstd{p}", [L, GB]) for p in range(2)]
        p_w = ps("tk_p_w", [128, 2, D])
        p_bias = ps("tk_p_bias", [L, D])
        p_y = [ps(f"tk_p_y{p}", [L, GB, D]) for p in range(2)]

        weights_in = sem("tk_weights_in")
        ident_zero = sem("tk_ident_zero")
        padded = sem("tk_padded")
        taps_scaled = sem("tk_taps_scaled")
        bias_col = sem("tk_bias_col")
        joined = sem("tk_joined")
        joined_sb = sem("tk_joined_sb")
        x_ready = [sem(f"tk_x_ready{p}") for p in range(2)]
        mm_done = sem("tk_mm_done")
        pre_ready = sem("tk_pre_ready")
        silu_done = sem("tk_silu_done")
        stats_done = sem("tk_stats_done")
        mv_done = sem("tk_mv_done")
        eps_added = sem("tk_eps_added")
        rstd_done = sem("tk_rstd_done")
        z_done = sem("tk_z_done")
        scaled = sem("tk_scaled")
        h_done = sem("tk_h_done")

        block = ctx.enter_context(nc.Block())

        @block.sync
        def _(sp):
            T.clear_old(sp)
            for dst, src in ((w_proj[:], t["w_proj"]), (w_pwT[:], t["w_pwT"]), (w_dw[:], t["w_dw"]),
                             (b_proj[:], t["b_proj"].unsqueeze(1)), (b_dw[:], t["b_dw"].unsqueeze(1)),
                             (b_pw[:], t["b_pw"].partition_broadcast(L)),
                             (gamma[:], t["gamma"].partition_broadcast(L)),
                             (beta[:], t["beta"].partition_broadcast(L))):
                sp.dma_start(dst, src).then_inc(weights_in, 16)

            def load(k, p):
                src = t["x"][bass.ds((2 * k + p) * GB, GB), :, :].rearrange("b c l -> c b l")
                sp.dma_start(x_in[p][0:CIN, :, 1:L + 1], src).then_inc(x_ready[p], 16)
                sp.dma_start(x_in[p][CIN:2 * CIN, :, 0:L - 1], src[:, :, 1:L]).then_inc(x_ready[p], 16)

            sp.wait_ge(padded, 4)
            load(0, 0)
            load(0, 1)
            with sp.Fori(1, NG // 2) as k:
                for p in range(2):
                    sp.wait_ge(mm_done, 2 * k + p - 1)
                    load(k, p)

        @block.gpsimd
        def _(pool):
            pool.memset(T.neg_half[:], -0.5)
            pool.memset(T.eps[:], EPS).then_inc(T.consts_done, 1)
            pool.memset(T.ident[:], 0.0).then_inc(ident_zero, 1)
            pool.wait_ge(ident_zero, 1)
            pool.affine_select(out=T.ident[:], in_=T.ident[:], compare_op=ALU.not_equal, fill=1.0,
                               base=0, pattern=[[-1, 128]], channel_multiplier=1).then_inc(T.consts_done, 1)
            pool.wait_ge(weights_in, 128)

            def rstd_of(k, p):
                g = 2 * k + p
                pool.wait_ge(mv_done, GB * (g + 1))
                pool.tensor_tensor(var_eps[p][:], mv[p][:, :, 1], T.eps[:], ALU.add).then_inc(eps_added, 1)
                pool.wait_ge(eps_added, g + 1)
                pool.tensor_tensor(rstd[p][:], var_eps[p][:], T.neg_half[:], ALU.pow).then_inc(rstd_done, 1)

            def scale_and_shift(k, p):
                g = 2 * k + p
                pool.wait_ge(z_done, g + 3)
                pool.tensor_tensor(z[p][:], z[p][:], over(gamma[:], GB), ALU.mult).then_inc(scaled, 1)
                pool.wait_ge(scaled, g + 1)
                pool.tensor_tensor(T.H[:, bass.ds(g * GB, GB), :], z[p][:], over(beta[:], GB),
                                   ALU.add).then_inc(h_done, 1)

            rstd_of(0, 0)
            with pool.Fori(0, NG // 2 - 1) as k:
                for p in range(2):
                    rstd_of(k + p, 1 - p)
                    scale_and_shift(k, p)
            rstd_of(NG // 2 - 1, 1)
            scale_and_shift(NG // 2 - 1, 0)
            scale_and_shift(NG // 2 - 1, 1)

        @block.tensor
        def _(pe):
            pe.wait_ge(weights_in, 128)
            pe.wait_ge(taps_scaled, 3)
            pe.matmul(p_w[0:CIN, 0, :], w_proj[:], w_pw_taps[:, 0, :], start=True, stop=True)
            pe.matmul(p_w[CIN:2 * CIN, 0, :], w_proj[:], w_pw_taps[:, 2, :], start=True, stop=True)
            pe.matmul(p_w[0:CIN, 1, :], w_proj[:], w_pw_taps[:, 1, :], start=True, stop=True)
            pe.wait_ge(bias_col, 4)
            pe.matmul(p_bias[:], conv_bias[:], w_pwT[:], start=True, stop=True).then_inc(joined, 1)
            pe.wait_ge(joined_sb, 3)
            with pe.Fori(0, NG // 2) as k:
                for p in range(2):
                    pe.wait_ge(x_ready[p], 32 * k + 32)
                    pe.wait_ge(pre_ready, 2 * k + p + 1)
                    for b in range(GB):
                        pe.matmul(p_y[p][:, b, :], x_in[p][:, b, 0:L], taps02[:], start=True, stop=False)
                        last = pe.matmul(p_y[p][:, b, :], x_in[p][0:CIN, b, 1:L + 1], tap1[:],
                                         start=False, stop=True)
                    last.then_inc(mm_done, 1)

        @block.scalar
        def _(act):
            with act.Fori(0, NG // 2) as k:
                for p in range(2):
                    act.wait_ge(pre_ready, 2 * k + p + 3)
                    act.wait_ge(z_done, 2 * k + p + 1)
                    act.activation(y[p][:], pre[p][:], ACT.Silu).then_inc(silu_done, 1)

        @block.vector
        def _(dve):
            for p in range(2):
                dve.memset(x_in[p][0:CIN, :, 0:1], 0.0)
                dve.memset(x_in[p][0:CIN, :, L + 1:L + 2], 0.0).then_inc(padded, 1)
                dve.memset(x_in[p][CIN:2 * CIN, :, L - 1:L + 2], 0.0).then_inc(padded, 1)
            dve.sem_inc(pre_ready, 2)
            dve.sem_inc(z_done, 2)
            dve.sem_inc(h_done, 2)
            dve.wait_ge(weights_in, 128)
            for j in range(3):
                dve.tensor_scalar(w_pw_taps[:, j, :], w_pwT[:], w_dw[:, j:j + 1], None,
                                  ALU.mult).then_inc(taps_scaled, 1)
            dve.tensor_scalar(edge[:, 0:3], w_dw[:], b_proj[:, 0:1], None, ALU.mult).then_inc(bias_col, 1)
            dve.wait_ge(bias_col, 1)
            dve.tensor_scalar(conv_bias[:], edge[:, 1:2].broadcast_to([D, L]), b_dw[:, 0:1], edge[:, 0:1],
                              ALU.add, ALU.add).then_inc(bias_col, 1)
            dve.wait_ge(bias_col, 2)
            dve.tensor_scalar(conv_bias[:, 0:1], conv_bias[:, 1:2], edge[:, 0:1], None,
                              ALU.subtract).then_inc(bias_col, 1)
            dve.wait_ge(bias_col, 3)
            dve.tensor_scalar(conv_bias[:, 0:L - 1], conv_bias[:, 0:L - 1], edge[:, 2:3], None,
                              ALU.add).then_inc(bias_col, 1)
            dve.wait_ge(joined, 1)
            dve.tensor_copy(taps02[:], p_w[:, 0, :]).then_inc(joined_sb, 1)
            dve.tensor_copy(tap1[:], p_w[0:CIN, 1, :]).then_inc(joined_sb, 1)
            dve.tensor_tensor(bias_tok[:], p_bias[:], b_pw[:], ALU.add).then_inc(joined_sb, 1)
            dve.wait_ge(joined_sb, 3)

            def add_bias(k, p):
                dve.wait_ge(mm_done, 2 * k + p + 1)
                dve.tensor_tensor(pre[p][:], p_y[p][:], over(bias_tok[:], GB), ALU.add).then_inc(pre_ready, 1)

            def moments(k, p):
                g = 2 * k + p
                dve.wait_ge(silu_done, g + 1)
                for b in range(GB):
                    dve.bn_stats(stats[p][:, b, :], y[p][:, b, :]).then_inc(stats_done, 1)
                T.wait_alone(dve, stats_done, GB * (g + 1))
                for b in range(GB):
                    dve.bn_aggr(mv[p][:, b, :], stats[p][:, b, :]).then_inc(mv_done, 1)

            def normalize(k, p):
                g = 2 * k + p
                dve.wait_ge(rstd_done, g + 1)
                dve.wait_ge(h_done, g + 1)
                for b in range(GB):
                    last = dve.tensor_scalar(z[p][:, b, :], y[p][:, b, :], mv[p][:, b, 0:1],
                                             rstd[p][:, b:b + 1], ALU.subtract, ALU.mult)
                last.then_inc(z_done, 1)

            add_bias(0, 0)
            add_bias(0, 1)
            moments(0, 0)
            with dve.Fori(0, NG // 2 - 1) as k:
                for p in range(2):
                    moments(k + p, 1 - p)
                    add_bias(k + 1, p)
                    normalize(k, p)
            moments(NG // 2 - 1, 1)
            normalize(NG // 2 - 1, 0)
            normalize(NG // 2 - 1, 1)


def stage_attention(T):
    nc, t, sem = T.nc, T.t, T.sem
    HALF = NH // 2
    NHF = 2 * GB
    with ExitStack() as ctx:
        def sb(name, shape, dt=F32):
            return ctx.enter_context(nc.sbuf_tensor(name, shape, dt))

        def ps(name, shape, dt=F32):
            return ctx.enter_context(nc.psum_tensor(name, shape, dt))

        w_qkvT = sb("at_w_qkvT", [D, 3, D])
        w_aggT = sb("at_w_aggT", [D, D])
        b_agg = sb("at_b_agg", [L, D])
        zeros = sb("at_zeros", [L, GT])
        head_mask = T.head_mask
        stats = sb("at_stats", [L, GB, 6])
        mv = sb("at_mv", [L, GB, 2])
        var_eps = sb("at_var_eps", [L, GB])
        rstd = sb("at_rstd", [L, GB])
        z = [sb(f"at_z{p}", [L, GB, D]) for p in range(2)]
        zT = [sb(f"at_zT{p}", [D, GB, L]) for p in range(2)]
        q_sb = [sb(f"at_q{p}", [D, GB, L]) for p in range(2)]
        k_sb = sb("at_k", [D, GB, L])
        k_heads = [sb(f"at_k_heads{p}", [D, NH, GB, L]) for p in range(2)]
        v_ones = [sb(f"at_v_ones{p}", [L, GB, NH, 32]) for p in range(2)]
        neg_top = sb("at_neg_top", [L, GB, NH])
        probs = [sb(f"at_probs{i}", [L, HALF, L]) for i in range(2)]
        probsT = [sb(f"at_probsT{i}", [L, HALF, L]) for i in range(2)]
        raw = sb("at_raw", [128, 4, L])
        inv_sum = sb("at_inv_sum", [L, GB, NH])
        heads_out = sb("at_heads_out", [L, GB, D])
        heads_outT = sb("at_heads_outT", [D, GB, L])
        p_s = [ps(f"at_p_s{i}", [128, 512]) for i in range(2)]
        p_st = [ps(f"at_p_st{i}", [L, HALF, L]) for i in range(2)]
        p_raw = ps("at_p_raw", [128, 512])
        p_o = ps("at_p_o", [128, 2, NH, 32])
        p_agg = ps("at_p_agg", [128, 512])
        p_q = ps("at_p_q", [128, 512])

        def tokens(bank, rows=L):
            return bank[0:rows, :].rearrange("p (b d) -> p b d", b=GB)

        def features(bank):
            return bank[:, 0:GT].rearrange("p (b l) -> p b l", b=GB)

        COPY_ACT = (2, 5, 7)
        COPY_DVE = tuple(f for f in range(NHF) if f not in COPY_ACT)

        def before(g, p, f, n):
            return (g, p, f - n) if f >= n else (g - 1, 1 - p, f - n + NHF)

        weights_in = sem("at_weights_in")
        cleared = sem("at_cleared")
        zeroed = sem("at_zeroed")
        pool_consts = sem("at_pool_consts")
        stats_done = sem("at_stats_done")
        mv_done = sem("at_mv_done")
        eps_added = sem("at_eps_added")
        rstd_done = sem("at_rstd_done")
        z_done = sem("at_z_done")
        zT_made = sem("at_zT_made")
        zT_kept = sem("at_zT_kept")
        q_made = sem("at_q_made")
        k_made = sem("at_k_made")
        v_made = sem("at_v_made")
        q_kept = sem("at_q_kept")
        k_kept = sem("at_k_kept")
        v_kept = sem("at_v_kept")
        k_masked = sem("at_k_masked")
        bias_added = sem("at_bias_added")
        s_made = sem("at_s_made")
        top_done = sem("at_top_done")
        turned = sem("at_turned")
        exp_done = sem("at_exp_done")
        kept_act = sem("at_kept_act")
        kept_dve = sem("at_kept_dve")
        pv_done = sem("at_pv_done")
        raw_kept = sem("at_raw_kept")
        o_turned = sem("at_o_turned")
        inv_done = sem("at_inv_done")
        out_done = sem("at_out_done")
        outT_made = sem("at_outT_made")
        outT_kept = sem("at_outT_kept")
        agg_made = sem("at_agg_made")
        h_done = sem("at_h_done")

        def wait_turned_kept(eng, g, f):
            done, fs = (kept_act, COPY_ACT) if f in COPY_ACT else (kept_dve, COPY_DVE)
            T.wait_alone(eng, done, len(fs) * g + fs.index(f) + 1)

        def copy_turned(eng, copy, g, f, done):
            T.wait_alone(eng, turned, NHF * g + f + 1)
            if at_least(g, 1) or f >= 2:
                T.wait_alone(eng, pv_done, NHF * g + f - 1)
            copy(probsT[f % 2][:], p_st[f % 2][:]).then_inc(done, 1)

        block = ctx.enter_context(nc.Block())

        @block.sync
        def _(sp):
            T.clear_old(sp)
            sp.dma_start(w_qkvT[:], t["w_qkvT"].rearrange("d (j e) -> d j e", j=3)).then_inc(weights_in, 16)
            sp.dma_start(w_aggT[:], t["w_aggT"]).then_inc(weights_in, 16)
            sp.dma_start(b_agg[:], t["b_agg"].partition_broadcast(L)).then_inc(weights_in, 16)
            sp.wait_ge(cleared, 1)
            cols = L * GB * NH
            for p in range(2):
                sp.dma_start(T.diagonals[p][OFFS[-1]:OFFS[-1] + L].rearrange("m n c -> m (n c)").rearrange(
                    "m (r c) -> m r c", c=GT), over(zeros[:], cols // GT)).then_inc(zeroed, 16)
            sp.wait_ge(zeroed, 32)

        @block.gpsimd
        def _(pool):
            pool.memset(head_mask[:], 1.0).then_inc(pool_consts, 1)
            pool.wait_ge(pool_consts, 1)
            pool.affine_select(out=head_mask[:], in_=head_mask[:], compare_op=ALU.is_ge, fill=0.0,
                               base=0, pattern=[[-DH, NH]], channel_multiplier=1).then_inc(pool_consts, 1)
            pool.wait_ge(pool_consts, 2)
            pool.affine_select(out=head_mask[:], in_=head_mask[:], compare_op=ALU.is_ge, fill=0.0,
                               base=DH - 1, pattern=[[DH, NH]], channel_multiplier=-1).then_inc(pool_consts, 1)
            pool.wait_ge(pool_consts, 3)

            def rstd_of(g):
                pool.wait_ge(mv_done, GB * (g + 1))
                pool.tensor_tensor(var_eps[:], mv[:, :, 1], T.eps[:], ALU.add).then_inc(eps_added, 1)
                pool.wait_ge(eps_added, g + 1)
                pool.tensor_tensor(rstd[:], var_eps[:], T.neg_half[:], ALU.pow).then_inc(rstd_done, 1)

            def mask_k(g, p):
                T.wait_alone(pool, k_kept, g + 1)
                if at_least(g, 2):
                    T.wait_alone(pool, s_made, NHF * (g - 1))
                for h in range(NH):
                    last = pool.tensor_scalar(k_heads[p][:, h], k_sb[:], head_mask[:, h:h + 1], 1.0, ALU.mult,
                                              ALU.mult)
                last.then_inc(k_masked, 1)

            def add_b_agg(g):
                rows = T.H[:, bass.ds(g * GB, GB), :]
                pool.wait_ge(z_done, g + 1)
                pool.tensor_tensor(rows, rows, over(b_agg[:], GB), ALU.add).then_inc(bias_added, 1)

            pool.wait_ge(weights_in, 48)
            rstd_of(0)
            rstd_of(1)
            mask_k(0, 0)
            add_b_agg(0)

            def turn(g, p):
                if below(g, NG - 2):
                    rstd_of(g + 2)
                if below(g, NG - 1):
                    mask_k(g + 1, 1 - p)
                    add_b_agg(g + 1)

            turn(0, 0)
            with pool.Fori(0, NG // 2 - 2) as k:
                turn(2 * k + 1, 1)
                turn(2 * k + 2, 0)
            turn(NG - 3, 1)
            turn(NG - 2, 0)
            turn(NG - 1, 1)

        @block.tensor
        def _(pe):
            pe.wait_ge(weights_in, 48)

            def z_transposes(g, p):
                T.wait_alone(pe, z_done, g + 1)
                if at_least(g, 1):
                    T.wait_alone(pe, q_kept, g)
                for b in range(GB):
                    last = pe.transpose(features(p_q)[:, b, :], z[p][:, b, :], T.ident[0:L, 0:L])
                last.then_inc(zT_made, 1)

            def queries(g, p):
                T.wait_alone(pe, zT_kept, g + 1)
                pe.matmul(features(p_q), w_qkvT[:, 0, :], zT[p][:], start=True, stop=True).then_inc(q_made, 1)

            def keys(g, p):
                if at_least(g, 3):
                    T.wait_alone(pe, h_done, g - 2)
                elif g >= 1:
                    pe.wait_ge(v_kept, g)
                pe.matmul(features(p_agg), w_qkvT[:, 1, :], zT[p][:], start=True, stop=True).then_inc(k_made, 1)

            def values(g, p):
                T.wait_alone(pe, k_kept, g + 1)
                for b in range(GB):
                    last = pe.matmul(tokens(p_agg)[:, b, :], zT[p][:, b, :], w_qkvT[:, 2, :],
                                     start=True, stop=True)
                last.then_inc(v_made, 1)

            def scores(g, p, f):
                b, half = f // 2, f % 2
                if f == 0:
                    T.wait_alone(pe, k_masked, g + 1)
                    T.wait_alone(pe, q_kept, g + 1)
                if at_least(g, 1) or f >= 2:
                    T.wait_alone(pe, exp_done, NHF * g + f - 1)
                pe.matmul(p_s[half][0:L, 0:HALF * L].rearrange("n (h m) -> n h m", h=HALF),
                          q_sb[p][:, b, :], k_heads[p][:, half * HALF:(half + 1) * HALF, b, :],
                          start=True, stop=True).then_inc(s_made, 1)

            def turn_probs(g, f):
                T.wait_alone(pe, exp_done, NHF * g + f + 1)
                if at_least(g, 1) or f >= 2:
                    wait_turned_kept(pe, *before(g, 0, f, 2)[0::2])
                for j in range(HALF):
                    last = pe.transpose(p_st[f % 2][:, j, :], probs[f % 2][:, j, :], T.ident[0:L, 0:L])
                last.then_inc(turned, 1)

            def times_v(g, p, f):
                b, half = f // 2, f % 2
                wait_turned_kept(pe, g, f)
                if f == 0:
                    T.wait_alone(pe, v_kept, g + 1)
                if f % 4 == 0 and (at_least(g, 1) or f >= 4):
                    T.wait_alone(pe, raw_kept, 2 * g + f // 4)
                for j in range(HALF):
                    last = pe.matmul(p_raw[32 * j:32 * j + 32, (f % 4) * L:(f % 4 + 1) * L],
                                     v_ones[p][:, b, half * HALF + j, :], probsT[half][:, j, :],
                                     start=True, stop=True)
                last.then_inc(pv_done, 1)

            def turn_sums(g, i):
                T.wait_alone(pe, raw_kept, 2 * g + i + 1)
                if at_least(g, 1) or i == 1:
                    T.wait_alone(pe, out_done, 2 * g + i)
                for b in range(2):
                    for half in range(2):
                        last = pe.transpose(p_o[0:L, b, half * HALF:(half + 1) * HALF, :].rearrange("n h d -> n (h d)"),
                                            raw[:, 2 * b + half, :], T.ident[:])
                last.then_inc(o_turned, 1)

            def out_transposes(g):
                T.wait_alone(pe, out_done, 2 * (g + 1))
                T.wait_alone(pe, v_kept, min(g + 3, NG) if isinstance(g, int) else g + 3)
                for b in range(GB):
                    last = pe.transpose(features(p_agg)[:, b, :], heads_out[:, b, :], T.ident[0:L, 0:L])
                last.then_inc(outT_made, 1)

            def aggregate(g):
                pe.wait_ge(outT_kept, g + 1)
                for b in range(GB):
                    last = pe.matmul(tokens(p_agg)[:, b, :], heads_outT[:, b, :], w_aggT[:],
                                     start=True, stop=True)
                last.then_inc(agg_made, 1)

            def turn(g, p):
                for f in range(NHF):
                    if here(g):
                        scores(g, p, f)
                    g1, _, f1 = before(g, p, f, 2)
                    if here(g1):
                        turn_probs(g1, f1)
                    g2, p2, f2 = before(g, p, f, 3)
                    if here(g2):
                        times_v(g2, p2, f2)
                    if here(g + 1):
                        if f == 0:
                            z_transposes(g + 1, 1 - p)
                        if f == 1:
                            queries(g + 1, 1 - p)
                            keys(g + 1, 1 - p)
                        if f == 2:
                            values(g + 1, 1 - p)
                    if here(g - 1):
                        if f == 3:
                            turn_sums(g - 1, 1)
                        if f == 5:
                            out_transposes(g - 1)
                        if f == 7:
                            aggregate(g - 1)
                    if here(g) and f == 7:
                        turn_sums(g, 0)

            z_transposes(0, 0)
            queries(0, 0)
            keys(0, 0)
            values(0, 0)
            turn(0, 0)
            turn(1, 1)
            with pe.Fori(1, NG // 2 - 1) as k:
                turn(2 * k, 0)
                turn(2 * k + 1, 1)
            turn(NG - 2, 0)
            turn(NG - 1, 1)
            turn(NG, 0)

        @block.scalar
        def _(act):
            def keep_zT(g, p):
                act.wait_ge(zT_made, g + 1)
                if at_least(g, 2):
                    act.wait_ge(v_made, g - 1)
                act.copy(zT[p][:], features(p_q)).then_inc(zT_kept, 1)

            def keep_q(g, p):
                act.wait_ge(q_made, g + 1)
                if at_least(g, 2):
                    act.wait_ge(s_made, NHF * (g - 1))
                act.mul(q_sb[p][:], features(p_q), -DH ** -0.5).then_inc(q_kept, 1)

            def keep_k(g):
                act.wait_ge(k_made, g + 1)
                if at_least(g, 1):
                    act.wait_ge(k_masked, g)
                act.copy(k_sb[:], features(p_agg)).then_inc(k_kept, 1)

            def keep_outT(g):
                act.wait_ge(outT_made, g + 1)
                if at_least(g, 1):
                    act.wait_ge(agg_made, g)
                act.copy(heads_outT[:], features(p_agg)).then_inc(outT_kept, 1)

            def exponentials(g, f):
                b, half = f // 2, f % 2
                act.wait_ge(top_done, NHF * g + f + 1)
                if at_least(g, 1) or f >= 2:
                    act.wait_ge(turned, NHF * g + f - 1)
                for j in range(HALF):
                    h = half * HALF + j
                    last = act.activation(probs[half][:, j, :], p_s[half][0:L, j * L:(j + 1) * L], ACT.Exp,
                                          bias=neg_top[:, b, h:h + 1], scale=-1.0)
                last.then_inc(exp_done, 1)

            def keep_raw(g, i):
                act.wait_ge(pv_done, NHF * g + 4 * (i + 1))
                if at_least(g, 1) or i == 1:
                    act.wait_ge(o_turned, 2 * g + i)
                act.copy(raw[:].rearrange("r u n -> r (u n)"), p_raw[:, 0:4 * L]).then_inc(raw_kept, 1)

            def turn(g, p):
                for f in range(NHF):
                    if here(g):
                        exponentials(g, f)
                    g1, _, f1 = before(g, p, f, 2)
                    if here(g1) and f1 in COPY_ACT:
                        copy_turned(act, act.copy, g1, f1, kept_act)
                    if here(g - 1) and f == 2:
                        keep_raw(g - 1, 1)
                    if here(g) and f == 6:
                        keep_raw(g, 0)
                    if here(g + 1):
                        if f == 0:
                            keep_zT(g + 1, 1 - p)
                        if f == 1:
                            keep_q(g + 1, 1 - p)
                            keep_k(g + 1)
                    if here(g - 1) and f == 6:
                        keep_outT(g - 1)

            keep_zT(0, 0)
            keep_q(0, 0)
            keep_k(0)
            turn(0, 0)
            turn(1, 1)
            with act.Fori(1, NG // 2 - 1) as k:
                turn(2 * k, 0)
                turn(2 * k + 1, 1)
            turn(NG - 2, 0)
            turn(NG - 1, 1)
            turn(NG, 0)

        @block.vector
        def _(dve):
            for p in range(2):
                dve.memset(v_ones[p][:], 1.0)
            dve.memset(zeros[:], 0.0).then_inc(cleared, 1)

            def moments(g):
                for b in range(GB):
                    dve.bn_stats(stats[:, b, :], T.H[:, g * GB + b, :]).then_inc(stats_done, 1)
                T.wait_alone(dve, stats_done, GB * (g + 1))
                for b in range(GB):
                    dve.bn_aggr(mv[:, b, :], stats[:, b, :]).then_inc(mv_done, 1)

            def normalize(g, p):
                T.wait_alone(dve, rstd_done, g + 1)
                if at_least(g, 2):
                    T.wait_alone(dve, zT_made, g - 1)
                for b in range(GB):
                    last = dve.tensor_scalar(z[p][:, b, :], T.H[:, g * GB + b, :], mv[:, b, 0:1],
                                             rstd[:, b:b + 1], ALU.subtract, ALU.mult)
                last.then_inc(z_done, 1)

            def keep_v(g, p):
                dve.wait_ge(v_made, g + 1)
                if at_least(g, 2):
                    dve.wait_ge(pv_done, NHF * (g - 1))
                dve.tensor_copy(v_ones[p][:, :, :, 0:DH],
                                p_agg[0:L, :].rearrange("p (b h d) -> p b h d", b=GB, h=NH)).then_inc(v_kept, 1)

            def least(g, f):
                b, half = f // 2, f % 2
                dve.wait_ge(s_made, NHF * g + f + 1)
                dve.tensor_reduce(neg_top[:, b, half * HALF:(half + 1) * HALF],
                                  p_s[half][0:L, 0:HALF * L].rearrange("n (h m) -> n h m", h=HALF),
                                  AX_X, ALU.min).then_inc(top_done, 1)

            def divide(g, i):
                dve.wait_ge(o_turned, 2 * g + i + 1)
                dve.reciprocal(inv_sum[:, 2 * i:2 * i + 2, :], p_o[0:L, :, :, DH]).then_inc(inv_done, 1)
                dve.wait_ge(inv_done, 2 * g + i + 1)
                if at_least(g, 1):
                    dve.wait_ge(outT_made, g)
                dve.tensor_tensor(heads_out[:, 2 * i:2 * i + 2, :].rearrange("n b (h d) -> n b h d", h=NH),
                                  p_o[0:L, :, :, 0:DH], over(inv_sum[:, 2 * i:2 * i + 2, :], DH, 3),
                                  ALU.mult).then_inc(out_done, 1)

            def add_to_h(g):
                dve.wait_ge(agg_made, g + 1)
                dve.wait_ge(bias_added, g + 1)
                rows = T.H[:, bass.ds(g * GB, GB), :]
                dve.tensor_tensor(rows, rows, tokens(p_agg), ALU.add).then_inc(h_done, 1)

            def turn(g, p):
                for f in range(NHF):
                    if here(g):
                        least(g, f)
                    g1, _, f1 = before(g, p, f, 2)
                    if here(g1) and f1 in COPY_DVE:
                        copy_turned(dve, dve.tensor_copy, g1, f1, kept_dve)
                    if here(g + 2):
                        if f == 1:
                            moments(g + 2)
                        if f == 5:
                            normalize(g + 2, p)
                    if here(g - 1):
                        if f == 0:
                            divide(g - 1, 0)
                        if f == 4:
                            divide(g - 1, 1)
                    if here(g - 2) and f == 0:
                        add_to_h(g - 2)
                    if here(g + 1) and f == 3:
                        keep_v(g + 1, 1 - p)

            for g in range(2):
                moments(g)
                normalize(g, g)
            keep_v(0, 0)
            turn(0, 0)
            turn(1, 1)
            with dve.Fori(1, NG // 2 - 1) as k:
                turn(2 * k, 0)
                turn(2 * k + 1, 1)
            turn(NG - 2, 0)
            turn(NG - 1, 1)
            turn(NG, 0)
            add_to_h(NG - 1)


def stage_router_logits(T):
    nc, t, sem = T.nc, T.t, T.sem
    with ExitStack() as ctx:
        def sb(name, shape, dt=F32):
            return ctx.enter_context(nc.sbuf_tensor(name, shape, dt))

        def ps(name, shape, dt=F32):
            return ctx.enter_context(nc.psum_tensor(name, shape, dt))

        w_router = sb("rl_w_router", [D, E])
        stats = [sb(f"rl_stats{p}", [L, GB, 6]) for p in range(2)]
        mv = [sb(f"rl_mv{p}", [L, GB, 2]) for p in range(2)]
        var_eps = [sb(f"rl_var_eps{p}", [L, GB]) for p in range(2)]
        rstd = [sb(f"rl_rstd{p}", [L, GB]) for p in range(2)]
        z = [sb(f"rl_z{p}", [L, GB, D]) for p in range(2)]
        zT = [sb(f"rl_zT{p}", [D, GB, L]) for p in range(2)]
        logits = [sb(f"rl_logits{p}", [E, GT]) for p in range(2)]
        p_zT = [ps(f"rl_p_zT{p}", [D, GB, L]) for p in range(2)]
        p_logits = [ps(f"rl_p_logits{p}", [E, GT]) for p in range(2)]

        weights_in = sem("rl_weights_in")
        stats_done = sem("rl_stats_done")
        mv_done = sem("rl_mv_done")
        eps_added = sem("rl_eps_added")
        rstd_done = sem("rl_rstd_done")
        z_done = sem("rl_z_done")
        z_stored = [sem(f"rl_z_stored{p}") for p in range(2)]
        zT_made = sem("rl_zT_made")
        zT_kept = sem("rl_zT_kept")
        logits_made = sem("rl_logits_made")
        logits_kept = sem("rl_logits_kept")
        logits_stored = [sem(f"rl_logits_stored{p}") for p in range(2)]
        h_stored = sem("rl_h_stored")

        block = ctx.enter_context(nc.Block())

        @block.sync
        def _(sp):
            T.clear_old(sp)
            sp.dma_start(w_router[:], t["w_router"]).then_inc(weights_in, 16)
            sp.dma_start(T.h_rows.rearrange("(b l) d -> l b d", l=L), T.H[:]).then_inc(h_stored, 16)
            z_rows = T.z_rows.rearrange("(b l) c -> l b c", l=L)

            def store_z(g, p):
                sp.wait_ge(z_done, g + 1)
                sp.dma_start(z_rows[:, bass.ds(g * GB, GB), 0:D], z[p][:]).then_inc(z_stored[p], 16)

            def store_logits(g, p):
                sp.wait_ge(logits_kept, g + 1)
                sp.dma_start(T.logits[:, bass.ds(g * GT, GT)], logits[p][:]).then_inc(logits_stored[p], 16)

            store_z(0, 0)
            store_z(1, 1)
            with sp.Fori(1, NG // 2) as k:
                for p in range(2):
                    store_z(2 * k + p, p)
                    store_logits(2 * k + p - 2, p)
            store_logits(NG - 2, 0)
            store_logits(NG - 1, 1)
            sp.wait_ge(h_stored, 16)
            for p in range(2):
                sp.wait_ge(z_stored[p], 16 * (NG // 2))
                sp.wait_ge(logits_stored[p], 16 * (NG // 2) + 16)

        @block.gpsimd
        def _(pool):
            with pool.Fori(0, NG // 2) as k:
                for p in range(2):
                    g = 2 * k + p
                    pool.wait_ge(mv_done, GB * (g + 1))
                    pool.tensor_tensor(var_eps[p][:], mv[p][:, :, 1], T.eps[:], ALU.add).then_inc(eps_added, 1)
                    pool.wait_ge(eps_added, g + 1)
                    pool.tensor_tensor(rstd[p][:], var_eps[p][:], T.neg_half[:], ALU.pow).then_inc(rstd_done, 1)

        @block.tensor
        def _(pe):
            pe.wait_ge(weights_in, 16)

            def transposes(g, p):
                T.wait_alone(pe, z_done, g + 1)
                if at_least(g, 2):
                    T.wait_alone(pe, zT_kept, g - 1)
                for b in range(GB):
                    last = pe.transpose(p_zT[p][:, b, :], z[p][:, b, :], T.ident[0:L, 0:L])
                last.then_inc(zT_made, 1)

            def route(g, p):
                T.wait_alone(pe, zT_kept, g + 1)
                if at_least(g, 2):
                    T.wait_alone(pe, logits_kept, g - 1)
                pe.matmul(p_logits[p][:], w_router[:], zT[p][:], start=True, stop=True).then_inc(logits_made, 1)

            transposes(0, 0)
            transposes(1, 1)
            route(0, 0)
            with pe.Fori(1, NG // 2) as k:
                transposes(2 * k, 0)
                route(2 * k - 1, 1)
                transposes(2 * k + 1, 1)
                route(2 * k, 0)
            route(NG - 1, 1)

        @block.scalar
        def _(act):
            with act.Fori(0, NG // 2) as k:
                for p in range(2):
                    act.wait_ge(zT_made, 2 * k + p + 1)
                    act.wait_ge(logits_made, 2 * k + p + 1)
                    act.copy(zT[p][:], p_zT[p][:]).then_inc(zT_kept, 1)

        @block.vector
        def _(dve):
            dve.sem_inc(logits_made, 2)
            for p in range(2):
                dve.sem_inc(logits_stored[p], 16)

            def moments(g, p):
                for b in range(GB):
                    dve.bn_stats(stats[p][:, b, :], T.H[:, g * GB + b, :]).then_inc(stats_done, 1)
                T.wait_alone(dve, stats_done, GB * (g + 1))
                for b in range(GB):
                    dve.bn_aggr(mv[p][:, b, :], stats[p][:, b, :]).then_inc(mv_done, 1)

            def normalize(g, p, w):
                T.wait_alone(dve, rstd_done, g + 1)
                if at_least(g, 2):
                    T.wait_alone(dve, zT_made, g - 1)
                    T.wait_alone(dve, z_stored[p], 16 * w)
                for b in range(GB):
                    last = dve.tensor_scalar(z[p][:, b, :], T.H[:, g * GB + b, :], mv[p][:, b, 0:1],
                                             rstd[p][:, b:b + 1], ALU.subtract, ALU.mult)
                last.then_inc(z_done, 1)

            def keep_logits(g, p, w):
                dve.wait_ge(logits_made, g + 3)
                dve.wait_ge(logits_stored[p], 16 * w + 16)
                dve.tensor_copy(logits[p][:], p_logits[p][:]).then_inc(logits_kept, 1)

            moments(0, 0)
            moments(1, 1)
            normalize(0, 0, 0)
            moments(2, 0)
            normalize(1, 1, 0)
            moments(3, 1)
            with dve.Fori(1, NG // 2 - 1) as k:
                for p in range(2):
                    normalize(2 * k + p, p, k)
                    moments(2 * k + p + 2, p)
                    keep_logits(2 * k + p - 2, p, k - 1)
            for p in range(2):
                normalize(NG - 2 + p, p, NG // 2 - 1)
                keep_logits(NG - 4 + p, p, NG // 2 - 2)
            keep_logits(NG - 2, 0, NG // 2 - 1)
            keep_logits(NG - 1, 1, NG // 2 - 1)


def stage_choose(T):
    nc, t, sem = T.nc, T.t, T.sem
    R = 128 // E
    C = N // R
    assert C == GT
    LO = 32
    HI = CAP // LO
    tiles = E * CAP // 128
    PB = 8
    NCH = B // PB
    STEPS = 16
    with ExitStack() as ctx:
        def sb(name, shape, dt=F32):
            return ctx.enter_context(nc.sbuf_tensor(name, shape, dt))

        def ps(name, shape, dt=F32):
            return ctx.enter_context(nc.psum_tensor(name, shape, dt))

        logit = sb("ch_logit", [128, C])
        u = sb("ch_u", [128, C])
        weight = sb("ch_weight", [128, C])
        same = sb("ch_same", [128, 128])
        before = sb("ch_before", [128, 128])
        ones = sb("ch_ones", [128, C])
        scratch = sb("ch_scratch", [128, C])
        lower = sb("ch_lower", [128, C])
        equal = sb("ch_equal", [128, C])
        tied = sb("ch_tied", [128, C])
        taken = sb("ch_taken", [128, C])
        count = sb("ch_count", [128, C])
        slot = sb("ch_slot", [128, C])
        row_max = sb("ch_row_max", [128, 1])
        max_e = sb("ch_max_e", [1, E])
        max_row = sb("ch_max_row", [1, E, R])
        top = sb("ch_top", [128, 1])
        row_sum = sb("ch_row_sum", [128, 1])
        inv_sum = sb("ch_inv_sum", [128, 1])
        kth = sb("ch_kth", [128, 1], I32)
        bit = sb("ch_bit", [128, 1])
        bits = sb("ch_bits", [128, STEPS + 1, 3])
        bits_int = sb("ch_bits_int", [128, STEPS + 1, 3], I32)
        worth = sb("ch_worth", [128, STEPS])
        below_cap = sb("ch_below_cap", [128, 3])
        gain_f = sb("ch_gain_f", [128, 1])
        with_next = sb("ch_with_next", [128, 3], I32)
        trial = sb("ch_trial", [128, 3], I32)
        gain = sb("ch_gain", [128, 1], I32)
        row_count = sb("ch_row_count", [128, 3])
        tie_room = sb("ch_tie_room", [128, 1])
        ahead = sb("ch_ahead", [128, 2])
        weightT = sb("ch_weightT", [L, B, E])
        slot_int = sb("ch_slot_int", [L, GB, 128], I32)
        hi_int = sb("ch_hi_int", [L, GB, 128], I32)
        lo_int = sb("ch_lo_int", [L, GB, 128], I32)
        hi = sb("ch_hi", [L, B, E], BF16)
        lo = sb("ch_lo", [L, B, E], BF16)
        iota = sb("ch_iota", [L, LO], BF16)
        iota_int = sb("ch_iota_int", [L, LO], I32)
        seq_no = sb("ch_seq_no", [L, B, E], BF16)
        seq_no_int = sb("ch_seq_no_int", [L, B, E], I32)
        tok_no = sb("ch_tok_no", [L, 1])
        tok_no_int = sb("ch_tok_no_int", [L, 1], I32)
        hot_hi = [sb(f"ch_hot_hi{p}", [L, PB * E, HI], BF16) for p in range(2)]
        hot_lo = [sb(f"ch_hot_lo{p}", [L, PB * E, LO], BF16) for p in range(2)]
        numbers = [sb(f"ch_numbers{p}", [L, PB * E, 2, LO], BF16) for p in range(2)]
        zeros = sb("ch_zeros", [L, 2 * LO], BF16)
        rows_f = sb("ch_rows_f", [128, E // 4, LO])
        rows_t = sb("ch_rows_t", [tiles, 128])
        p_small = ps("ch_p_small", [128, 512])
        p_tot = ps("ch_p_tot", [128, 3])
        p_slot = ps("ch_p_slot", [L, GB, 128])
        p_weight = ps("ch_p_weight", [L, GB, 128])
        p_chosen = ps("ch_p_chosen", [128, tiles])
        p_rows = [ps(f"ch_p_rows{i}", [128, 2, LO]) for i in range(E // 4)]

        loaded = sem("ch_loaded")
        consts = sem("ch_consts")
        small = sem("ch_small")
        max_made = sem("ch_max_made")
        max_spread = sem("ch_max_spread")
        u_done = sem("ch_u_done")
        exp_done = sem("ch_exp_done")
        sum_made = sem("ch_sum_made")
        weight_done = sem("ch_weight_done")
        trial_done = sem("ch_trial_done")
        counted = sem("ch_counted")
        total_made = sem("ch_total_made")
        gain_done = sem("ch_gain_done")
        kth_done = sem("ch_kth_done")
        bit_done = sem("ch_bit_done")
        next_bits = sem("ch_next_bits")
        next_done = sem("ch_next_done")
        gain_f_done = sem("ch_gain_f_done")
        marked = sem("ch_marked")
        offsets_made = sem("ch_offsets_made")
        slot_done = sem("ch_slot_done")
        turned = sem("ch_turned")
        weightT_kept = sem("ch_weightT_kept")
        parts_done = sem("ch_parts_done")
        hot_done = sem("ch_hot_done")
        lo_hot_done = sem("ch_lo_hot_done")
        tok_numbered = sem("ch_tok_numbered")
        seq_numbered = sem("ch_seq_numbered")
        chunk_used = sem("ch_chunk_used")
        rows_made = sem("ch_rows_made")
        rows_out = sem("ch_rows_out")
        rows_back = sem("ch_rows_back")
        rows_turned = sem("ch_rows_turned")
        chosen_done = sem("ch_chosen_done")
        weights_stored = sem("ch_weights_stored")

        block = ctx.enter_context(nc.Block())

        @block.sync
        def _(sp):
            T.clear_old(sp)
            sp.dma_start(logit[:], T.logits.rearrange("e (r c) -> (e r) c", r=R)).then_inc(loaded, 16)
            sp.wait_ge(weightT_kept, 1)
            sp.dma_start(T.z_rows.rearrange("(b l) c -> l b c", l=L)[:, :, D:D + E],
                         weightT[:]).then_inc(weights_stored, 16)
            sp.wait_ge(slot_done, 1 + E // 4)
            sp.dma_start(T.chosen_rows.rearrange("(g p c) -> p g c", p=128, c=LO), rows_f[:]).then_inc(rows_out, 16)
            sp.wait_ge(rows_out, 16)
            sp.dma_start(rows_t[:], T.chosen_rows.rearrange("(t p) -> t p", p=128)).then_inc(rows_back, 16)
            sp.wait_ge(weights_stored, 16)

        @block.gpsimd
        def _(pool):
            pool.memset(same[:], 1.0).then_inc(consts, 1)
            pool.wait_ge(consts, 1)
            sameb = same[:].rearrange("p (e r) -> p e r", e=E)
            pool.affine_select(out=sameb, in_=sameb, compare_op=ALU.is_ge, fill=0.0, base=0,
                               pattern=[[-R, E], [0, R]], channel_multiplier=1).then_inc(consts, 1)
            pool.wait_ge(consts, 2)
            pool.affine_select(out=sameb, in_=sameb, compare_op=ALU.is_ge, fill=0.0, base=R - 1,
                               pattern=[[R, E], [0, R]], channel_multiplier=-1).then_inc(consts, 1)
            pool.wait_ge(consts, 3)
            pool.affine_select(out=before[:], in_=same[:], compare_op=ALU.is_gt, fill=0.0, base=0,
                               pattern=[[1, 128]], channel_multiplier=-1).then_inc(consts, 1)
            pool.iota(iota_int[:], pattern=[[1, LO]], base=0, channel_multiplier=0).then_inc(consts, 1)
            pool.iota(seq_no_int[:], pattern=[[1, B], [0, E]], base=0, channel_multiplier=0).then_inc(consts, 1)
            pool.iota(tok_no_int[:], pattern=[[0, 1]], base=0, channel_multiplier=1).then_inc(consts, 1)
            pool.memset(zeros[:], 0.0)
            pool.wait_ge(consts, 7)
            pool.tensor_copy(iota[:], iota_int[:]).then_inc(consts, 1)
            pool.tensor_copy(seq_no[:], seq_no_int[:]).then_inc(consts, 1)
            pool.tensor_copy(tok_no[:], tok_no_int[:]).then_inc(consts, 1)
            pool.wait_ge(consts, 10)

            def number_sequences(c, p):
                T.wait_alone(pool, lo_hot_done, c + 1)
                T.wait_alone(pool, chunk_used, c + 1)
                pool.tensor_tensor(numbers[p][:, :, 1, :], hot_lo[p][:],
                                   over(seq_no[:, bass.ds(c * PB, PB), :].rearrange("l b e -> l (b e)"), LO, 2),
                                   ALU.mult).then_inc(seq_numbered, 1)

            with pool.Fori(0, NCH // 2) as k:
                for p in range(2):
                    number_sequences(2 * k + p, p)

        @block.tensor
        def _(pe):
            pe.wait_ge(small, 1)
            pe.matmul(p_small[0:1, 0:128], row_max[:], T.ident[:], start=True, stop=True).then_inc(max_made, 1)
            pe.wait_ge(small, 3)
            pe.matmul(p_small[:, 128:129], max_row[:].rearrange("o e r -> o (e r)"), ones[0:1, 0:1],
                      start=True, stop=True).then_inc(max_spread, 1)
            pe.wait_ge(consts, 10)
            pe.wait_ge(exp_done, 1)
            pe.matmul(p_small[:, 129:130], same[:], row_sum[:], start=True, stop=True).then_inc(sum_made, 1)
            with pe.Fori(0, STEPS) as i:
                T.wait_alone(pe, counted, i + 1)
                pe.matmul(p_tot[:], same[:], row_count[:], start=True, stop=True).then_inc(total_made, 1)
            pe.wait_ge(marked, 1)
            pe.matmul(p_tot[:, 0:1], same[:], row_count[:, 0:1], start=True, stop=True).then_inc(offsets_made, 1)
            pe.wait_ge(marked, 3)
            pe.matmul(p_small[:, 130:131], before[:], count[:, C - 1:C], start=True, stop=True).then_inc(offsets_made, 1)
            pe.wait_ge(weight_done, 1)
            for i in range(GB):
                last = pe.transpose(p_weight[:, i, :], weight[:, i * L:(i + 1) * L], T.ident[:])
            last.then_inc(turned, 1)
            pe.wait_ge(marked, 6)
            pe.matmul(p_small[:, 131:132], before[:], count[:, C - 1:C], start=True, stop=True).then_inc(offsets_made, 1)
            pe.wait_ge(slot_done, 1)
            for i in range(GB):
                last = pe.transpose(p_slot[:, i, :], slot[:, i * L:(i + 1) * L], T.ident[:])
            last.then_inc(turned, 1)

            def sums(lhsT, rhs, e, **flags):
                q = e % 4
                return pe.matmul(p_rows[e // 4][HI * q:HI * (q + 1), :, :].rearrange("h s c -> h (s c)"), lhsT, rhs,
                                 skip_group_check=True, **flags)

            for e in range(E):
                sums(zeros[:, 0:HI], zeros[:], e, start=True, stop=False)
            with pe.Fori(0, NCH // 2) as k:
                for p in range(2):
                    c = 2 * k + p
                    T.wait_alone(pe, hot_done, c + 1)
                    T.wait_alone(pe, tok_numbered, c + 1)
                    T.wait_alone(pe, seq_numbered, c + 1)
                    for b in range(PB):
                        for e in range(E):
                            i = b * E + e
                            last = sums(hot_hi[p][:, i, :], numbers[p][:, i, :, :].rearrange("l s c -> l (s c)"), e,
                                        start=False, stop=False)
                    last.then_inc(chunk_used, 1)
            for e in range(E):
                last = sums(zeros[:, 0:HI], zeros[:], e, start=False, stop=True)
            last.then_inc(rows_made, 1)
            pe.wait_ge(rows_back, 16)
            pe.transpose(p_chosen[:], rows_t[:], T.ident[0:tiles, 0:tiles]).then_inc(rows_turned, 1)

        @block.scalar
        def _(act):
            act.wait_ge(u_done, 1)
            act.activation(weight[:], u[:], ACT.Exp, scale=-1.0, accum_out=row_sum[:]).then_inc(exp_done, 1)
            act.wait_ge(consts, 10)

            def number_tokens(c, p):
                act.wait_ge(lo_hot_done, c + 1)
                act.wait_ge(chunk_used, c + 1)
                act.activation(numbers[p][:, :, 0, :], hot_lo[p][:], ACT.Copy, scale=tok_no[:, 0:1]).then_inc(tok_numbered, 1)

            with act.Fori(0, NCH // 2) as k:
                for p in range(2):
                    number_tokens(2 * k + p, p)

        @block.vector
        def _(dve):
            dve.sem_inc(chunk_used, 2)
            dve.memset(ones[:], 1.0).then_inc(bit_done, 1)
            dve.memset(kth[:], 0).then_inc(kth_done, 1)
            dve.memset(gain[:], 0).then_inc(gain_done, 1)
            dve.memset(bits[:], 1.0).then_inc(next_bits, 1)
            dve.wait_ge(next_bits, 1)
            for i in range(STEPS - 1):
                low = float(2 ** (29 - 2 * i))
                for j in range(3):
                    dve.memset(bits[:, i, j:j + 1], low * (j + 1))
                dve.memset(worth[:, i:i + 1], low)
            dve.memset(worth[:, STEPS - 1:STEPS], 1.0 / 3.0).then_inc(next_bits, 1)
            dve.wait_ge(next_bits, 2)
            dve.tensor_copy(bits_int[:], bits[:]).then_inc(bit_done, 1)
            dve.wait_ge(bit_done, 2)
            dve.tensor_copy(trial[:], bits_int[:, 0, :]).then_inc(trial_done, 1)
            dve.wait_ge(loaded, 16)
            dve.tensor_reduce(row_max[:], logit[:], AX_X, ALU.max).then_inc(small, 1)
            dve.wait_ge(max_made, 1)
            dve.tensor_reduce(max_e[:], p_small[0:1, 0:128].rearrange("o (e r) -> o e r", e=E), AX_X,
                              ALU.max).then_inc(small, 1)
            dve.wait_ge(small, 2)
            dve.tensor_copy(max_row[:], over(max_e[:], R, 2)).then_inc(small, 1)
            dve.wait_ge(max_spread, 1)
            dve.tensor_copy(top[:], p_small[:, 128:129]).then_inc(small, 1)
            dve.wait_ge(small, 4)
            dve.tensor_scalar(u[:], logit[:], -1.0, top[:, 0:1], ALU.mult, ALU.add).then_inc(u_done, 1)
            dve.wait_ge(sum_made, 1)
            dve.reciprocal(inv_sum[:], p_small[:, 129:130]).then_inc(small, 1)
            dve.wait_ge(small, 5)
            dve.tensor_scalar(weight[:], weight[:], inv_sum[:, 0:1], None, ALU.mult).then_inc(weight_done, 1)

            with dve.Fori(0, STEPS) as i:
                T.wait_alone(dve, trial_done, i + 1)
                for j in range(3):
                    last = dve.tensor_scalar((scratch, lower, equal)[j][:], u[:], trial[:, j:j + 1].bitcast(F32), None, ALU.is_lt, ALU.add,
                                             accum_out=row_count[:, j:j + 1])
                last.then_inc(counted, 1)
                dve.tensor_tensor(kth[:], kth[:], gain[:], ALU.bitwise_or).then_inc(kth_done, 1)
                dve.tensor_copy(bit[:], worth[:, bass.ds(i, 1)]).then_inc(bit_done, 1)
                dve.wait_ge(kth_done, i + 2)
                dve.tensor_tensor(with_next[:], kth[:].broadcast_to([128, 3]),
                                  bits_int[:, bass.ds(i + 1, 1), :].rearrange("p o j -> p (o j)"), ALU.bitwise_or
                                  ).then_inc(next_done, 1)
                dve.wait_ge(bit_done, i + 3)
                dve.wait_ge(total_made, i + 1)
                dve.tensor_scalar(below_cap[:], p_tot[:], CAP - 0.5, bit[:, 0:1], ALU.is_lt, ALU.mult).then_inc(gain_f_done, 1)
                dve.wait_ge(gain_f_done, 2 * i + 1)
                dve.tensor_reduce(gain_f[:], below_cap[:], AX_X, ALU.add).then_inc(gain_f_done, 1)
                dve.wait_ge(gain_f_done, 2 * i + 2)
                dve.tensor_copy(gain[:], gain_f[:]).then_inc(gain_done, 1)
                dve.wait_ge(next_done, i + 1)
                dve.wait_ge(gain_done, i + 2)
                dve.tensor_tensor(trial[:], with_next[:], gain[:].broadcast_to([128, 3]), ALU.bitwise_or
                                  ).then_inc(trial_done, 1)

            dve.tensor_tensor(kth[:], kth[:], gain[:], ALU.bitwise_or).then_inc(kth_done, 1)
            dve.wait_ge(kth_done, STEPS + 2)
            kth_f = kth[:].bitcast(F32)
            dve.tensor_scalar(lower[:], u[:], kth_f, None, ALU.is_lt, ALU.add, accum_out=row_count[:, 0:1]).then_inc(marked, 1)
            dve.tensor_scalar(equal[:], u[:], kth_f, None, ALU.is_equal).then_inc(marked, 1)
            dve.wait_ge(marked, 2)
            dve.tensor_tensor_scan(count[:], ones[:], equal[:], 0.0, ALU.mult, ALU.add).then_inc(marked, 1)
            dve.wait_ge(offsets_made, 2)
            dve.tensor_copy(ahead[:, 0:1], p_small[:, 130:131]).then_inc(marked, 1)
            dve.wait_ge(marked, 4)
            dve.tensor_tensor(tie_room[:], p_tot[:, 0:1], ahead[:, 0:1], ALU.add).then_inc(small, 1)
            dve.wait_ge(small, 6)
            dve.tensor_scalar(tie_room[:], tie_room[:], -1.0, float(CAP), ALU.mult, ALU.add).then_inc(small, 1)
            dve.wait_ge(small, 7)
            dve.scalar_tensor_tensor(out=tied[:], in0=count[:], scalar=tie_room[:, 0:1], in1=equal[:],
                                     op0=ALU.is_le, op1=ALU.mult).then_inc(small, 1)
            dve.wait_ge(small, 8)
            dve.tensor_tensor(taken[:], lower[:], tied[:], ALU.add).then_inc(marked, 1)
            dve.wait_ge(marked, 5)
            dve.tensor_tensor_scan(count[:], ones[:], taken[:], 0.0, ALU.mult, ALU.add).then_inc(marked, 1)
            dve.wait_ge(offsets_made, 3)
            dve.tensor_copy(ahead[:, 1:2], p_small[:, 131:132]).then_inc(marked, 1)
            dve.wait_ge(marked, 7)
            dve.scalar_tensor_tensor(out=slot[:], in0=count[:], scalar=ahead[:, 1:2], in1=taken[:],
                                     op0=ALU.add, op1=ALU.mult).then_inc(marked, 1)
            dve.wait_ge(marked, 8)
            dve.tensor_scalar(slot[:], slot[:], -1.0, None, ALU.add).then_inc(slot_done, 1)
            dve.wait_ge(turned, 1)

            def by_sequence(tile):
                return tile[:].rearrange("l (r i) e -> l i e r", i=GB)

            def by_group(tile):
                return tile.rearrange("l i (e r) -> l i e r", e=E)

            dve.tensor_copy(by_sequence(weightT), by_group(p_weight[:])).then_inc(weightT_kept, 1)
            dve.wait_ge(turned, 2)
            dve.tensor_copy(slot_int[:], p_slot[:]).then_inc(parts_done, 1)
            dve.wait_ge(parts_done, 1)
            dve.tensor_scalar(hi_int[:], slot_int[:], 5, None, ALU.arith_shift_right).then_inc(parts_done, 1)
            dve.tensor_scalar(lo_int[:], slot_int[:], LO - 1, None, ALU.bitwise_and).then_inc(parts_done, 1)
            dve.wait_ge(parts_done, 3)
            dve.tensor_copy(by_sequence(hi), by_group(hi_int[:])).then_inc(parts_done, 1)
            dve.tensor_copy(by_sequence(lo), by_group(lo_int[:])).then_inc(parts_done, 1)
            dve.wait_ge(parts_done, 5)
            dve.wait_ge(consts, 10)

            def one_hot(c, p):
                T.wait_alone(dve, chunk_used, c + 1)
                pairs = PB * E

                def of(x):
                    return over(x[:, bass.ds(c * PB, PB), :].rearrange("l b e -> l (b e)"), LO, 2)

                dve.tensor_tensor(hot_lo[p][:], over(iota[:], pairs), of(lo), ALU.is_equal).then_inc(lo_hot_done, 1)
                dve.tensor_tensor(hot_hi[p][:], over(iota[:], pairs), of(hi), ALU.is_equal).then_inc(hot_done, 1)

            with dve.Fori(0, NCH // 2) as k:
                for p in range(2):
                    one_hot(2 * k + p, p)
            dve.wait_ge(rows_made, 1)
            for i in range(E // 4):
                dve.tensor_copy(rows_f[:, i, :], p_rows[i][:, 0, :]).then_inc(marked, 1)
                dve.wait_ge(marked, 9 + i)
                dve.scalar_tensor_tensor(out=rows_f[:, i, :], in0=p_rows[i][:, 1, :], scalar=float(L),
                                         in1=rows_f[:, i, :], op0=ALU.mult, op1=ALU.add).then_inc(slot_done, 1)
            dve.wait_ge(rows_turned, 1)
            dve.tensor_copy(T.chosen[:], p_chosen[:]).then_inc(chosen_done, 1)


def stage_expert_choice(T):
    nc, t, sem = T.nc, T.t, T.sem
    ET = CAP // 128
    HT = ET // 2
    FC = F // 128
    HS = HT * 128
    with ExitStack() as ctx:
        def sb(name, shape, dt=F32):
            return ctx.enter_context(nc.sbuf_tensor(name, shape, dt))

        def ps(name, shape, dt=F32):
            return ctx.enter_context(nc.psum_tensor(name, shape, dt))

        w1 = [sb(f"ec_w1{p}", [D, F]) for p in range(2)]
        w2 = [sb(f"ec_w2{p}", [128, FC, D]) for p in range(2)]
        b1 = sb("ec_b1", [128, E, FC])
        b1_now = [sb(f"ec_b1_now{p}", [128, FC]) for p in range(2)]
        b2 = sb("ec_b2", [128, E, D])
        rows_in = [sb(f"ec_rows_in{p}", [128, ET], I32) for p in range(2)]
        rows_out = sb("ec_rows_out", [128, ET], I32)
        x = [sb(f"ec_x{p}", [128, ET, D + E]) for p in range(2)]
        weight = [sb(f"ec_weight{p}", [128, ET]) for p in range(2)]
        xT = [sb(f"ec_xT{s}", [D, HT, 128]) for s in range(2)]
        hidden = [sb(f"ec_hidden{s}", [128, FC, HS]) for s in range(2)]
        plus_b2 = sb("ec_plus_b2", [128, HT, D])
        y = [sb(f"ec_y{p}", [128, ET, D]) for p in range(2)]
        p_xT = ps("ec_p_xT", [D, HT, 128])
        p_hidden = [ps(f"ec_p_hidden{c}", [128, HS]) for c in range(FC)]
        p_y = [ps(f"ec_p_y{s}", [128, HT, D]) for s in range(2)]

        biases_in = sem("ec_biases_in")
        weights_in = [sem(f"ec_weights_in{p}") for p in range(2)]
        rows_in_set = sem("ec_rows_in_set")
        rows_out_set = sem("ec_rows_out_set")
        gathered = [[sem(f"ec_gathered{p}{s}") for s in range(2)] for p in range(2)]
        weight_set = sem("ec_weight_set")
        xT_made = sem("ec_xT_made")
        xT_kept = sem("ec_xT_kept")
        hidden_made = sem("ec_hidden_made")
        gelu_done = sem("ec_gelu_done")
        y_made = sem("ec_y_made")
        b2_added = sem("ec_b2_added")
        y_done = sem("ec_y_done")
        added = [sem(f"ec_added{p}") for p in range(2)]

        block = ctx.enter_context(nc.Block())


        @block.sync
        def _(sp):
            T.clear_old(sp)
            sp.dma_start(b1[:], t["e_b1"]).then_inc(biases_in, 16)
            sp.dma_start(b2[:], t["e_b2"].rearrange("e d -> (e d)").partition_broadcast(128)).then_inc(biases_in, 16)

            def load(w, p):
                e = 2 * w + p
                sp.dma_start(w1[p][:], t["e_w1"][bass.ds(e * D, D), :]).then_inc(weights_in[p], 16)
                sp.dma_start(w2[p][:], t["e_w2"][bass.ds(e * F, F), :].rearrange("(c k) d -> k c d", k=128)
                             ).then_inc(weights_in[p], 16)

            load(0, 0)
            load(0, 1)
            with sp.Fori(1, E // 2) as w:
                for p in range(2):
                    sp.wait_ge(y_made, 2 * (2 * w + p - 1))
                    load(w, p)
            for p in range(2):
                sp.wait_ge(added[p], 16 * ET * (E // 2))

        @block.gpsimd
        def _(pool):
            def gather(w, p):
                e = 2 * w + p
                if at_least(w, 1):
                    T.wait_alone(pool, xT_made, 2 * (e - 1))
                    T.wait_alone(pool, weight_set, e - 1)
                pool.tensor_copy(rows_in[p][:], T.chosen[:, bass.ds(e * ET, ET)]).then_inc(rows_in_set, 1)
                T.wait_alone(pool, rows_in_set, e + 1)
                for s in range(ET):
                    pool.indirect_dma_start(out=x[p][:, s, :], out_offset=None, in_=T.z_rows,
                                            in_offset=bass.IndirectOffsetOnAxis(ap=rows_in[p][:, s:s + 1], axis=0)
                                            ).then_inc(gathered[p][s // HT], 16)

            def add(w, p):
                e = 2 * w + p
                if at_least(w, 1) or p == 1:
                    T.wait_alone(pool, added[1 - p], 16 * ET * (w + p))
                pool.tensor_copy(rows_out[:], T.chosen[:, bass.ds(e * ET, ET)]).then_inc(rows_out_set, 1)
                T.wait_alone(pool, rows_out_set, e + 1)
                for s in range(ET):
                    if s % HT == 0:
                        T.wait_alone(pool, y_done, 2 * e + 1 + s // HT)
                    pool.indirect_dma_start(out=T.h_rows,
                                            out_offset=bass.IndirectOffsetOnAxis(ap=rows_out[:, s:s + 1], axis=0),
                                            in_=y[p][:, s, :], in_offset=None,
                                            compute_op=ALU.add).then_inc(added[p], 16)

            gather(0, 0)
            gather(0, 1)
            with pool.Fori(0, E // 2 - 1) as w:
                for p in range(2):
                    gather(w + 1, p)
                    add(w, p)
            add(E // 2 - 1, 0)
            add(E // 2 - 1, 1)

        @block.tensor
        def _(pe):
            def transposes(w, p, s):
                u = 4 * w + 2 * p + s
                T.wait_alone(pe, gathered[p][s], 16 * HT * (w + 1))
                if at_least(w, 1) or p + s > 0:
                    T.wait_alone(pe, xT_kept, u)
                for i in range(HT):
                    last = pe.transpose(p_xT[:, i, :], x[p][:, s * HT + i, 0:D], T.ident[:])
                last.then_inc(xT_made, 1)

            def into_hidden(w, p, s):
                u = 4 * w + 2 * p + s
                T.wait_alone(pe, weights_in[p], 32 * (w + 1))
                T.wait_alone(pe, xT_kept, u + 1)
                for c in range(FC):
                    if at_least(w, 1) or p + s > 0:
                        pe.wait_ge(gelu_done, FC * (u - 1) + c + 1)
                    pe.matmul(p_hidden[c][:], w1[p][:, c * 128:(c + 1) * 128],
                              xT[s][:].rearrange("d i n -> d (i n)"), start=True, stop=True).then_inc(hidden_made, 1)

            def out_of_hidden(w, p, s):
                u = 4 * w + 2 * p + s
                T.wait_alone(pe, gelu_done, FC * (u + 1))
                if at_least(w, 1) or p > 0:
                    T.wait_alone(pe, b2_added, u - 1)
                for i in range(HT):
                    for c in range(FC):
                        last = pe.matmul(p_y[s][:, i, :], hidden[s][:, c, i * 128:(i + 1) * 128], w2[p][:, c, :],
                                         start=(c == 0), stop=(c == FC - 1))
                last.then_inc(y_made, 1)

            transposes(0, 0, 0)
            transposes(0, 0, 1)
            into_hidden(0, 0, 0)

            def steps(w, p):
                transposes(w + p, 1 - p, 0)
                into_hidden(w, p, 1)
                out_of_hidden(w, p, 0)
                transposes(w + p, 1 - p, 1)
                into_hidden(w + p, 1 - p, 0)
                out_of_hidden(w, p, 1)

            steps(0, 0)
            with pe.Fori(0, E // 2 - 1) as w:
                steps(w, 1)
                steps(w + 1, 0)
            into_hidden(E // 2 - 1, 1, 1)
            out_of_hidden(E // 2 - 1, 1, 0)
            out_of_hidden(E // 2 - 1, 1, 1)

        @block.scalar
        def _(act):
            def gelus(w, p, s):
                u = 4 * w + 2 * p + s
                if at_least(w, 1) or p > 0:
                    T.wait_alone(act, y_made, u - 1)
                for c in range(FC):
                    act.wait_ge(hidden_made, FC * u + c + 1)
                    act.activation(hidden[s][:, c, :], p_hidden[c][:], ACT.Gelu,
                                   bias=b1_now[p][:, c:c + 1]).then_inc(gelu_done, 1)

            def expert(w, p):
                T.wait_alone(act, weight_set, 2 * w + p + 1)
                gelus(w, p, 0)
                gelus(w, p, 1)

            expert(0, 0)
            expert(0, 1)
            with act.Fori(1, E // 2) as w:
                expert(w, 0)
                expert(w, 1)

        @block.vector
        def _(dve):
            def take_weights(w, p):
                e = 2 * w + p
                for s in range(2):
                    T.wait_alone(dve, gathered[p][s], 16 * HT * (w + 1))
                if at_least(w, 1):
                    T.wait_alone(dve, gelu_done, 2 * FC * (e - 1))
                    T.wait_alone(dve, y_done, 2 * (e - 1))
                dve.tensor_copy(weight[p][:], x[p][:, :, bass.ds(D + e, 1)].rearrange("n s o -> n (s o)"))
                dve.tensor_copy(b1_now[p][:], b1[:, bass.ds(e, 1), :].rearrange("n o c -> n (o c)")
                                ).then_inc(weight_set, 1)

            def keep_xT(w, p, s):
                u = 4 * w + 2 * p + s
                T.wait_alone(dve, xT_made, u + 1)
                if at_least(w, 1) or p > 0:
                    T.wait_alone(dve, hidden_made, FC * (u - 1))
                dve.tensor_copy(xT[s][:], p_xT[:]).then_inc(xT_kept, 1)

            def weigh(w, p, s):
                e, u = 2 * w + p, 4 * w + 2 * p + s
                T.wait_alone(dve, y_made, u + 1)
                if at_least(w, 1) or p + s > 0:
                    T.wait_alone(dve, y_done, u)
                if at_least(w, 1):
                    T.wait_alone(dve, added[p], 16 * ET * w)
                dve.tensor_tensor(plus_b2[:], p_y[s][:],
                                  over(b2[:, bass.ds(e, 1), :].rearrange("n o d -> n (o d)"), HT),
                                  ALU.add).then_inc(b2_added, 1)
                T.wait_alone(dve, b2_added, u + 1)
                dve.tensor_tensor(y[p][:, s * HT:(s + 1) * HT, :], plus_b2[:],
                                  over(weight[p][:, s * HT:(s + 1) * HT], D, 2), ALU.mult).then_inc(y_done, 1)

            def steps(w, p):
                take_weights(w + p, 1 - p)
                keep_xT(w + p, 1 - p, 0)
                weigh(w, p, 0)
                keep_xT(w + p, 1 - p, 1)
                weigh(w, p, 1)

            dve.wait_ge(biases_in, 32)
            take_weights(0, 0)
            keep_xT(0, 0, 0)
            keep_xT(0, 0, 1)
            steps(0, 0)
            with dve.Fori(0, E // 2 - 1) as w:
                steps(w, 1)
                steps(w + 1, 0)
            weigh(E // 2 - 1, 1, 0)
            weigh(E // 2 - 1, 1, 1)


def stage_offset_attention(T):
    nc, t, sem = T.nc, T.t, T.sem
    NO = len(OFFS)
    BH = GB * NH
    NLOC = OFF_LOCAL + 1
    PAD = OFFS[-1]
    CHUNK = 16
    NCH = (NO + CHUNK - 1) // CHUNK
    LAST = NO - CHUNK * (NCH - 1)
    UNITS = [("pool", 0, 0), ("dve", 0, 1), ("dve", 0, 2), ("dve", 0, 3),
             ("dve", 1, 0), ("pool", 1, 1), ("dve", 1, 2), ("pool", 1, 3), ("pool", 2, 0)]
    NU = len(UNITS)
    SLOT = {u: sum(v[0] == UNITS[u][0] for v in UNITS[:u]) for u in range(NU)}
    DVE_UNITS = [u for u in range(NU) if UNITS[u][0] == "dve"]
    NDVE, NPOOL = (sum(v[0] == who for v in UNITS) for who in ("dve", "pool"))
    with ExitStack() as ctx:
        def sb(name, shape, dt=F32):
            return ctx.enter_context(nc.sbuf_tensor(name, shape, dt))

        def ps(name, shape, dt=F32):
            return ctx.enter_context(nc.psum_tensor(name, shape, dt))

        w_qk = sb("oa_w_qk", [D, 2, D])
        w_vg = sb("oa_w_vg", [D, 2, D])
        w_out = sb("oa_w_out", [D, D])
        w_out_scaled = sb("oa_w_out_scaled", [D, D])
        gain = sb("oa_gain", [D, 1])
        b_qk = sb("oa_b_qk", [D, 2])
        biases = sb("oa_biases", [3, 3, D])
        rest = sb("oa_rest", [3, 3, D])
        part = [sb(f"oa_part{i}", [3, 3, D], BF16) for i in range(2)]
        bias_acc = sb("oa_bias_acc", [3, 3, D])
        bias_rows = sb("oa_bias_rows", [3, 3, D], BF16)
        ones_rows = sb("oa_ones_rows", [3, L], BF16)
        shift = sb("oa_shift", [D, NO])
        sum_w = sb("oa_sum_w", [D, NO, 4 * NH])
        pos_bias = sb("oa_pos_bias", [128, NCH])
        cosines = sb("oa_cosines", [128, NCH])
        amp = sb("oa_amp", [128, 1])
        bias_col = sb("oa_bias_col", [128, NCH])
        bias = sb("oa_bias", [128, NCH, L])
        stats = sb("oa_stats", [L, GB, 6])
        mv = sb("oa_mv", [L, GB, 2])
        var_eps = sb("oa_var_eps", [L, GB])
        rstd = sb("oa_rstd", [L, GB])
        shift_by = sb("oa_shift_by", [L, GB])
        z = [sb(f"oa_z{p}", [L, GB, D]) for p in range(2)]
        zT = [sb(f"oa_zT{p}", [D, GB, L]) for p in range(2)]
        q_sb = [sb(f"oa_q{p}", [D, GB, L]) for p in range(2)]
        k_sb = [sb(f"oa_k{p}", [D, PAD + GT]) for p in range(2)]
        v_ones = [sb(f"oa_v_ones{p}", [L, GB, NH, 32]) for p in range(2)]
        gate = [sb(f"oa_gate{p}", [L, GB, D]) for p in range(2)]
        prod_dve = [sb(f"oa_prod_dve{i}", [D, 4, GB, L]) for i in range(NDVE)]
        prod_pool = [sb(f"oa_prod_pool{i}", [D, 4, GB, L]) for i in range(NPOOL)]
        biased = sb("oa_biased", [128, NCH, GB, L])
        top = [sb(f"oa_top{i}", [L, NH]) for i in range(2)]
        probs = [sb(f"oa_probs{p}", [L, NO, GB, NH]) for p in range(2)]
        dense = [sb(f"oa_dense{p}", [L, L, BH]) for p in range(2)]
        raw = sb("oa_raw", [128, 4, L])
        inv_sum = sb("oa_inv_sum", [L, GB, NH])
        heads_out = sb("oa_heads_out", [L, GB, D])
        gated = sb("oa_gated", [L, GB, D])
        gatedT = sb("oa_gatedT", [D, GB, L])
        p_sc = [ps(f"oa_p_sc{i}", [128, 512]) for i in range(2)]
        p_turned = [ps(f"oa_p_turned{i}", [128, 512]) for i in range(2)]
        p_qk = ps("oa_p_qk", [D, GB, L])
        p_vg = ps("oa_p_vg", [L, 2, 2, D])
        p_o = ps("oa_p_o", [128, 2, NH, 32])
        p_out = ps("oa_p_out", [128, 512])
        p_gatedT = p_out[:, 0:GT].rearrange("p (b l) -> p b l", b=GB)
        p_rows = p_out[0:L, :].rearrange("p (b d) -> p b d", b=GB)

        def sc_of(p, c):
            return p_sc[(NCH * p + c) % 2]

        def turned(b):
            return p_turned[b % 2][0:L, 0:NO * NH].rearrange("n (o h) -> n o h", h=NH)

        def products(eng, p, u, done):
            who, c, place = UNITS[u]
            buf = (prod_dve if who == "dve" else prod_pool)[SLOT[u]]
            js = [CHUNK * c + 4 * i + place for i in range(4)] if c < NCH - 1 else list(range(CHUNK * c, NO))
            runs = [(0, 4)] if c < NCH - 1 else [(i, i + 1) for i in range(LAST)]
            for a, e in runs:
                lo = OFFS[js[e - 1]]
                n = e - a
                k0 = k_sb[p][:, PAD - OFFS[js[a]] + lo:PAD - OFFS[js[a]] + lo + 1]
                q0 = q_sb[p][:, 0, lo:lo + 1]
                k_win = bass.AP(k0.tensor, k0.offset, [list(k0.ap[0]), [4, n], [L, GB], [1, L - lo]])
                q_win = bass.AP(q0.tensor, q0.offset, [list(q0.ap[0]), [0, n], [L, GB], [1, L - lo]])
                last = eng.tensor_tensor(buf[:, a:e, :, lo:L], q_win, k_win, ALU.mult)
            last.then_inc(done, 1)

        h_in = [sem(f"oa_h_in{i}") for i in range(4)]
        weights_in = sem("oa_weights_in")
        scaled = sem("oa_scaled")
        split = sem("oa_split")
        bias_steps = sem("oa_bias_steps")
        masked = sem("oa_masked")
        cleared = sem("oa_cleared")
        first_cleared = sem("oa_first_cleared")
        stats_done = sem("oa_stats_done")
        mv_done = sem("oa_mv_done")
        eps_added = sem("oa_eps_added")
        rstd_done = sem("oa_rstd_done")
        shift_done = sem("oa_shift_done")
        z_done = sem("oa_z_done")
        zT_made = sem("oa_zT_made")
        zT_kept = sem("oa_zT_kept")
        q_made = sem("oa_q_made")
        q_kept = sem("oa_q_kept")
        k_made = sem("oa_k_made")
        k_kept = sem("oa_k_kept")
        vg_made = sem("oa_vg_made")
        v_kept = sem("oa_v_kept")
        gate_done = sem("oa_gate_done")
        pool_prods = sem("oa_pool_prods")
        dve_prods = sem("oa_dve_prods")
        summed = sem("oa_summed")
        chunk_made = sem("oa_chunk_made")
        bias_added = sem("oa_bias_added")
        turned_made = sem("oa_turned_made")
        top_done = sem("oa_top_done")
        sub_done = sem("oa_sub_done")
        exp_done = sem("oa_exp_done")
        skewed = [sem(f"oa_skewed{p}") for p in range(2)]
        dense_in = [sem(f"oa_dense_in{p}") for p in range(2)]
        pv_done = sem("oa_pv_done")
        raw_kept = sem("oa_raw_kept")
        o_turned = sem("oa_o_turned")
        inv_done = sem("oa_inv_done")
        out_done = sem("oa_out_done")
        gated_done = sem("oa_gated_done")
        gatedT_made = sem("oa_gatedT_made")
        gatedT_kept = sem("oa_gatedT_kept")
        rows_made = sem("oa_rows_made")
        h_done = sem("oa_h_done")

        block = ctx.enter_context(nc.Block())

        @block.sync
        def _(sp):
            T.clear_old(sp)
            for i in range(4):
                b0 = i * B // 4
                sp.dma_start(T.H[:, b0:b0 + B // 4, :],
                             T.h_rows.rearrange("(b l) d -> l b d", l=L)[:, b0:b0 + B // 4, :]).then_inc(h_in[i], 16)
            for dst, src in ((w_qk[:], t["o_wqkv"][:, 0:2 * D].rearrange("d (j e) -> d j e", j=2)),
                             (w_vg[:, 0, :], t["o_wqkv"][:, 2 * D:3 * D]), (w_vg[:, 1, :], t["o_wgate"]),
                             (w_out[:], t["o_wout"]), (gain[:], t["o_gain"].unsqueeze(1)),
                             (b_qk[:], t["o_bqk"]),
                             (biases[:, 0:2, :].rearrange("r j d -> r (j d)"), t["o_bvg"].partition_broadcast(3)),
                             (biases[:, 2, :], t["o_bout"].partition_broadcast(3)), (shift[:], t["o_scale"]),
                             (pos_bias[:], t["o_pos"]),
                             (cosines[:], t["o_cos"]),
                             (amp[:], t["o_amp"].unsqueeze(1))):
                sp.dma_start(dst, src).then_inc(weights_in, 16)

            sp.wait_ge(cleared, 2)
            sp.wait_ge(first_cleared, 1)

            def along_diagonals(g, p, w):
                row, col = L * BH, BH
                d = T.diagonals[p]
                T.wait_alone(sp, exp_done, GB * (g + 1))
                if at_least(g, 2):
                    T.wait_alone(sp, dense_in[p], 64 * w)
                sp.dma_start(bass.AP(d.tensor, (PAD - OFF_LOCAL) * row, [[row + col, L], [row, NLOC], [1, BH]]),
                             probs[p][:, 0:NLOC].rearrange("n o b h -> n o (b h)")).then_inc(skewed[p], 16)
                for j in range(NLOC, NO):
                    sp.dma_start(bass.AP(d.tensor, (PAD - OFFS[j]) * row, [[row + col, L], [1, BH]]),
                                 probs[p][:, j].rearrange("n b h -> n (b h)")).then_inc(skewed[p], 16)

            def as_matrices(g, p, w):
                T.wait_alone(sp, skewed[p], 16 * (1 + NO - NLOC) * (w + 1))
                if at_least(g, 2):
                    T.wait_alone(sp, pv_done, 2 * (g - 1))
                for m in range(0, L, 32):
                    e = min(m + 32, L)
                    sp.dma_start(dense[p][m:e, m:L, :], T.diagonals[p][PAD + m:PAD + e, m:L]).then_inc(dense_in[p], 16)

            for g in range(2):
                along_diagonals(g, g, 0)
                as_matrices(g, g, 0)
            with sp.Fori(1, NG // 2) as k:
                for p in range(2):
                    along_diagonals(2 * k + p, p, k)
                    as_matrices(2 * k + p, p, k)

        @block.gpsimd
        def _(pool):
            pool.wait_ge(bias_steps, 1)
            for c in range(NCH - 1):
                pool.affine_select(out=bias[:, c, :], in_=bias[:, c, :], compare_op=ALU.is_ge, fill=-1e30,
                                   base=NH * (CHUNK * c - OFF_LOCAL), pattern=[[NH, L]],
                                   channel_multiplier=1).then_inc(masked, 1)
            for i in range(1, LAST):
                rows, far = slice(32 * i, 32 * i + 32), OFFS[CHUNK * (NCH - 1) + i]
                pool.wait_ge(masked, NCH - 2 + i)
                pool.affine_select(out=bias[rows, NCH - 1, :], in_=bias[rows, NCH - 1, :], compare_op=ALU.is_ge,
                                   fill=-1e30, base=-far, pattern=[[1, L]], channel_multiplier=0).then_inc(masked, 1)

            def rstd_of(g):
                pool.wait_ge(mv_done, GB * (g + 1))
                if at_least(g, 1):
                    pool.wait_ge(z_done, g)
                pool.tensor_tensor(var_eps[:], mv[:, :, 1], T.eps[:], ALU.add).then_inc(eps_added, 1)
                pool.wait_ge(eps_added, g + 1)
                pool.tensor_tensor(rstd[:], var_eps[:], T.neg_half[:], ALU.pow).then_inc(rstd_done, 1)

            def turn(g, p):
                for u in range(NU):
                    if UNITS[u][0] == "pool":
                        if SLOT[u] == 0:
                            T.wait_alone(pool, k_kept, g + 1)
                        if at_least(g, 1):
                            T.wait_alone(pool, summed, NU * (g - 1) + u + 1)
                        products(pool, p, u, pool_prods)
                        if SLOT[u] == 1 and below(g, NG - 2):
                            rstd_of(g + 2)

            rstd_of(0)
            rstd_of(1)
            pool.memset(dense[0][:], 0.0).then_inc(first_cleared, 1)
            pool.wait_ge(cleared, 2)
            for g in range(4):
                turn(g, g % 2)
            with pool.Fori(2, NG // 2 - 1) as k:
                turn(2 * k, 0)
                turn(2 * k + 1, 1)
            turn(NG - 2, 0)
            turn(NG - 1, 1)

        @block.tensor
        def _(pe):
            pe.wait_ge(weights_in, 16 * 12)
            pe.wait_ge(scaled, 7)
            pe.wait_ge(split, 8)

            def z_transposes(g, p):
                T.wait_alone(pe, z_done, g + 1)
                if at_least(g, 1):
                    T.wait_alone(pe, k_kept, g)
                if at_least(g, 4):
                    T.wait_alone(pe, raw_kept, 2 * (g - 3))
                for b in range(GB):
                    last = pe.transpose(p_qk[:, b, :], z[p][:, b, :], T.ident[0:L, 0:L])
                last.then_inc(zT_made, 1)

            def queries(g, p):
                T.wait_alone(pe, zT_kept, g + 1)
                pe.matmul(p_qk[:], w_qk[:, 0, :], zT[p][:], start=True, stop=True).then_inc(q_made, 1)

            def keys(g, p):
                T.wait_alone(pe, q_kept, g + 1)
                pe.matmul(p_qk[:], w_qk[:, 1, :], zT[p][:], start=True, stop=True).then_inc(k_made, 1)

            def values_gate(g, p, i):
                if at_least(g, 1) or i == 1:
                    T.wait_alone(pe, gate_done, 2 * g + i)
                for j in range(2):
                    b = 2 * i + j
                    pe.matmul(p_vg[:, j], zT[p][:, b, :], w_vg[:], start=True, stop=False)
                    last = pe.matmul(p_vg[:, j], ones_rows[:], bias_rows[:, 0:2, :], start=False, stop=True)
                last.then_inc(vg_made, 1)

            def sums(g, p, u):
                who, c, place = UNITS[u]
                if u == 0 or UNITS[u - 1][1] != c:
                    if at_least(g, 1) or c >= 2:
                        T.wait_alone(pe, bias_added, NCH * g + c - 1)
                if who == "dve":
                    T.wait_alone(pe, dve_prods, NDVE * g + SLOT[u] + 1)
                    buf = prod_dve[SLOT[u]]
                else:
                    T.wait_alone(pe, pool_prods, NPOOL * g + SLOT[u] + 1)
                    buf = prod_pool[SLOT[u]]
                for i in range(4):
                    j = CHUNK * c + (4 * i + place if c < NCH - 1 else i)
                    last = pe.matmul(sc_of(p, c)[32 * i:32 * i + 32, 0:GT], sum_w[:, j, :],
                                     buf[:, i].rearrange("d b l -> d (b l)"), start=(place == 0),
                                     stop=(place == 3 or c == NCH - 1), skip_group_check=True)
                last.then_inc(summed, 1)
                if u == NU - 1 or UNITS[u + 1][1] != c:
                    pe.wait_ge(summed, NU * g + u + 1)
                    pe.sem_inc(chunk_made, 1)

            def turn_scores(g, b):
                s = GB * g + b
                T.wait_alone(pe, bias_added, NCH * (g + 1))
                if at_least(g, 1) or b >= 2:
                    T.wait_alone(pe, sub_done, s - 1)
                for c in range(NCH - 1):
                    pe.transpose(p_turned[b % 2][0:L, c * 128:(c + 1) * 128], biased[:, c, b, :], T.ident[:])
                pe.matmul(p_turned[b % 2][0:L, (NCH - 1) * 128:NO * NH], biased[:, NCH - 1, b, :],
                          T.ident[:].rearrange("r (i m) -> r i m", i=LAST)[:, :, 0:NH], start=True, stop=True
                          ).then_inc(turned_made, 1)

            def values(g, p, w, i):
                if i == 0:
                    T.wait_alone(pe, dense_in[p], 64 * (w + 1))
                    T.wait_alone(pe, v_kept, 2 * (g + 1))
                    T.wait_alone(pe, k_kept, min(g + 4, NG) if isinstance(g, int) else g + 4)
                else:
                    T.wait_alone(pe, raw_kept, 2 * g + 1)
                for j in range(2):
                    for half in range(2):
                        b = 2 * i + j
                        for q in range(4):
                            h = 4 * half + q
                            last = pe.matmul(p_qk[32 * q:32 * q + 32, 2 * j + half, :], v_ones[p][:, b, h, :],
                                             dense[p][:, :, b * NH + h], start=True, stop=True)
                last.then_inc(pv_done, 1)

            def turn_sums(g, i):
                T.wait_alone(pe, raw_kept, 2 * g + i + 1)
                if at_least(g, 1) or i == 1:
                    T.wait_alone(pe, out_done, 2 * g + i)
                for j in range(2):
                    for half in range(2):
                        last = pe.transpose(p_o[0:L, j, 4 * half:4 * half + 4, :].rearrange("n h d -> n (h d)"),
                                            raw[:, 2 * j + half, :], T.ident[:])
                last.then_inc(o_turned, 1)

            def gated_transposes(g):
                T.wait_alone(pe, gated_done, g + 1)
                if at_least(g, 1):
                    T.wait_alone(pe, h_done, g)
                for b in range(GB):
                    last = pe.transpose(p_gatedT[:, b, :], gated[:, b, :], T.ident[0:L, 0:L])
                last.then_inc(gatedT_made, 1)

            def project_out(g):
                T.wait_alone(pe, gatedT_kept, g + 1)
                for b in range(GB):
                    pe.matmul(p_rows[:, b, :], gatedT[:, b, :], w_out_scaled[:], start=True, stop=False)
                    last = pe.matmul(p_rows[:, b, :], ones_rows[:], bias_rows[:, 2, :], start=False, stop=True)
                last.then_inc(rows_made, 1)

            def turn(g, p, w):
                if here(g - 1):
                    values_gate(g - 1, 1 - p, 0)
                if here(g):
                    sums(g, p, 0)
                if here(g - 1):
                    values_gate(g - 1, 1 - p, 1)
                if here(g + 1):
                    z_transposes(g + 1, 1 - p)
                if here(g):
                    sums(g, p, 1)
                if here(g + 1):
                    queries(g + 1, 1 - p)
                if here(g):
                    sums(g, p, 2)
                if here(g + 1):
                    keys(g + 1, 1 - p)
                if here(g - 1):
                    turn_scores(g - 1, 0)
                    turn_scores(g - 1, 1)
                if here(g - 2):
                    values(g - 2, p, w - 1, 0)
                if here(g - 1):
                    turn_scores(g - 1, 2)
                    turn_scores(g - 1, 3)
                if here(g):
                    sums(g, p, 3)
                if here(g - 2):
                    turn_sums(g - 2, 0)
                    values(g - 2, p, w - 1, 1)
                if here(g):
                    sums(g, p, 4)
                if here(g - 3):
                    gated_transposes(g - 3)
                if here(g):
                    sums(g, p, 5)
                if here(g - 2):
                    turn_sums(g - 2, 1)
                if here(g):
                    sums(g, p, 6)
                if here(g - 3):
                    project_out(g - 3)
                if here(g):
                    sums(g, p, 7)
                    sums(g, p, 8)

            z_transposes(0, 0)
            queries(0, 0)
            keys(0, 0)
            for g in range(4):
                turn(g, g % 2, g // 2)
            with pe.Fori(2, NG // 2 - 1) as k:
                turn(2 * k, 0, k)
                turn(2 * k + 1, 1, k)
            for g in range(NG - 2, NG + 4):
                turn(g, g % 2, g // 2)

        @block.scalar
        def _(act):
            act.wait_ge(weights_in, 16 * 12)
            act.wait_ge(cleared, 2)

            def normalize(g, p):
                act.wait_ge(shift_done, g + 1)
                if at_least(g, 2):
                    T.wait_alone(act, zT_made, g - 1)
                for b in range(GB):
                    last = act.activation(z[p][:, b, :], T.H[:, g * GB + b, :], ACT.Identity,
                                          bias=shift_by[:, b:b + 1], scale=rstd[:, b:b + 1])
                last.then_inc(z_done, 1)

            def keep_zT(g, p):
                act.wait_ge(zT_made, g + 1)
                if at_least(g, 2):
                    act.wait_ge(vg_made, 2 * (g - 1))
                act.copy(zT[p][:], p_qk[:]).then_inc(zT_kept, 1)

            def keep_qk(g, p):
                act.wait_ge(q_made, g + 1)
                if at_least(g, 2):
                    act.wait_ge(dve_prods, NDVE * (g - 1))
                    act.wait_ge(pool_prods, NPOOL * (g - 1))
                act.activation(q_sb[p][:], p_qk[:], ACT.Identity, bias=b_qk[:, 0:1]).then_inc(q_kept, 1)
                act.wait_ge(k_made, g + 1)
                act.activation(k_sb[p][:, PAD:PAD + GT].rearrange("p (b l) -> p b l", b=GB), p_qk[:], ACT.Identity,
                               bias=b_qk[:, 1:2]).then_inc(k_kept, 1)

            def keep_vg(g, p, i):
                act.wait_ge(vg_made, 2 * g + i + 1)
                if at_least(g, 2):
                    act.wait_ge(pv_done, 2 * (g - 1))
                    act.wait_ge(gated_done, g - 1)
                act.copy(v_ones[p][:, 2 * i:2 * i + 2, :, 0:DH],
                         p_vg[:, :, 0, :].rearrange("l j (h d) -> l j h d", h=NH)).then_inc(v_kept, 1)
                act.activation(gate[p][:, 2 * i:2 * i + 2, :], p_vg[:, :, 1, :], ACT.Tanh,
                               scale=0.5).then_inc(gate_done, 1)

            def exponential(g, p, b):
                act.wait_ge(sub_done, GB * g + b + 1)
                act.activation(probs[p][:, :, b, :], probs[p][:, :, b, :], ACT.Exp).then_inc(exp_done, 1)

            def keep_raw(g, i):
                act.wait_ge(pv_done, 2 * g + i + 1)
                if at_least(g, 1) or i == 1:
                    act.wait_ge(o_turned, 2 * g + i)
                act.copy(raw[:], p_qk[:]).then_inc(raw_kept, 1)

            def keep_gatedT(g):
                act.wait_ge(gatedT_made, g + 1)
                if at_least(g, 1):
                    act.wait_ge(rows_made, g)
                act.copy(gatedT[:], p_gatedT).then_inc(gatedT_kept, 1)

            def turn(g, p):
                if here(g - 1):
                    keep_vg(g - 1, 1 - p, 0)
                    keep_vg(g - 1, 1 - p, 1)
                if here(g + 1):
                    keep_zT(g + 1, 1 - p)
                    keep_qk(g + 1, 1 - p)
                if here(g - 1):
                    exponential(g - 1, 1 - p, 0)
                    exponential(g - 1, 1 - p, 1)
                if here(g - 2):
                    keep_raw(g - 2, 0)
                if here(g - 1):
                    exponential(g - 1, 1 - p, 2)
                    exponential(g - 1, 1 - p, 3)
                if here(g - 2):
                    keep_raw(g - 2, 1)
                if here(g - 3):
                    keep_gatedT(g - 3)
                if here(g + 2):
                    normalize(g + 2, p)

            normalize(0, 0)
            normalize(1, 1)
            keep_zT(0, 0)
            keep_qk(0, 0)
            for g in range(4):
                turn(g, g % 2)
            with act.Fori(2, NG // 2 - 1) as k:
                turn(2 * k, 0)
                turn(2 * k + 1, 1)
            for g in range(NG - 2, NG + 4):
                turn(g, g % 2)

        @block.vector
        def _(dve):
            for u in range(NU):
                who, c, place = UNITS[u]
                buf = (prod_dve if who == "dve" else prod_pool)[SLOT[u]]
                for i in range(4):
                    offset = OFFS[CHUNK * c + (4 * i + place if c < NCH - 1 else i)]
                    if offset > 0:
                        dve.memset(buf[:, i, :, 0:offset], 0.0)
            for i in range(2):
                dve.memset(k_sb[i][:, 0:PAD], 0.0)
                dve.memset(v_ones[i][:], 1.0)
            dve.memset(sum_w[:], 0.0)
            dve.memset(bias[:], 0.0).then_inc(bias_steps, 1)
            dve.memset(ones_rows[:], 1.0).then_inc(cleared, 1)
            dve.memset(dense[1][:], 0.0).then_inc(cleared, 1)
            dve.wait_ge(weights_in, 16 * 12)
            dve.tensor_copy(part[0][:], biases[:]).then_inc(split, 1)
            dve.wait_ge(split, 1)
            dve.tensor_scalar(bias_acc[:], part[0][:], T.ident[0:3, 0:1], None, ALU.mult).then_inc(split, 1)
            dve.tensor_tensor(rest[:], biases[:], part[0][:], ALU.subtract).then_inc(split, 1)
            dve.wait_ge(split, 3)
            dve.tensor_copy(part[1][:], rest[:]).then_inc(split, 1)
            dve.wait_ge(split, 4)
            dve.scalar_tensor_tensor(out=bias_acc[:], in0=part[1][:], scalar=T.ident[0:3, 1:2], in1=bias_acc[:],
                                     op0=ALU.mult, op1=ALU.add).then_inc(split, 1)
            dve.tensor_tensor(rest[:], rest[:], part[1][:], ALU.subtract).then_inc(split, 1)
            dve.wait_ge(split, 6)
            dve.scalar_tensor_tensor(out=bias_acc[:], in0=rest[:], scalar=T.ident[0:3, 2:3], in1=bias_acc[:],
                                     op0=ALU.mult, op1=ALU.add).then_inc(split, 1)
            dve.wait_ge(split, 7)
            dve.tensor_copy(bias_rows[:], bias_acc[:]).then_inc(split, 1)
            dve.tensor_scalar(bias_col[:], cosines[:], amp[:, 0:1], None, ALU.mult).then_inc(bias_steps, 1)
            dve.tensor_scalar(shift[:], shift[:], 1.0, DH ** -0.5, ALU.add, ALU.mult).then_inc(scaled, 1)
            dve.tensor_scalar(w_out_scaled[:], w_out[:], gain[:, 0:1], 0.5, ALU.mult, ALU.mult).then_inc(scaled, 1)
            dve.wait_ge(scaled, 2)
            near = CHUNK * (NCH - 1)
            for place in range(4):
                dve.tensor_tensor(sum_w[:, place:near:4, NH * place:NH * (place + 1)], over(shift[:, place:near:4], NH, 2),
                                  over(T.head_mask[:], near // 4), ALU.mult).then_inc(scaled, 1)
            dve.tensor_tensor(sum_w[:, near:NO, 0:NH], over(shift[:, near:NO], NH, 2),
                              over(T.head_mask[:], LAST), ALU.mult).then_inc(scaled, 1)
            dve.wait_ge(bias_steps, 2)
            dve.tensor_tensor(bias_col[:], bias_col[:], pos_bias[:], ALU.add).then_inc(bias_steps, 1)
            dve.wait_ge(bias_steps, 3)
            dve.wait_ge(masked, NCH - 1 + LAST - 1)
            dve.tensor_tensor(bias[:], bias[:], over(bias_col[:], L, 2), ALU.add).then_inc(bias_steps, 1)

            def moments(g):
                if isinstance(g, int) and g % (NG // 4) == 0 and g < 6:
                    dve.wait_ge(h_in[g // (NG // 4)], 16)
                for b in range(GB):
                    dve.bn_stats(stats[:, b, :], T.H[:, g * GB + b, :]).then_inc(stats_done, 1)
                T.wait_alone(dve, stats_done, GB * (g + 1))
                for b in range(GB):
                    dve.bn_aggr(mv[:, b, :], stats[:, b, :]).then_inc(mv_done, 1)

            def shift_of(g):
                dve.wait_ge(rstd_done, g + 1)
                if at_least(g, 1):
                    dve.wait_ge(z_done, g)
                dve.scalar_tensor_tensor(out=shift_by[:], in0=mv[:, :, 0], scalar=-1.0, in1=rstd[:], op0=ALU.mult,
                                         op1=ALU.mult).then_inc(shift_done, 1)

            def products_of(g, p, u):
                if u == DVE_UNITS[0]:
                    T.wait_alone(dve, k_kept, g + 1)
                if at_least(g, 1):
                    T.wait_alone(dve, summed, NU * (g - 1) + u + 1)
                products(dve, p, u, dve_prods)

            def add_bias(g, p, c):
                dve.wait_ge(chunk_made, NCH * g + c + 1)
                if at_least(g, 1):
                    dve.wait_ge(turned_made, GB * g)
                dve.tensor_tensor(biased[:, c], sc_of(p, c)[:, 0:GT].rearrange("r (b l) -> r b l", b=GB),
                                  over(bias[:, c], GB), ALU.add).then_inc(bias_added, 1)

            def less_maximum(g, p, b, w):
                s = GB * g + b
                dve.wait_ge(turned_made, s + 1)
                dve.tensor_reduce(top[b % 2][:], turned(b).rearrange("n o h -> n h o"), AX_X,
                                  ALU.max).then_inc(top_done, 1)
                dve.wait_ge(top_done, s + 1)
                if b == 0 and at_least(g, 2):
                    dve.wait_ge(skewed[p], 16 * (1 + NO - NLOC) * w)
                dve.tensor_tensor(probs[p][:, :, b, :], turned(b), over(top[b % 2][:], NO),
                                  ALU.subtract).then_inc(sub_done, 1)

            def divide(g, i):
                dve.wait_ge(o_turned, 2 * g + i + 1)
                dve.reciprocal(inv_sum[:, 2 * i:2 * i + 2, :], p_o[0:L, :, :, DH]).then_inc(inv_done, 1)
                dve.wait_ge(inv_done, 2 * g + i + 1)
                dve.tensor_tensor(heads_out[:, 2 * i:2 * i + 2, :].rearrange("n b (h d) -> n b h d", h=NH),
                                  p_o[0:L, :, :, 0:DH], over(inv_sum[:, 2 * i:2 * i + 2, :], DH, 3),
                                  ALU.mult).then_inc(out_done, 1)

            def apply_gate(g, p):
                dve.wait_ge(out_done, 2 * (g + 1))
                dve.wait_ge(gate_done, 2 * (g + 1))
                if at_least(g, 1):
                    dve.wait_ge(gatedT_made, g)
                dve.scalar_tensor_tensor(out=gated[:], in0=gate[p][:], scalar=1.0, in1=heads_out[:], op0=ALU.add,
                                         op1=ALU.mult).then_inc(gated_done, 1)

            def add_to_h(g):
                dve.wait_ge(rows_made, g + 1)
                rows = T.H[:, bass.ds(g * GB, GB), :]
                dve.tensor_tensor(rows, rows, p_rows, ALU.add).then_inc(h_done, 1)

            def turn(g, p, w):
                if here(g):
                    products_of(g, p, DVE_UNITS[0])
                if here(g + 2):
                    moments(g + 2)
                if here(g - 1):
                    add_bias(g - 1, 1 - p, 1)
                if here(g):
                    products_of(g, p, DVE_UNITS[1])
                if here(g - 4):
                    add_to_h(g - 4)
                if here(g - 1):
                    add_bias(g - 1, 1 - p, 2)
                if here(g):
                    products_of(g, p, DVE_UNITS[2])
                if here(g - 1):
                    less_maximum(g - 1, 1 - p, 0, w - 1 + p)
                    less_maximum(g - 1, 1 - p, 1, w - 1 + p)
                if here(g):
                    products_of(g, p, DVE_UNITS[3])
                if here(g - 1):
                    less_maximum(g - 1, 1 - p, 2, w - 1 + p)
                    less_maximum(g - 1, 1 - p, 3, w - 1 + p)
                if here(g - 2):
                    divide(g - 2, 0)
                if here(g):
                    products_of(g, p, DVE_UNITS[4])
                    add_bias(g, p, 0)
                if here(g + 2):
                    shift_of(g + 2)
                if here(g - 2):
                    divide(g - 2, 1)
                    apply_gate(g - 2, p)

            for g in range(2):
                moments(g)
                shift_of(g)
            for g in range(4):
                turn(g, g % 2, g // 2)
            for i in range(2, 4):
                dve.wait_ge(h_in[i], 16)
            with dve.Fori(2, NG // 2 - 1) as k:
                turn(2 * k, 0, k)
                turn(2 * k + 1, 1, k)
            for g in range(NG - 2, NG + 4):
                turn(g, g % 2, g // 2)


def stage_dispatch(T):
    nc, t, sem = T.nc, T.t, T.sem
    with ExitStack() as ctx:
        def sb(name, shape, dt=F32):
            return ctx.enter_context(nc.sbuf_tensor(name, shape, dt))

        def ps(name, shape, dt=F32):
            return ctx.enter_context(nc.psum_tensor(name, shape, dt))

        T.experts = T.sb("experts", [128, E, F + F // 128 * D + F // 128])
        T.expert_b2 = T.sb("expert_b2", [128, E, D])
        w_gate = sb("di_w_gate", [D, E])
        b_gate = sb("di_b_gate", [1, E])
        ones_row = sb("di_ones_row", [1, L])
        earlier = sb("di_earlier", [L, L], BF16)
        all_ones = sb("di_all_ones", [L, L], BF16)
        empty = sb("di_empty", [128, ROW])
        stats = [sb(f"di_stats{p}", [L, GB, 6]) for p in range(2)]
        mv = [sb(f"di_mv{p}", [L, GB, 2]) for p in range(2)]
        var_eps = [sb(f"di_var_eps{p}", [L, GB]) for p in range(2)]
        rstd = [sb(f"di_rstd{p}", [L, GB]) for p in range(2)]
        z = [sb(f"di_z{p}", [L, GB, D]) for p in range(2)]
        zT = [sb(f"di_zT{p}", [D, GB, L]) for p in range(2)]
        rows = sb("di_rows", [L, B, ROW])
        best = sb("di_best", [L, B])
        less = sb("di_less", [L, B, E])
        preference = sb("di_preference", [L, B, E])
        preference_int = sb("di_preference_int", [L, B, E], I32)
        candidates = sb("di_candidates", [L, B, E])
        first = sb("di_first", [L, B])
        hot = sb("di_hot", [L, B, E])
        hot_bf = sb("di_hot_bf", [L, B, E], BF16)
        score_sum = sb("di_score_sum", [L, B])
        totals = sb("di_totals", [L, E, B])
        same_expert = sb("di_same_expert", [L, E, B])
        running = sb("di_running", [L, E, B])
        tiles_int = sb("di_tiles_int", [L, E], I32)
        tiles_shifted = sb("di_tiles_shifted", [L, E], I32)
        tiles = sb("di_tiles", [L, E])
        ones_e = sb("di_ones_e", [L, E])
        tile_end = sb("di_tile_end", [L, E])
        base = sb("di_base", [L, E])
        place = sb("di_place", [L, B, E])
        slot_f = sb("di_slot_f", [L, B])
        slot = sb("di_slot", [L, B], I32)
        tile_no = sb("di_tile_no", [1, NTILES])
        tile_no_int = sb("di_tile_no_int", [1, NTILES], I32)
        passed = sb("di_passed", [1, NTILES, E])
        tile_expert_f = sb("di_tile_expert_f", [1, NTILES])
        p_zT = [ps(f"di_p_zT{p}", [D, GB, L]) for p in range(2)]
        p_logits = ps("di_p_logits", [L, B, E])
        p_before = ps("di_p_before", [L, B, E])
        p_total = ps("di_p_total", [L, B, E])

        weights_in = sem("di_weights_in")
        consts = sem("di_consts")
        emptied = sem("di_emptied")
        experts_in = sem("di_experts_in")
        stats_done = sem("di_stats_done")
        mv_done = sem("di_mv_done")
        eps_added = sem("di_eps_added")
        rstd_done = sem("di_rstd_done")
        z_done = sem("di_z_done")
        z_copied = sem("di_z_copied")
        h_copied = sem("di_h_copied")
        zT_made = sem("di_zT_made")
        zT_kept = sem("di_zT_kept")
        logits_made = sem("di_logits_made")
        step = sem("di_step")
        less_done = sem("di_less_done")
        exp_done = sem("di_exp_done")
        hot_done = sem("di_hot_done")
        counts_made = sem("di_counts_made")
        score_done = sem("di_score_done")
        slot_done = sem("di_slot_done")
        tile_expert_done = sem("di_tile_expert_done")
        dispatched = sem("di_dispatched")

        block = ctx.enter_context(nc.Block())

        @block.sync
        def _(sp):
            T.clear_old(sp)
            sp.dma_start(w_gate[:], t["r_w"]).then_inc(weights_in, 16)
            sp.dma_start(b_gate[:], t["r_b"].unsqueeze(0)).then_inc(weights_in, 16)
            sp.wait_ge(consts, 8)
            sp.dma_start(T.slot_rows.rearrange("(i n) c -> n i c", n=128), over(empty[:], NTILES * TILE // 128)
                         ).then_inc(emptied, 16)
            sp.dma_start(T.experts[:], t["m_pack"]).then_inc(experts_in, 16)
            sp.dma_start(T.expert_b2[:], t["m_b2"].rearrange("e d -> (e d)").partition_broadcast(128)
                         ).then_inc(experts_in, 16)
            sp.wait_ge(emptied, 16)
            sp.wait_ge(experts_in, 32)

        @block.gpsimd
        def _(pool):
            pool.memset(all_ones[:], 1.0).then_inc(consts, 1)
            pool.wait_ge(consts, 1)
            pool.affine_select(out=earlier[:], in_=all_ones[:], compare_op=ALU.is_gt, fill=0.0, base=0,
                               pattern=[[1, L]], channel_multiplier=-1).then_inc(consts, 1)
            pool.iota(preference_int[:], pattern=[[0, B], [-1, E]], base=E, channel_multiplier=0).then_inc(consts, 1)
            pool.iota(tile_no_int[:], pattern=[[1, NTILES]], base=0, channel_multiplier=0).then_inc(consts, 1)
            pool.wait_ge(consts, 4)
            pool.tensor_copy(preference[:], preference_int[:]).then_inc(consts, 1)
            pool.tensor_copy(tile_no[:], tile_no_int[:]).then_inc(consts, 1)
            pool.memset(empty[:], 0.0).then_inc(consts, 1)
            pool.wait_ge(consts, 7)
            pool.memset(empty[:, 2 * D:2 * D + 1].bitcast(I32), N).then_inc(consts, 1)
            pool.wait_ge(consts, 8)
            pool.iota(rows[:, :, 2 * D:2 * D + 1].bitcast(I32), pattern=[[L, B], [0, 1]], base=0,
                      channel_multiplier=1).then_inc(consts, 1)

            def finish(g, p):
                pool.wait_ge(mv_done, GB * (g + 1))
                pool.tensor_tensor(var_eps[p][:], mv[p][:, :, 1], T.eps[:], ALU.add).then_inc(eps_added, 1)
                pool.wait_ge(eps_added, g + 1)
                pool.tensor_tensor(rstd[p][:], var_eps[p][:], T.neg_half[:], ALU.pow).then_inc(rstd_done, 1)

            with pool.Fori(0, NG // 2) as k:
                finish(2 * k, 0)
                finish(2 * k + 1, 1)
            pool.wait_ge(h_copied, NG)
            pool.wait_ge(score_done, 1)
            pool.wait_ge(slot_done, 1)
            pool.wait_ge(consts, 9)
            pool.wait_ge(emptied, 16)
            pool.wait_ge(z_copied, NG)
            for b in range(B):
                pool.indirect_dma_start(out=T.slot_rows,
                                        out_offset=bass.IndirectOffsetOnAxis(ap=slot[:, b:b + 1], axis=0),
                                        in_=rows[:, b, :], in_offset=None).then_inc(dispatched, 16)
            pool.wait_ge(dispatched, 16 * B)

        @block.tensor
        def _(pe):
            pe.wait_ge(weights_in, 32)

            def transposes(g, p):
                T.wait_alone(pe, z_done, g + 1)
                if at_least(g, 2):
                    T.wait_alone(pe, zT_kept, g - 1)
                for b in range(GB):
                    last = pe.transpose(p_zT[p][:, b, :], z[p][:, b, :], T.ident[0:L, 0:L])
                last.then_inc(zT_made, 1)

            def route(g, p):
                T.wait_alone(pe, zT_kept, g + 1)
                for b in range(GB):
                    last = pe.matmul(p_logits[:, bass.ds(g * GB + b, 1), :].rearrange("l o e -> l (o e)"),
                                     zT[p][:, b, :], w_gate[:], start=False, stop=True, skip_group_check=True)
                last.then_inc(logits_made, 1)

            pe.wait_ge(step, 1)
            pe.matmul(p_logits[:], ones_row[:], over(b_gate[:], B), start=True, stop=False, skip_group_check=True)
            transposes(0, 0)
            transposes(1, 1)
            route(0, 0)
            with pe.Fori(1, NG // 2) as k:
                transposes(2 * k, 0)
                route(2 * k - 1, 1)
                transposes(2 * k + 1, 1)
                route(2 * k, 0)
            route(NG - 1, 1)
            pe.wait_ge(hot_done, 1)
            pe.wait_ge(consts, 2)
            pe.matmul(p_total[:], all_ones[:], hot_bf[:], start=True, stop=True).then_inc(counts_made, 1)
            pe.matmul(p_before[:], earlier[:], hot_bf[:], start=True, stop=True).then_inc(counts_made, 1)

        @block.scalar
        def _(act):
            with act.Fori(0, NG // 2) as k:
                for p in range(2):
                    g = 2 * k + p
                    act.wait_ge(zT_made, g + 1)
                    act.wait_ge(logits_made, g + 1)
                    act.copy(zT[p][:], p_zT[p][:]).then_inc(zT_kept, 1)
                    act.copy(rows[:, bass.ds(g * GB, GB), 0:D], z[p][:]).then_inc(z_copied, 1)
                    act.copy(rows[:, bass.ds(g * GB, GB), D:2 * D], T.H[:, bass.ds(g * GB, GB), :]).then_inc(h_copied, 1)
            act.wait_ge(less_done, 1)
            act.activation(less[:], less[:], ACT.Exp).then_inc(exp_done, 1)

        @block.vector
        def _(dve):
            dve.sem_inc(logits_made, 2)
            dve.memset(ones_row[:], 1.0)
            dve.memset(ones_e[:], 1.0)
            dve.memset(same_expert[:], 1.0).then_inc(step, 1)
            dve.wait_ge(step, 1)
            dve.memset(same_expert[:, :, 0:1], 0.0).then_inc(step, 1)

            def moments(g, p):
                for b in range(GB):
                    dve.bn_stats(stats[p][:, b, :], T.H[:, g * GB + b, :]).then_inc(stats_done, 1)
                T.wait_alone(dve, stats_done, GB * (g + 1))
                for b in range(GB):
                    dve.bn_aggr(mv[p][:, b, :], stats[p][:, b, :]).then_inc(mv_done, 1)

            def normalize(g, p):
                T.wait_alone(dve, rstd_done, g + 1)
                if at_least(g, 2):
                    T.wait_alone(dve, zT_made, g - 1)
                    T.wait_alone(dve, z_copied, g - 1)
                for b in range(GB):
                    last = dve.tensor_scalar(z[p][:, b, :], T.H[:, g * GB + b, :], mv[p][:, b, 0:1],
                                             rstd[p][:, b:b + 1], ALU.subtract, ALU.mult)
                last.then_inc(z_done, 1)

            moments(0, 0)
            moments(1, 1)
            normalize(0, 0)
            moments(2, 0)
            normalize(1, 1)
            moments(3, 1)
            with dve.Fori(1, NG // 2 - 1) as k:
                for p in range(2):
                    normalize(2 * k + p, p)
                    moments(2 * k + p + 2, p)
            normalize(NG - 2, 0)
            normalize(NG - 1, 1)

            dve.wait_ge(logits_made, NG + 2)
            dve.tensor_reduce(best[:], p_logits[:], AX_X, ALU.max).then_inc(step, 1)
            dve.wait_ge(step, 3)
            dve.tensor_tensor(less[:], p_logits[:], over(best[:], E, 2), ALU.subtract).then_inc(less_done, 1)
            dve.wait_ge(consts, 6)
            dve.tensor_tensor(candidates[:], p_logits[:], over(best[:], E, 2), ALU.is_equal).then_inc(step, 1)
            dve.wait_ge(step, 4)
            dve.tensor_tensor(candidates[:], candidates[:], preference[:], ALU.mult).then_inc(step, 1)
            dve.wait_ge(step, 5)
            dve.tensor_reduce(first[:], candidates[:], AX_X, ALU.max).then_inc(step, 1)
            dve.wait_ge(step, 6)
            dve.tensor_tensor(hot_bf[:], candidates[:], over(first[:], E, 2), ALU.is_equal).then_inc(hot_done, 1)
            dve.tensor_tensor(hot[:], candidates[:], over(first[:], E, 2), ALU.is_equal).then_inc(step, 1)
            dve.wait_ge(exp_done, 1)
            dve.tensor_reduce(score_sum[:], less[:], AX_X, ALU.add).then_inc(step, 1)
            dve.wait_ge(step, 8)
            dve.reciprocal(rows[:, :, 2 * D + 1:2 * D + 2].rearrange("l b o -> l (b o)"), score_sum[:]
                           ).then_inc(score_done, 1)
            dve.wait_ge(counts_made, 2)
            dve.tensor_copy(totals[:].rearrange("l e b -> l b e"), p_total[:]).then_inc(step, 1)
            dve.wait_ge(step, 9)
            dve.tensor_tensor_scan(running[:].rearrange("l e b -> l (e b)"),
                                   same_expert[:].rearrange("l e b -> l (e b)"),
                                   totals[:].rearrange("l e b -> l (e b)"), 0.0, ALU.mult, ALU.add).then_inc(step, 1)
            dve.wait_ge(step, 10)
            dve.tensor_scalar(tiles_int[:], running[:, :, B - 1], float(TILE - 1), None, ALU.add).then_inc(step, 1)
            dve.wait_ge(step, 11)
            dve.tensor_scalar(tiles_shifted[:], tiles_int[:], TILE.bit_length() - 1, None,
                              ALU.arith_shift_right).then_inc(step, 1)
            dve.wait_ge(step, 12)
            dve.tensor_copy(tiles[:], tiles_shifted[:]).then_inc(step, 1)
            dve.wait_ge(step, 13)
            dve.tensor_tensor_scan(tile_end[:], ones_e[:], tiles[:], 0.0, ALU.mult, ALU.add).then_inc(step, 1)
            dve.wait_ge(step, 14)
            dve.tensor_tensor(base[:], tile_end[:], tiles[:], ALU.subtract).then_inc(step, 1)
            dve.wait_ge(step, 15)
            dve.tensor_scalar(base[:], base[:], float(TILE), None, ALU.mult).then_inc(step, 1)
            dve.tensor_tensor(running[:], running[:], totals[:], ALU.subtract).then_inc(step, 1)
            dve.wait_ge(step, 17)
            dve.tensor_tensor(running[:], running[:], over(base[:], B, 2), ALU.add).then_inc(step, 1)
            dve.wait_ge(step, 18)
            dve.tensor_tensor(place[:], p_before[:], running[:].rearrange("l e b -> l b e"), ALU.add).then_inc(step, 1)
            dve.wait_ge(step, 19)
            dve.tensor_tensor(place[:], place[:], hot[:], ALU.mult).then_inc(step, 1)
            dve.wait_ge(step, 20)
            dve.tensor_reduce(slot_f[:], place[:], AX_X, ALU.add).then_inc(step, 1)
            dve.wait_ge(step, 21)
            dve.tensor_copy(slot[:], slot_f[:]).then_inc(slot_done, 1)
            dve.tensor_tensor(passed[:], over(tile_end[0:1, :], NTILES), over(tile_no[:], E, 2),
                              ALU.is_le).then_inc(step, 1)
            dve.wait_ge(step, 22)
            dve.tensor_reduce(tile_expert_f[:], passed[:], AX_X, ALU.add).then_inc(step, 1)
            dve.wait_ge(step, 23)
            dve.tensor_scalar(T.tile_expert[:], tile_expert_f[:], float(E - 1), None, ALU.min
                              ).then_inc(tile_expert_done, 1)


def stage_top1(T):
    nc, t, sem = T.nc, T.t, T.sem
    S = TILE // 128
    FC = F // 128
    W1, W2, B1 = 0, F, F + FC * D
    PACK = B1 + FC
    with ExitStack() as ctx:
        def sb(name, shape, dt=F32):
            return ctx.enter_context(nc.sbuf_tensor(name, shape, dt))

        def ps(name, shape, dt=F32):
            return ctx.enter_context(nc.psum_tensor(name, shape, dt))

        experts, b2 = T.experts, T.expert_b2
        now = [sb(f"tp_now{p}", [128, PACK]) for p in range(2)]
        rows = [sb(f"tp_rows{a}", [128, S, ROW]) for a in range(4)]
        xT = [sb(f"tp_xT{p}", [D, TILE]) for p in range(2)]
        hidden = [sb(f"tp_hidden{p}", [128, FC, TILE]) for p in range(2)]
        plus_b2 = [sb(f"tp_plus_b2{p}", [128, S, D]) for p in range(2)]
        result = [sb(f"tp_result{a}", [128, S, D]) for a in range(4)]
        token = [sb(f"tp_token{a}", [128, S], I32) for a in range(4)]
        BANK = 512
        p_xT = [ps(f"tp_p_xT{p}", [D, BANK]) for p in range(2)]
        p_hidden = [ps(f"tp_p_hidden{c}", [128, BANK]) for c in range(FC)]
        p_y = [ps(f"tp_p_y{p}", [128, BANK // D, D]) for p in range(2)]

        rows_in = [sem(f"tp_rows_in{a}") for a in range(4)]
        now_done = sem("tp_now_done")
        xT_made = sem("tp_xT_made")
        xT_kept = sem("tp_xT_kept")
        hidden_made = sem("tp_hidden_made")
        relu_done = sem("tp_relu_done")
        y_made = sem("tp_y_made")
        b2_added = sem("tp_b2_added")
        result_done = sem("tp_result_done")
        stored = [sem(f"tp_stored{a}") for a in range(4)]

        block = ctx.enter_context(nc.Block())


        @block.sync
        def _(sp):
            T.clear_old(sp)

            def load(w, a):
                i = 4 * w + a
                sp.dma_start(rows[a][:], T.slot_rows[bass.ds(i * TILE, TILE), :].rearrange("(s n) c -> n s c", n=128)
                             ).then_inc(rows_in[a], 16)

            for a in range(4):
                load(0, a)
            with sp.Fori(1, NTILES // 4) as w:
                for a in range(4):
                    sp.wait_ge(result_done, 4 * w + a - 3)
                    load(w, a)

        @block.gpsimd
        def _(pool):
            with pool.Fori(0, NTILES // 4) as w:
                for a in range(4):
                    T.wait_alone(pool, result_done, 4 * w + a + 1)
                    for s in range(S):
                        pool.indirect_dma_start(out=T.out_rows,
                                                out_offset=bass.IndirectOffsetOnAxis(ap=token[a][:, s:s + 1], axis=0),
                                                in_=result[a][:, s, :], in_offset=None, bounds_check=N - 1,
                                                oob_is_err=False).then_inc(stored[a], 16)
            for a in range(4):
                pool.wait_ge(stored[a], 16 * S * NTILES // 4)

        @block.tensor
        def _(pe):
            def transposes(w, a):
                i, p = 4 * w + a, a % 2
                T.wait_alone(pe, rows_in[a], 16 * (w + 1))
                if at_least(i, 2):
                    T.wait_alone(pe, xT_kept, i - 1)
                for s in range(S):
                    last = pe.transpose(p_xT[p][:, s * 128:(s + 1) * 128], rows[a][:, s, 0:D], T.ident[:])
                last.then_inc(xT_made, 1)

            def into_hidden(w, a):
                i, p = 4 * w + a, a % 2
                T.wait_alone(pe, now_done, i + 1)
                T.wait_alone(pe, xT_kept, i + 1)
                for c in range(FC):
                    if at_least(i, 1):
                        T.wait_alone(pe, relu_done, FC * (i - 1) + c + 1)
                    pe.matmul(p_hidden[c][:, 0:TILE], now[p][:, W1 + c * 128:W1 + (c + 1) * 128], xT[p][:],
                              start=True, stop=True).then_inc(hidden_made, 1)

            def out_of_hidden(i, p):
                T.wait_alone(pe, relu_done, FC * (i + 1))
                if at_least(i, 2):
                    T.wait_alone(pe, b2_added, i - 1)
                for s in range(S):
                    for c in range(FC):
                        last = pe.matmul(p_y[p][:, s, :], hidden[p][:, c, s * 128:(s + 1) * 128],
                                         now[p][:, W2 + c * D:W2 + (c + 1) * D], start=(c == 0), stop=(c == FC - 1))
                last.then_inc(y_made, 1)

            def tile(w, a):
                transposes(w, a)
                if at_least(4 * w + a, 1):
                    out_of_hidden(4 * w + a - 1, (a + 1) % 2)
                into_hidden(w, a)

            for a in range(4):
                tile(0, a)
            with pe.Fori(1, NTILES // 4) as w:
                for a in range(4):
                    tile(w, a)
            out_of_hidden(NTILES - 1, 1)

        @block.scalar
        def _(act):
            def tile(w, a):
                i, p = 4 * w + a, a % 2
                T.wait_alone(act, xT_made, i + 1)
                if at_least(i, 2):
                    T.wait_alone(act, y_made, i - 1)
                act.copy(xT[p][:], p_xT[p][:, 0:TILE]).then_inc(xT_kept, 1)
                for c in range(FC):
                    act.wait_ge(hidden_made, FC * i + c + 1)
                    act.activation(hidden[p][:, c, :], p_hidden[c][:, 0:TILE], ACT.Relu,
                                   bias=now[p][:, B1 + c:B1 + c + 1]).then_inc(relu_done, 1)

            for a in range(4):
                tile(0, a)
            with act.Fori(1, NTILES // 4) as w:
                for a in range(4):
                    tile(w, a)

        @block.vector
        def _(dve):
            def bring(i, p):
                if at_least(i, 2):
                    T.wait_alone(dve, y_made, i - 1)
                e = dve.value_load(T.tile_expert[0:1, bass.ds(i, 1)], min_val=0, max_val=E - 1)
                dve.tensor_copy(now[p][:], experts[:, bass.ds(e, 1), :].rearrange("k o n -> k (o n)")
                                ).then_inc(now_done, 1)

            def finish(i, a, w):
                p = a % 2
                T.wait_alone(dve, y_made, i + 1)
                e = dve.value_load(T.tile_expert[0:1, bass.ds(i, 1)], min_val=0, max_val=E - 1)
                dve.tensor_tensor(plus_b2[p][:], p_y[p][:, 0:S, :],
                                  over(b2[:, bass.ds(e, 1), :].rearrange("n o d -> n (o d)"), S),
                                  ALU.add).then_inc(b2_added, 1)
                T.wait_alone(dve, b2_added, i + 1)
                if at_least(i, 4):
                    T.wait_alone(dve, stored[a], 16 * S * w)
                dve.tensor_copy(token[a][:], rows[a][:, :, 2 * D].bitcast(I32))
                for s in range(S):
                    last = dve.scalar_tensor_tensor(out=result[a][:, s, :], in0=plus_b2[p][:, s, :],
                                                    scalar=rows[a][:, s, 2 * D + 1:2 * D + 2],
                                                    in1=rows[a][:, s, D:2 * D], op0=ALU.mult, op1=ALU.add)
                last.then_inc(result_done, 1)

            bring(0, 0)
            for i in range(1, 5):
                bring(i, i % 2)
                finish(i - 1, i - 1, 0)
            with dve.Fori(1, NTILES // 4 - 1) as w:
                for a in range(4):
                    bring(4 * w + a + 1, (a + 1) % 2)
                    finish(4 * w + a, a, w)
            for a in range(4):
                if a < 3:
                    bring(NTILES - 3 + a, (a + 1) % 2)
                finish(NTILES - 4 + a, a, NTILES // 4 - 1)


STAGES = [stage_tokenizer, stage_attention, stage_router_logits, stage_choose, stage_expert_choice,
          stage_offset_attention, stage_dispatch, stage_top1]


def build(nc, t, out):
    with ExitStack() as ctx:
        T = Tower(nc, ctx, t, out)
        for stage in STAGES:
            T.next_stage()
            stage(T)


def layouts(v):
    import numpy as np
    a = {
        "x": v["x"], "w_proj": v["L0_tok_W_proj"], "w_pwT": v["L0_tok_W_pw"].T, "w_dw": v["L0_tok_W_dw"],
        "b_proj": v["L0_tok_b_proj"], "b_dw": v["L0_tok_b_dw"], "b_pw": v["L0_tok_b_pw"],
        "gamma": v["L0_tok_gamma"], "beta": v["L0_tok_beta"],
        "w_qkvT": v["L0_attn_w_qkv"].T, "w_aggT": v["L0_attn_w_agg"].T, "b_agg": v["L0_attn_b_agg"],
        "w_router": v["L0_ffn_Wr"], "e_w1": v["L0_ffn_W1"].reshape(E * D, F), "e_w2": v["L0_ffn_W2"].reshape(E * F, D),
        "e_b1": v["L0_ffn_b1"].reshape(E, F // 128, 128).transpose(2, 0, 1), "e_b2": v["L0_ffn_b2"],
    }
    tables = list(range(OFF_LOCAL, -1, -1)) + list(range(OFF_LOCAL + 1, len(OFFS)))
    omega = np.array([0.0, 0.0, 1.0, 1.0, 4.0, 4.0, 6.0, 6.0]) * np.pi / np.log(1.0 + 4096.0)
    cosines = np.cos(omega[None, :] * np.log(1.0 + np.array(OFFS, np.float64))[:, None]) * (omega > 0.0)

    def chunked(table):
        out = np.zeros((128, 3), np.float32)
        out[:, 0:2] = table[0:32].reshape(2, 128).T
        out.reshape(4, 32, 3)[:, 0:NH, 2] = table[32:36]
        return out

    a.update({
        "o_wqkv": v["L1_attn_W_qkv"], "o_wgate": v["L1_attn_W_gate"], "o_wout": v["L1_attn_W_out"],
        "o_gain": np.repeat(v["L1_attn_if_gain"], DH), "o_bqk": v["L1_attn_b_qkv"][0:2 * D].reshape(2, D).T,
        "o_bvg": np.concatenate([v["L1_attn_b_qkv"][2 * D:], v["L1_attn_b_gate"]]), "o_bout": v["L1_attn_b_out"],
        "o_scale": np.tile(v["L1_attn_scale_embed"][tables].T, (NH, 1)),
        "o_pos": chunked(v["L1_attn_pos_bias"][tables]), "o_cos": chunked(cosines.astype(np.float32)),
        "o_amp": np.tile(v["L1_attn_disp_amp"], 128 // NH),
        "r_w": v["L1_ffn_Wg"], "r_b": v["L1_ffn_bg"], "m_b2": v["L1_ffn_b2"],
        "m_pack": np.concatenate([
            v["L1_ffn_W1"].transpose(1, 0, 2),
            v["L1_ffn_W2"].reshape(E, F // 128, 128, D).transpose(2, 0, 1, 3).reshape(128, E, F // 128 * D),
            v["L1_ffn_b1"].reshape(E, F // 128, 128).transpose(2, 0, 1)], axis=2),
    })
    return {k: np.ascontiguousarray(x) for k, x in a.items()}


def kernel(**inputs):
    import numpy as _np
    import concourse.bacc as _bacc
    from concourse import mybir as _mybir
    from concourse.bass_utils import run_bass_kernel_spmd as _run

    nc = _bacc.Bacc("TRN2", target_bir_lowering=False, num_devices=1)
    arrays, aps = {}, {}
    for name, a in layouts({k: _np.asarray(v) for k, v in inputs.items()}).items():
        arrays[f"in_{name}_dram"] = a
        aps[name] = nc.dram_tensor(f"in_{name}_dram", a.shape, _mybir.dt.from_np(a.dtype), kind="ExternalInput").ap()
    out = nc.dram_tensor("out_dram", (B, L, D), F32, kind="ExternalOutput").ap()
    build(nc, aps, out)
    r = _run(nc, [arrays], core_ids=[0])
    return r.results[0]["out_dram"]
```
